# Optimizing a Trainium2 kernel written in Bass

```python
import numpy as np
import jax
import jax.numpy as jnp

def _softmax(x, axis=-1):
    return jax.nn.softmax(x, axis=axis)

def _gelu(x):
    return jax.nn.gelu(x, approximate=True)

def _silu(x):
    return jax.nn.silu(x)

def _sigmoid(x):
    return jax.nn.sigmoid(x)

def _layernorm(x, axis=-1, eps=1e-05):
    m = jnp.mean(x, axis=axis, keepdims=True)
    v = jnp.var(x, axis=axis, keepdims=True)
    return (x - m) / jnp.sqrt(v + eps)

def _scatter_add(tgt, idx, src, axis=0):
    return tgt.at[idx].add(src)

def _segment_sum(src, seg, n):
    return jax.ops.segment_sum(src, seg, n)
kernel_name = 'mk_hybrid_d1_jaxref_r4_eada00'

def setup_inputs(seed: int=0):
    np.random.seed(seed)
    _w = jnp.asarray

    def _L0_attn_a_setup():
        import jax, jax.numpy as jnp
        import numpy as np
        HEADS = 16
        HIDDEN = 256
        key = jax.random.key(seed)
        ks = jax.random.split(key, 9)
        E, H = (256, HIDDEN)
        N, L = (4, 512)
        s = 0.02
        return {'X_embed': jax.random.normal(ks[0], (N, L, E), dtype=jnp.float32), 'Wq': jax.random.normal(ks[1], (E, H), dtype=jnp.float32) * s, 'bq': jax.random.normal(ks[2], (H,), dtype=jnp.float32) * s, 'Wk': jax.random.normal(ks[3], (E, H), dtype=jnp.float32) * s, 'bk': jax.random.normal(ks[4], (H,), dtype=jnp.float32) * s, 'Wv': jax.random.normal(ks[5], (E, H), dtype=jnp.float32) * s, 'bv': jax.random.normal(ks[6], (H,), dtype=jnp.float32) * s, 'Wo': jax.random.normal(ks[7], (H, H), dtype=jnp.float32) * s, 'bo': jax.random.normal(ks[8], (H,), dtype=jnp.float32) * s}
    _L0_attn_a_in = _L0_attn_a_setup()

    def _L0_attn_b_setup():
        import jax, jax.numpy as jnp
        import numpy as np
        D_MODEL = 256
        NHEAD = 16
        D_K = D_MODEL // NHEAD
        MAX_REL = 256
        key = jax.random.key(seed)
        ks = jax.random.split(key, 6)
        B, S = (4, 512)
        s = 1.0 / np.sqrt(D_MODEL)
        x = jax.random.normal(ks[0], (B, S, D_MODEL), dtype=jnp.float32)
        W_qkv = jax.random.normal(ks[1], (D_MODEL, 3 * D_MODEL), dtype=jnp.float32) * s
        b_qkv = jnp.zeros((3 * D_MODEL,), dtype=jnp.float32)
        W_out = jax.random.normal(ks[2], (D_MODEL, D_MODEL), dtype=jnp.float32) * s
        b_out = jnp.zeros((D_MODEL,), dtype=jnp.float32)
        rel_bias = jax.random.normal(ks[3], (2 * MAX_REL + 1, NHEAD), dtype=jnp.float32) * 0.02
        return {'x': x, 'W_qkv': W_qkv, 'b_qkv': b_qkv, 'W_out': W_out, 'b_out': b_out, 'rel_bias': rel_bias}
    _L0_attn_b_in = _L0_attn_b_setup()

    def _L0_ffn_setup():
        import jax, jax.numpy as jnp
        import numpy as np
        D_MODEL, FF_DIM = (256, 512)
        N_SHARED, N_ROUTED, TOP_K = (1, 8, 2)
        BATCH, SEQ = (2, 512)
        key = jax.random.key(seed)
        ks = jax.random.split(key, 8)
        init = lambda k, shape: jax.random.normal(k, shape, jnp.float32) * 0.02
        x = jax.random.normal(ks[0], (BATCH, SEQ, D_MODEL), jnp.float32)
        Wg = init(ks[1], (D_MODEL, N_ROUTED))
        Ws1 = init(ks[2], (D_MODEL, FF_DIM))
        Ws3 = init(ks[3], (D_MODEL, FF_DIM))
        Ws2 = init(ks[4], (FF_DIM, D_MODEL))
        We1 = init(ks[5], (N_ROUTED, D_MODEL, FF_DIM))
        We3 = init(ks[6], (N_ROUTED, D_MODEL, FF_DIM))
        We2 = init(ks[7], (N_ROUTED, FF_DIM, D_MODEL))
        return {'x': x, 'Wg': Wg, 'Ws1': Ws1, 'Ws3': Ws3, 'Ws2': Ws2, 'We1': We1, 'We3': We3, 'We2': We2}
    _L0_ffn_in = _L0_ffn_setup()
    _d = {'L0_attn_a_X_embed': _L0_attn_a_in['X_embed'], 'L0_attn_a_Wq': _L0_attn_a_in['Wq'], 'L0_attn_a_bq': _L0_attn_a_in['bq'], 'L0_attn_a_Wk': _L0_attn_a_in['Wk'], 'L0_attn_a_bk': _L0_attn_a_in['bk'], 'L0_attn_a_Wv': _L0_attn_a_in['Wv'], 'L0_attn_a_bv': _L0_attn_a_in['bv'], 'L0_attn_a_Wo': _L0_attn_a_in['Wo'], 'L0_attn_a_bo': _L0_attn_a_in['bo'], 'L0_attn_b_W_qkv': _L0_attn_b_in['W_qkv'], 'L0_attn_b_b_qkv': _L0_attn_b_in['b_qkv'], 'L0_attn_b_W_out': _L0_attn_b_in['W_out'], 'L0_attn_b_b_out': _L0_attn_b_in['b_out'], 'L0_attn_b_rel_bias': _L0_attn_b_in['rel_bias'], 'L0_ffn_Wg': _L0_ffn_in['Wg'], 'L0_ffn_Ws1': _L0_ffn_in['Ws1'], 'L0_ffn_Ws3': _L0_ffn_in['Ws3'], 'L0_ffn_Ws2': _L0_ffn_in['Ws2'], 'L0_ffn_We1': _L0_ffn_in['We1'], 'L0_ffn_We3': _L0_ffn_in['We3'], 'L0_ffn_We2': _L0_ffn_in['We2']}
    _x0 = _d['L0_attn_a_X_embed']
    _d['L0_attn_a_X_embed'] = jax.random.normal(jax.random.fold_in(jax.random.key(seed), 1), (8, 512, 256), dtype=_x0.dtype)
    del _x0
    return _d

def reference(L0_attn_a_X_embed, L0_attn_a_Wq, L0_attn_a_bq, L0_attn_a_Wk, L0_attn_a_bk, L0_attn_a_Wv, L0_attn_a_bv, L0_attn_a_Wo, L0_attn_a_bo, L0_attn_b_W_qkv, L0_attn_b_b_qkv, L0_attn_b_W_out, L0_attn_b_b_out, L0_attn_b_rel_bias, L0_ffn_Wg, L0_ffn_Ws1, L0_ffn_Ws3, L0_ffn_Ws2, L0_ffn_We1, L0_ffn_We3, L0_ffn_We2):

    def _L0_attn_a_ref(X_embed, Wq, bq, Wk, bk, Wv, bv, Wo, bo):
        import jax, jax.numpy as jnp
        import numpy as np
        HEADS = 16
        HIDDEN = 256
        N, L, _ = X_embed.shape
        H, heads = (HIDDEN, HEADS)
        dh = H // heads
        Q = X_embed @ Wq + bq
        K = X_embed @ Wk + bk
        V = X_embed @ Wv + bv
        Q = Q.reshape(N, heads, L, dh)
        K = K.reshape(N, heads, L, dh)
        V = V.reshape(N, heads, L, dh)
        scale = np.float32(1.0 / np.sqrt(H))
        Q = Q * scale
        K = K * scale
        scores = jnp.einsum('neax,nebx->neab', Q, K)
        A = jax.nn.softmax(scores, axis=2)
        Out = jnp.einsum('neab,neax->neax', A, V)
        Out = Out.reshape(N, L, H)
        return Out @ Wo + bo

    def _L0_attn_b_ref(x, W_qkv, b_qkv, W_out, b_out, rel_bias):
        import jax, jax.numpy as jnp
        import numpy as np
        D_MODEL = 256
        NHEAD = 16
        D_K = D_MODEL // NHEAD
        MAX_REL = 256
        B, S, D = x.shape
        qkv = x @ W_qkv + b_qkv
        qkv = qkv.reshape(B, S, 3, NHEAD, D_K)
        q, k, v = (qkv[:, :, 0], qkv[:, :, 1], qkv[:, :, 2])
        scores = jnp.einsum('bihd,bjhd->bhij', q, k) / jnp.sqrt(jnp.float32(D_K))
        idxs = jnp.arange(S)
        rel = jnp.clip(idxs[:, None] - idxs[None, :] + MAX_REL, 0, 2 * MAX_REL)
        bias = rel_bias[rel]
        scores = scores + jnp.transpose(bias, (2, 0, 1))[None]
        attn = jax.nn.softmax(scores, axis=-1)
        out = jnp.einsum('bhij,bjhd->bihd', attn, v).reshape(B, S, D)
        return out @ W_out + b_out

    def _L0_ffn_ref(x, Wg, Ws1, Ws3, Ws2, We1, We3, We2):
        import jax, jax.numpy as jnp
        import numpy as np
        D_MODEL, FF_DIM = (256, 512)
        N_SHARED, N_ROUTED, TOP_K = (1, 8, 2)
        BATCH, SEQ = (2, 512)
        B, S, d = x.shape
        E = Wg.shape[1]
        xf = x.reshape(-1, d)
        T = xf.shape[0]
        gates = jax.nn.sigmoid(xf @ Wg)
        vals, idx = jax.lax.top_k(gates, TOP_K)
        vals = vals / vals.sum(axis=-1, keepdims=True)
        w = jnp.zeros((T, E), x.dtype).at[jnp.arange(T)[:, None], idx].add(vals)
        shared = jax.nn.silu(xf @ Ws1) * (xf @ Ws3) @ Ws2
        h = jax.nn.silu(jnp.einsum('td,edf->tef', xf, We1)) * jnp.einsum('td,edf->tef', xf, We3)
        routed = jnp.einsum('tef,efd,te->td', h, We2, w)
        out = (shared + routed) / (N_SHARED + TOP_K)
        return out.reshape(B, S, d)
    x = L0_attn_a_X_embed
    x = x + _L0_attn_a_ref(_layernorm(x, axis=-1), L0_attn_a_Wq, L0_attn_a_bq, L0_attn_a_Wk, L0_attn_a_bk, L0_attn_a_Wv, L0_attn_a_bv, L0_attn_a_Wo, L0_attn_a_bo)
    x = x + _L0_ffn_ref(_layernorm(x, axis=-1), L0_ffn_Wg, L0_ffn_Ws1, L0_ffn_Ws3, L0_ffn_Ws2, L0_ffn_We1, L0_ffn_We3, L0_ffn_We2)
    x = x + _L0_attn_b_ref(_layernorm(x, axis=-1), L0_attn_b_W_qkv, L0_attn_b_b_qkv, L0_attn_b_W_out, L0_attn_b_b_out, L0_attn_b_rel_bias)
    x = x + _L0_ffn_ref(_layernorm(x, axis=-1), L0_ffn_Wg, L0_ffn_Ws1, L0_ffn_Ws3, L0_ffn_Ws2, L0_ffn_We1, L0_ffn_We3, L0_ffn_We2)
    return x

_drawn_inputs = setup_inputs


def setup_inputs(seed=0):
    import zlib

    import numpy as np

    out = dict(_drawn_inputs(seed))
    spreads = {'L0_attn_b_b_qkv': (0.0, 0.1), 'L0_attn_b_b_out': (0.0, 0.1)}
    factors = {'L0_attn_a_Wq': 8.0,
     'L0_attn_a_bq': 49.473,
     'L0_attn_a_Wk': 25.936,
     'L0_attn_a_bk': 29.47,
     'L0_attn_a_bv': 6.218,
     'L0_attn_b_rel_bias': 8.0,
     'L0_ffn_Wg': 6.099,
     'L0_ffn_Ws1': 3.671,
     'L0_ffn_Ws3': 3.636,
     'L0_ffn_Ws2': 3.619,
     'L0_ffn_We1': 5.291,
     'L0_ffn_We3': 5.245,
     'L0_ffn_We2': 5.226}
    for name, (base, spread) in spreads.items():
        noise = np.random.default_rng([zlib.crc32(name.encode()), seed]).standard_normal(out[name].shape)
        drawn = base * np.exp(spread * noise) if base else spread * noise
        out[name] = jnp.asarray(drawn.astype(out[name].dtype))
    for name, factor in factors.items():
        out[name] = (out[name] * factor).astype(out[name].dtype)
    return out
```

```python
import concourse.bass as bass
from concourse import mybir
from contextlib import ExitStack

F32 = mybir.dt.float32
F32R = mybir.dt.float32r
ALU = mybir.AluOpType
ACT = mybir.ActivationFunctionType
AX = mybir.AxisListType

P = 128
D = 256
KD = D // P
HEADS = 16
DH = D // HEADS
T = 4096
TILES = T // P
EPS = 1e-5


def wait(eng, sem, value):
    if not isinstance(value, int) or value > 0:
        eng.wait_ge(sem, value)


def wait_apart(eng, sem, value):
    wait(eng, sem, value)
    if not isinstance(value, int):
        eng.nop(nofuse=True)


def build_attention_a(nc, x_in, Wq, bq, Wk, bk, Wv, bv, Wo, bo, x_out, v_d, rs_d):
    HT = 4
    R = P // HT
    L = R * HEADS
    G = 4
    SCALE = 1.0 / D
    with ExitStack() as ctx:
        def sb(name, shape, dt=F32):
            return ctx.enter_context(nc.sbuf_tensor("aa_" + name, shape, dt))

        def pb(name):
            return ctx.enter_context(nc.psum_tensor("aa_" + name, [P, 512], F32))

        sems = []

        def sem(name):
            sems.append(nc.alloc_semaphore("aa_" + name))
            return sems[-1]

        ident = sb("ident", [P, P])
        w_qkv = sb("w_qkv", [P, KD, 3 * D])
        w_o = sb("w_o", [P, KD, D])
        b_qkv = sb("b_qkv", [P, 3 * D])
        b_o = sb("b_o", [P, D])
        minus_half = sb("minus_half", [P, 1])
        x_t = sb("x_t", [P, 2, D])
        stats = sb("stats", [P, 6])
        mean_var = sb("mean_var", [P, 2, 2])
        rstd = sb("rstd", [P, 2])
        xn = sb("xn", [P, 2, D])
        xn_T = sb("xn_T", [P, 2, KD, P])
        qk = sb("qk", [P, 2, 2 * D])
        v_t = sb("v_t", [P, 2, D])
        parts = sb("parts", [P, 2, HEADS, 8, DH])
        qk_T = sb("qk_T", [P, 2, HT, HEADS, R], F32R)
        k_T = sb("k_T", [64, 2, HT, HEADS * R], F32R)
        neg_max = sb("neg_max", [P, 8])
        e_t = sb("e_t", [P, 2, HT, L])
        den = sb("den", [P, 2, HT])
        inv = sb("inv", [P, 2, HT])
        rs_sb = sb("rs_sb", [P, L])
        rs_t = sb("rs_t", [P, 2, HEADS])
        v_p = sb("v_p", [P, 2, D])
        x_p = sb("x_p", [P, 2, D])
        xb = sb("xb", [P, 2, D])
        o_t = sb("o_t", [P, 2, D])
        o_T = sb("o_T", [P, KD, P])
        y_t = sb("y_t", [P, 2, D])
        S = [pb(f"s{i}") for i in range(4)]
        M = [pb(f"m{i}") for i in range(3)]
        RS = pb("rs")

        w_loaded = sem("w_loaded")
        wq_scaled = sem("wq_scaled")
        ident_zeroed = sem("ident_zeroed")
        ident_ready = sem("ident_ready")
        x_loaded = [sem(f"x_loaded{p}") for p in range(2)]
        stats_done = sem("stats_done")
        mv_done = sem("mv_done")
        pool_step = sem("pool_step")
        xn_ready = sem("xn_ready")
        xt_ps = sem("xt_ps")
        xn_T_ready = sem("xn_T_ready")
        qk_ps = sem("qk_ps")
        v_ps = sem("v_ps")
        qk_ready = sem("qk_ready")
        v_ready = sem("v_ready")
        v_stored = [sem(f"v_stored{p}") for p in range(2)]
        hi_ready = sem("hi_ready")
        parts_ready = sem("parts_ready")
        t_ps = sem("t_ps")
        t_by_act = sem("t_by_act")
        t_by_dve = sem("t_by_dve")
        k_T_moved = [sem(f"k_T_moved{p}") for p in range(2)]
        s_done = sem("s_done")
        max_done = sem("max_done")
        exp_done = sem("exp_done")
        inv_done = sem("inv_done")
        rs_done = sem("rs_done")
        rs_copied = sem("rs_copied")
        rs_stored = sem("rs_stored")
        post_loaded = [sem(f"post_loaded{p}") for p in range(2)]
        xb_ready = sem("xb_ready")
        out_ready = sem("out_ready")
        ot_ps = sem("ot_ps")
        o_T_ready = sem("o_T_ready")
        wo_ps = sem("wo_ps")
        y_ready = sem("y_ready")
        y_stored = [sem(f"y_stored{p}") for p in range(2)]

        block = ctx.enter_context(nc.Block())


        def run(eng, step):
            step(0, 0, 0)
            step(1, 1, 0)
            with eng.Fori(1, TILES // 2) as h:
                step(2 * h, 0, h)
                step(2 * h + 1, 1, h)

        def has(i, back):
            return not isinstance(i, int) or i >= back

        PE_R = {0: -2, 4: -1, 8: 0, 12: 1}
        PE_OT, PE_WO, PE_XT, PE_QK, PE_V = 1, 3, 5, (11, 13), 14
        PE_T = {6: 0, 7: 1, 9: 2, 10: 3}
        ACT_OT, ACT_RS, ACT_XT = 0, 3, 4
        ACT_T = {5: 0, 8: 2}
        DVE_INV = {3: -1, 7: 0, 11: 1, 15: 2}
        DVE_Y, DVE_STATS, DVE_QK, DVE_V = 4, 9, 14, 15
        DVE_T = {8: 1, 11: 3}

        @block.sync
        def _(sp):
            def load_x(j, p, h):
                tile = j % TILES if isinstance(j, int) else sp.snap(j % TILES, min_val=0, max_val=TILES - 1)
                wait(sp, xn_ready, j - 1)
                sp.dma_start(x_t[:, p, :], x_in[bass.ts(tile, P), :]).then_inc(x_loaded[p], 16)

            def store_v(j, p, h):
                wait(sp, v_ready, j + 1)
                sp.dma_start(v_d[bass.ts(j, P), :], v_t[:, p, :]).then_inc(v_stored[p], 16)

            def move_k(j, p, h):
                wait(sp, t_by_act, 2 * j + 2)
                wait(sp, t_by_dve, 2 * j + 2)
                wait(sp, s_done, 16 * (j - 1))
                sp.dma_start(k_T[:, p, :, :].bitcast(F32), qk_T[64:P, p, :, :, :].rearrange("p e c r -> p e (c r)").bitcast(F32)).then_inc(k_T_moved[p], 16)

            def post_loads(j, p, h):
                wait(sp, rs_copied, j + 1)
                sp.dma_start(rs_d[bass.ts(j, HT), :], rs_sb[0:P - R + 1:R, :])\
                    .then_inc(rs_stored, 16)
                wait(sp, out_ready, j - 1)
                wait_apart(sp, xb_ready, j - 1)
                wait(sp, v_stored[p], 16 * (h + 1))
                sp.dma_start(v_p[:, p, :], v_d[bass.ts(j, P), :]).then_inc(post_loaded[p], 16)
                sp.dma_start(x_p[:, p, :], x_in[bass.ts(j, P), :]).then_inc(post_loaded[p], 16)
                wait(sp, rs_stored, 16 * (j + 1))
                sp.dma_start(rs_t[:, p, :], rs_d.rearrange("e (r c) -> (e r) c", c=HEADS)[bass.ts(j, P), :])\
                    .then_inc(post_loaded[p], 16)

            def store_y(j, p, h):
                wait(sp, y_ready, j + 1)
                sp.dma_start(x_out[bass.ts(j, P), :], y_t[:, p, :]).then_inc(y_stored[p], 16)

            for w, part in ((Wq, 0), (Wk, 1), (Wv, 2)):
                sp.dma_start(w_qkv[:, :, part * D:(part + 1) * D], w.rearrange("(k p) n -> p k n", p=P))\
                    .then_inc(w_loaded, 16)
            for b, part in ((bq, 0), (bk, 1), (bv, 2)):
                sp.dma_start(b_qkv[:, part * D:(part + 1) * D], b.partition_broadcast(P)).then_inc(w_loaded, 16)
            sp.dma_start(w_o[:], Wo.rearrange("(k p) n -> p k n", p=P)).then_inc(w_loaded, 16)
            sp.dma_start(b_o[:], bo.partition_broadcast(P)).then_inc(w_loaded, 16)
            load_x(0, 0, 0)
            load_x(1, 1, 0)
            load_x(2, 0, 1)
            store_v(0, 0, 0)
            store_v(1, 1, 0)
            move_k(0, 0, 0)

            def step(i, p, h):
                load_x(i + 3, 1 - p, h + 1 + p)
                if has(i, 1):
                    post_loads(i - 1, 1 - p, h - 1 + p)
                if has(i, 2):
                    store_y(i - 2, p, h - 1)
                move_k(i + 1, 1 - p, h + p)
                store_v(i + 2, p, h + 1)

            run(sp, step)
            post_loads(TILES - 1, 1, TILES // 2 - 1)
            store_y(TILES - 2, 0, TILES // 2 - 1)
            store_y(TILES - 1, 1, TILES // 2 - 1)
            for p in range(2):
                sp.wait_ge(y_stored[p], 16 * (TILES // 2))
                sp.wait_ge(v_stored[p], 16 * (TILES // 2 + 1))

        @block.gpsimd
        def _(pool):
            steps = [0]

            nc.gpsimd.memset(ident[:], 0.0).then_inc(ident_zeroed, 1)
            pool.wait_ge(ident_zeroed, 1)
            nc.gpsimd.affine_select(out=ident[:], in_=ident[:], compare_op=ALU.not_equal, fill=1.0, base=0,
                                    pattern=[[-1, P]], channel_multiplier=1).then_inc(ident_ready, 1)
            nc.gpsimd.memset(minus_half[:], -0.5).then_inc(ident_zeroed, 1)
            pool.wait_ge(ident_zeroed, 2)

            def normalise(j, p, h):
                wait_apart(pool, mv_done, j + 1)
                nc.gpsimd.tensor_scalar(rstd[:, p:p + 1], mean_var[:, p, 1:2], EPS, None, ALU.add)\
                    .then_inc(pool_step, 1)
                wait(pool, pool_step, 2 * j + 1)
                nc.gpsimd.tensor_tensor(rstd[:, p:p + 1], rstd[:, p:p + 1], minus_half[:], ALU.pow)\
                    .then_inc(pool_step, 1)
                wait(pool, pool_step, 2 * j + 2)
                wait_apart(pool, xt_ps, j - 1)
                nc.gpsimd.tensor_scalar(xn[:, p, :], x_t[:, p, :], mean_var[:, p, 0:1], rstd[:, p:p + 1],
                                        ALU.subtract, ALU.mult).then_inc(xn_ready, 1)

            def split(j, p, h):
                wait(pool, qk_ready, j + 1)
                wait_apart(pool, t_ps, 4 * (j - 1))
                for m, hi, lo in ((0, slice(0, 2), slice(2, 4)), (1, slice(4, 8, 2), slice(5, 8, 2))):
                    src = qk[:, p, m * D:(m + 1) * D].rearrange("p (c x) -> p c x", x=DH).unsqueeze(1)\
                        .broadcast_to([P, 2, HEADS, DH])
                    nc.gpsimd.tensor_scalar(parts[:, p, :, hi, :].rearrange("p c a x -> p a c x").bitcast(F32R), src, 1.0, None, ALU.mult)\
                        .then_inc(hi_ready, 1)
                for m, hi, lo in ((0, slice(0, 2), slice(2, 4)), (1, slice(4, 8, 2), slice(5, 8, 2))):
                    src = qk[:, p, m * D:(m + 1) * D].rearrange("p (c x) -> p c x", x=DH).unsqueeze(1)\
                        .broadcast_to([P, 2, HEADS, DH])
                    wait(pool, hi_ready, 2 * j + 1 + m)
                    nc.gpsimd.tensor_tensor(parts[:, p, :, lo, :].rearrange("p c a x -> p a c x").bitcast(F32R), src, parts[:, p, :, hi, :].rearrange("p c a x -> p a c x"),
                                            ALU.subtract).then_inc(parts_ready, 1)

            def weigh(j, p, h):
                wait(pool, post_loaded[p], 48 * (h + 1))
                wait(pool, y_ready, j - 1)
                nc.gpsimd.tensor_tensor(xb[:, p, :], x_p[:, p, :], b_o[:], ALU.add).then_inc(xb_ready, 1)
                wait(pool, ot_ps, j - 1)
                nc.gpsimd.tensor_tensor(o_t[:, p, :].rearrange("p (c x) -> p c x", x=DH),
                                        v_p[:, p, :].rearrange("p (c x) -> p c x", x=DH),
                                        rs_t[:, p, :].unsqueeze(2).broadcast_to([P, HEADS, DH]),
                                        ALU.mult).then_inc(out_ready, 1)

            pool.wait_ge(w_loaded, 8 * 16)
            normalise(0, 0, 0)
            normalise(1, 1, 0)
            split(0, 0, 0)
            normalise(2, 0, 1)
            split(1, 1, 0)

            def step(i, p, h):
                if has(i, 1):
                    weigh(i - 1, 1 - p, h - 1 + p)
                normalise(i + 3, 1 - p, h + 1 + p)
                split(i + 2, p, h + 1)

            run(pool, step)
            weigh(TILES - 1, 1, TILES // 2 - 1)

        def t_out(p, n):
            return qk_T[:, p, :, 4 * n:4 * n + 4, :].rearrange("p e c r -> p c e r")

        T_BANK = [0, 2, 0, 1]
        XT_BANK, QK_BANK, V_BANK, OT_BANK, WO_BANK = 1, 2, 0, 1, 1

        @block.scalar
        def _(act):
            def copy_xn_T(j, p, h):
                wait(act, xt_ps, j + 1)
                wait(act, v_ps, j - 1)
                nc.scalar.activation(xn_T[:, p, :, :], M[XT_BANK][:, 0:D].rearrange("p (k t) -> p k t", k=KD),
                                     ACT.Copy).then_inc(xn_T_ready, 1)

            def copy_t(j, p, n):
                wait(act, t_ps, 4 * j + n + 1)
                wait(act, s_done, 16 * (j - 1))
                wait(act, k_T_moved[p], 16 * ((j - p) // 2) if isinstance(j, int) else k_moves(j, p))
                nc.scalar.activation(t_out(p, n), M[T_BANK[n]][:].rearrange("p (c e r) -> p c e r", c=4, e=HT), ACT.Copy)\
                    .then_inc(t_by_act, 1)

            def exp(i, p, g, e):
                n = 16 * i + 4 * g + e
                wait(act, max_done, n + 1)
                if e == 0:
                    wait(act, rs_done, 4 * i + g - 1)
                nc.scalar.activation(e_t[:, g % 2, e, :], S[e][:], ACT.Exp, bias=neg_max[:, 4 * (g % 2) + e:4 * (g % 2) + e + 1],
                                     scale=-1.0, accum_out=den[:, g % 2, e:e + 1]).then_inc(exp_done, 1)

            def copy_rs(j):
                wait(act, rs_done, 4 * (j + 1))
                wait(act, rs_stored, 16 * j)
                nc.scalar.activation(rs_sb[:].rearrange("p (r c) -> p r c", c=HEADS),
                                     RS[:].rearrange("p (c r) -> p r c", c=HEADS), ACT.Copy).then_inc(rs_copied, 1)

            def copy_o_T(j):
                wait(act, ot_ps, j + 1)
                wait(act, wo_ps, j)
                nc.scalar.activation(o_T[:], M[OT_BANK][:, 0:D].rearrange("p (k t) -> p k t", k=KD), ACT.Copy)\
                    .then_inc(o_T_ready, 1)

            def k_moves(j, p):
                return 8 * (j - p)

            copy_xn_T(0, 0, 0)
            copy_xn_T(1, 1, 0)
            copy_t(0, 0, 0)
            copy_t(0, 0, 2)

            def step(i, p, h):
                for s in range(16):
                    exp(i, p, s // 4, s % 4)
                    if s == ACT_OT and has(i, 2):
                        copy_o_T(i - 2)
                    if s == ACT_RS and has(i, 1):
                        copy_rs(i - 1)
                    if s == ACT_XT:
                        copy_xn_T(i + 2, p, h + 1)
                    if s in ACT_T:
                        copy_t(i + 1, 1 - p, ACT_T[s])

            run(act, step)
            copy_o_T(TILES - 2)
            copy_rs(TILES - 1)
            copy_o_T(TILES - 1)

        @block.vector
        def _(dve):
            def statistics(j, p):
                wait(dve, x_loaded[p], 16 * (j // 2 + 1) if isinstance(j, int) else 8 * (j - p) + 16)
                wait(dve, mv_done, j)
                nc.vector.bn_stats(stats[:], x_t[:, p, :]).then_inc(stats_done, 1)
                wait(dve, stats_done, j + 1)
                wait_apart(dve, xn_ready, j - 1)
                nc.vector.bn_aggr(mean_var[:, p, :], stats[:]).then_inc(mv_done, 1)

            def add_qk(j, p):
                wait(dve, qk_ps, j + 1)
                wait(dve, parts_ready, 2 * (j - 1))
                nc.vector.tensor_tensor(qk[:, p, :], M[QK_BANK][:], b_qkv[:, 0:2 * D], ALU.add).then_inc(qk_ready, 1)

            def add_v(j, p):
                wait(dve, v_ps, j + 1)
                wait(dve, v_stored[p], 16 * (j // 2) if isinstance(j, int) else 8 * (j - p))
                nc.vector.tensor_tensor(v_t[:, p, :], M[V_BANK][:, 0:D], b_qkv[:, 2 * D:3 * D], ALU.add)\
                    .then_inc(v_ready, 1)

            def copy_t(j, p, n):
                wait(dve, t_ps, 4 * j + n + 1)
                wait(dve, s_done, 16 * (j - 1))
                wait(dve, k_T_moved[p], 16 * (j // 2) if isinstance(j, int) else 8 * (j - p))
                nc.vector.tensor_copy(t_out(p, n), M[T_BANK[n]][:].rearrange("p (c e r) -> p c e r", c=4, e=HT))\
                    .then_inc(t_by_dve, 1)

            def maximum(i, g, e):
                wait(dve, s_done, 16 * i + 4 * g + e + 1)
                nc.vector.tensor_reduce(neg_max[:, 4 * (g % 2) + e:4 * (g % 2) + e + 1], S[e][:], AX.X, ALU.min)\
                    .then_inc(max_done, 1)

            def invert(group, gp):
                wait(dve, exp_done, 4 * (group + 1))
                nc.vector.reciprocal(inv[:, gp, :], den[:, gp, :]).then_inc(inv_done, 1)

            def add_residual(j, p):
                wait(dve, wo_ps, j + 1)
                wait(dve, xb_ready, j + 1)
                wait(dve, y_stored[p], 16 * (j // 2) if isinstance(j, int) else 8 * (j - p))
                nc.vector.tensor_tensor(y_t[:, p, :], M[WO_BANK][:, 0:D], xb[:, p, :], ALU.add).then_inc(y_ready, 1)

            dve.wait_ge(w_loaded, 8 * 16)
            nc.vector.tensor_scalar(w_qkv[:, :, 0:D], w_qkv[:, :, 0:D], -SCALE, None, ALU.mult).then_inc(wq_scaled, 1)
            nc.vector.tensor_scalar(b_qkv[:, 0:D], b_qkv[:, 0:D], -SCALE, None, ALU.mult).then_inc(wq_scaled, 1)
            dve.wait_ge(wq_scaled, 2)
            statistics(0, 0)
            statistics(1, 1)
            add_qk(0, 0)
            add_v(0, 0)
            statistics(2, 0)
            add_qk(1, 1)
            add_v(1, 1)
            copy_t(0, 0, 1)
            copy_t(0, 0, 3)

            def step(i, p, h):
                for s in range(16):
                    maximum(i, s // 4, s % 4)
                    if s in DVE_INV and has(4 * i, -DVE_INV[s]):
                        invert(4 * i + DVE_INV[s], DVE_INV[s] % 2)
                    if s == DVE_Y and has(i, 2):
                        add_residual(i - 2, p)
                    if s in DVE_T:
                        copy_t(i + 1, 1 - p, DVE_T[s])
                    if s == DVE_STATS:
                        statistics(i + 3, 1 - p)
                    if s == DVE_QK:
                        add_qk(i + 2, p)
                    if s == DVE_V:
                        add_v(i + 2, p)

            run(dve, step)
            invert(4 * TILES - 1, 1)
            add_residual(TILES - 2, 0)
            add_residual(TILES - 1, 1)

        @block.tensor
        def _(pe):
            def transpose_x(j, p):
                wait(pe, xn_ready, j + 1)
                wait(pe, y_ready, j - 3)
                wait(pe, xn_T_ready, j)
                for k in range(KD):
                    last = nc.tensor.transpose(M[XT_BANK][:, k * P:(k + 1) * P], xn[:, p, k * P:(k + 1) * P], ident[:])
                last.then_inc(xt_ps, 1)

            def project_qk(j, p, k):
                if k == 0:
                    wait(pe, xn_T_ready, j + 1)
                    wait(pe, t_by_dve, 2 * (j - 1) + 1 if not isinstance(j, int) or j >= 2 else 0)
                    wait(pe, qk_ready, j)
                product = nc.tensor.matmul(M[QK_BANK][:], xn_T[:, p, k, :], w_qkv[:, k, 0:2 * D],
                                           start=k == 0, stop=k == KD - 1)
                if k == KD - 1:
                    product.then_inc(qk_ps, 1)

            def project_v(j, p):
                wait(pe, t_by_act, 2 * j if not isinstance(j, int) or j >= 2 else 0)
                wait(pe, v_ready, j)
                for k in range(KD):
                    last = nc.tensor.matmul(M[V_BANK][:, 0:D], xn_T[:, p, k, :], w_qkv[:, k, 2 * D:3 * D],
                                            start=k == 0, stop=k == KD - 1)
                last.then_inc(v_ps, 1)

            def transpose_parts(j, p, n):
                wait(pe, parts_ready, 2 * (j + 1))
                start = isinstance(j, int) and j == 0
                if n == 0:
                    wait(pe, v_ready, j + 1 + start)
                elif n == 1:
                    wait(pe, qk_ready, j + 1 + start)
                elif n == 2:
                    wait(pe, t_by_act, 2 * j + 1)
                else:
                    wait(pe, xn_T_ready, j + 2)
                for c in range(4):
                    last = nc.tensor.transpose(M[T_BANK[n]][:, c * P:(c + 1) * P],
                                               parts[:, p, 4 * n + c, :, :].rearrange("p a x -> p (a x)"), ident[:])
                last.then_inc(t_ps, 1)

            def scores(i, p, g, e):
                n = 16 * i + 4 * g + e
                wait(pe, exp_done, n - 3)
                nc.tensor.matmul(S[e][:], k_T[:, p, e, g * P:(g + 1) * P],
                                 qk_T[0:64, p, e, :, :].rearrange("p c r -> p (c r)"), start=True, stop=True).then_inc(s_done, 1)

            def row_sums(i, group, g):
                wait(pe, inv_done, group + 1)
                if g == 0:
                    wait(pe, rs_copied, i)
                for e in range(4):
                    last = nc.tensor.matmul(RS[e * R:(e + 1) * R, :], inv[:, g % 2, e:e + 1].broadcast_to([P, R]),
                                            e_t[:, g % 2, e, :], start=g == 0, stop=g == 3)
                last.then_inc(rs_done, 1)

            def transpose_o(j, p):
                wait(pe, out_ready, j + 1)
                if isinstance(j, int) and j >= TILES - 2:
                    wait(pe, t_by_dve, 2 * (TILES + 1))
                    wait(pe, y_ready, j)
                for k in range(KD):
                    last = nc.tensor.transpose(M[OT_BANK][:, k * P:(k + 1) * P], o_t[:, p, k * P:(k + 1) * P], ident[:])
                last.then_inc(ot_ps, 1)

            def output(j, p):
                wait(pe, o_T_ready, j + 1)
                for k in range(KD):
                    last = nc.tensor.matmul(M[WO_BANK][:, 0:D], o_T[:, k, :], w_o[:, k, :],
                                            start=k == 0, stop=k == KD - 1)
                last.then_inc(wo_ps, 1)

            pe.wait_ge(ident_ready, 1)
            pe.wait_ge(wq_scaled, 2)
            transpose_x(0, 0)
            transpose_x(1, 1)
            for j in range(2):
                for k in range(KD):
                    project_qk(j, j, k)
                project_v(j, j)
            for n in range(4):
                transpose_parts(0, 0, n)

            def step(i, p, h):
                for s in range(16):
                    if s == 0:
                        wait(pe, k_T_moved[p], 8 * (i - p) + 16)
                    scores(i, p, s // 4, s % 4)
                    if s in PE_R and has(4 * i, -PE_R[s]):
                        g = PE_R[s] % 4
                        row_sums(i, 4 * i + PE_R[s], g)
                    if s == PE_OT and has(i, 2):
                        transpose_o(i - 2, p)
                    if s == PE_WO and has(i, 2):
                        output(i - 2, p)
                    if s == PE_XT:
                        transpose_x(i + 2, p)
                    if s in PE_T:
                        transpose_parts(i + 1, 1 - p, PE_T[s])
                    if s in PE_QK:
                        project_qk(i + 2, p, PE_QK.index(s))
                    if s == PE_V:
                        project_v(i + 2, p)

            run(pe, step)
            transpose_o(TILES - 2, 0)
            output(TILES - 2, 0)
            row_sums(TILES, 4 * TILES - 2, 2)
            row_sums(TILES, 4 * TILES - 1, 3)
            transpose_o(TILES - 1, 1)
            output(TILES - 1, 1)

    nc.clear_and_free_semaphores(sems)
    nc.all_engine_barrier()


MAX_REL = 256
SEQ = 512
BATCHES = T // SEQ
IB = SEQ // P
EXT = SEQ + P - 1 + SEQ - P
TOEP = 2 * SEQ - P


def build_bias_rows(nc, rel_bias, ext_sb, ext_d, ext_stored):
    NR = 2 * MAX_REL + 1
    LO = EXT // 2 - MAX_REL
    with ExitStack() as ctx:
        def sb(name, shape):
            return ctx.enter_context(nc.sbuf_tensor("rb_" + name, shape, F32))

        def sem(name):
            return ctx.enter_context(nc.semaphore("rb_" + name))

        r_t = sb("r_t", [P, NR // P, HEADS])
        r_last = sb("r_last", [1, HEADS])
        minus_flip = sb("minus_flip", [P, P])
        minus_one = sb("minus_one", [1, 1])
        flipped = ctx.enter_context(nc.psum_tensor("rb_flipped", [P, 512], F32))
        last_ps = ctx.enter_context(nc.psum_tensor("rb_last_ps", [P, 512], F32))
        loaded = sem("loaded")
        zeroed = sem("zeroed")
        flip_ready = sem("flip_ready")
        flip_ps = sem("flip_ps")
        mid_ready = sem("mid_ready")
        ext_ready = sem("ext_ready")
        block = ctx.enter_context(nc.Block())

        @block.sync
        def _(sp):
            sp.dma_start(r_t[:], rel_bias[0:NR - 1, :].rearrange("(a p) h -> p a h", p=P)).then_inc(loaded, 16)
            sp.dma_start(r_last[:], rel_bias[NR - 1:NR, :]).then_inc(loaded, 16)
            sp.wait_ge(ext_ready, 2)
            sp.dma_start(ext_d.rearrange("h (p w) -> h p w", w=EXT),
                         ext_sb[:].unsqueeze(1).broadcast_to([HEADS, P, EXT])).then_inc(ext_stored, 16)

        @block.gpsimd
        def _(pool):
            nc.gpsimd.memset(minus_flip[:], 0.0).then_inc(zeroed, 1)
            nc.gpsimd.memset(minus_one[:], -1.0).then_inc(flip_ready, 1)
            pool.wait_ge(zeroed, 1)
            nc.gpsimd.affine_select(out=minus_flip[:], in_=minus_flip[:], compare_op=ALU.not_equal, fill=-1.0,
                                    base=-(P - 1), pattern=[[1, P]], channel_multiplier=1).then_inc(flip_ready, 1)

        @block.tensor
        def _(pe):
            pe.wait_ge(loaded, 32)
            pe.wait_ge(flip_ready, 2)
            for a in range(NR // P):
                at = (NR // P - 1 - a) * P
                nc.tensor.matmul(flipped[0:HEADS, at:at + P], r_t[:, a, :], minus_flip[:], start=True, stop=True)
            nc.tensor.matmul(last_ps[0:HEADS, 0:1], r_last[:], minus_one[:], start=True, stop=True)\
                .then_inc(flip_ps, 1)

        @block.vector
        def _(dve):
            dve.wait_ge(flip_ps, 1)
            nc.vector.tensor_copy(ext_sb[:, LO + 1:LO + NR], flipped[0:HEADS, 0:NR - 1]).then_inc(mid_ready, 1)
            nc.vector.tensor_copy(ext_sb[:, 0:LO + 1], last_ps[0:HEADS, 0:1].broadcast_to([HEADS, LO + 1]))\
                .then_inc(ext_ready, 1)
            dve.wait_ge(mid_ready, 1)
            nc.vector.tensor_copy(ext_sb[:, LO + NR:EXT],
                                  ext_sb[:, LO + NR - 1:LO + NR].broadcast_to([HEADS, EXT - LO - NR]))\
                .then_inc(ext_ready, 1)


def build_attention_b(nc, x_in, W_qkv, b_qkv_d, W_out, b_out, x_out, ext_d, ext_stored):
    N = TILES
    with ExitStack() as ctx:
        def sb(name, shape, dt=F32):
            return ctx.enter_context(nc.sbuf_tensor("ab_" + name, shape, dt))

        def pb(name):
            return ctx.enter_context(nc.psum_tensor("ab_" + name, [P, 512], F32))

        sems = []

        def sem(name):
            sems.append(nc.alloc_semaphore("ab_" + name))
            return sems[-1]

        VW = 32
        ident = sb("ident", [P, P])
        w_qkv = sb("w_qkv", [P, KD, 3 * D])
        w_o = sb("w_o", [P, KD, D])
        b_qkv = sb("b_qkv", [P, 3 * D])
        b_o = sb("b_o", [P, D])
        minus_half = sb("minus_half", [P, 1])
        toep = sb("toep", [P, HEADS, TOEP])
        x_t = sb("x_t", [P, 2, D])
        stats = sb("stats", [P, 6])
        mean_var = sb("mean_var", [P, 2, 2])
        rstd = sb("rstd", [P, 2])
        xn = sb("xn", [P, 2, D])
        xn_T = sb("xn_T", [P, KD, P])
        qk = sb("qk", [P, 2 * D])
        parts = sb("parts", [P, 2, HEADS, 4, DH])
        q_T = sb("q_T", [P, 2, HEADS // 2, SEQ], F32R)
        k_T = sb("k_T", [P, 2, HEADS // 2, SEQ], F32R)
        v_t = sb("v_t", [P, 2, IB, HEADS, VW])
        neg_max = sb("neg_max", [P, 4])
        e_t = sb("e_t", [P, 4, SEQ])
        e_T = sb("e_T", [P, 2, 4, IB, P])
        o_sb = sb("o_sb", [P, P])
        rec = sb("rec", [P, 4])
        o_t = sb("o_t", [P, 2, D])
        o_T = sb("o_T", [P, KD, P])
        x_p = sb("x_p", [P, 2, D])
        xb = sb("xb", [P, 2, D])
        y_t = sb("y_t", [P, 2, D])
        S = [pb(f"s{i}") for i in range(3)]
        ET = [pb(f"et{i}") for i in range(2)]
        O = pb("o")
        M = [pb(f"m{i}") for i in range(2)]

        w_loaded = sem("w_loaded")
        toep_loaded = sem("toep_loaded")
        wq_scaled = sem("wq_scaled")
        ident_zeroed = sem("ident_zeroed")
        ident_ready = sem("ident_ready")
        v_cleared = sem("v_cleared")
        v_ones = sem("v_ones")
        x_loaded = [sem(f"x_loaded{p}") for p in range(2)]
        xp_loaded = [sem(f"xp_loaded{p}") for p in range(2)]
        stats_done = sem("stats_done")
        mv_done = sem("mv_done")
        pool_step = sem("pool_step")
        xn_ready = sem("xn_ready")
        xt_ps = sem("xt_ps")
        xn_T_ready = sem("xn_T_ready")
        qk_ps = sem("qk_ps")
        v_ps = sem("v_ps")
        qk_ready = sem("qk_ready")
        v_ready = sem("v_ready")
        hi_ready = sem("hi_ready")
        parts_ready = sem("parts_ready")
        t_ps = sem("t_ps")
        t_by_act = sem("t_by_act")
        t_by_dve = sem("t_by_dve")
        s_done = sem("s_done")
        max_done = sem("max_done")
        exp_done = sem("exp_done")
        et_ps = sem("et_ps")
        et_by_act = sem("et_by_act")
        et_by_dve = sem("et_by_dve")
        pv_done = sem("pv_done")
        o_copied = sem("o_copied")
        ot_ps = sem("ot_ps")
        rec_done = sem("rec_done")
        norm_done = sem("norm_done")
        oT_ps = sem("oT_ps")
        o_T_ready = sem("o_T_ready")
        wo_ps = sem("wo_ps")
        xb_ready = sem("xb_ready")
        y_ready = sem("y_ready")
        y_stored = [sem(f"y_stored{p}") for p in range(2)]
        block = ctx.enter_context(nc.Block())
        AHEAD = IB
        BODY = 2 * IB

        def run(eng, step):
            for k in range(BODY):
                step(k, k)
            with eng.Fori(1, N // BODY) as u:
                for k in range(BODY):
                    step(BODY * u + k, k)

        def own(j, k):
            return 8 * (j - k % 2) + 16

        @block.sync
        def _(sp):
            def load_x(j, k):
                tile = j % N if isinstance(j, int) else sp.snap(j % N, min_val=0, max_val=N - 1)
                wait(sp, xn_ready, j - 1)
                sp.dma_start(x_t[:, k % 2, :], x_in[bass.ts(tile, P), :]).then_inc(x_loaded[k % 2], 16)

            def load_xp(i, k):
                wait(sp, xb_ready, i - 1)
                sp.dma_start(x_p[:, k % 2, :], x_in[bass.ts(i, P), :]).then_inc(xp_loaded[k % 2], 16)

            def store_y(j, k):
                wait(sp, y_ready, j + 1)
                sp.dma_start(x_out[bass.ts(j, P), :], y_t[:, k % 2, :]).then_inc(y_stored[k % 2], 16)

            sp.dma_start(w_qkv[:], W_qkv.rearrange("(k p) n -> p k n", p=P)).then_inc(w_loaded, 16)
            sp.dma_start(b_qkv[:], b_qkv_d.partition_broadcast(P)).then_inc(w_loaded, 16)
            sp.dma_start(w_o[:], W_out.rearrange("(k p) n -> p k n", p=P)).then_inc(w_loaded, 16)
            sp.dma_start(b_o[:], b_out.partition_broadcast(P)).then_inc(w_loaded, 16)
            load_x(0, 0)
            load_x(1, 1)
            sp.wait_ge(ext_stored, 16)
            sp.dma_start(toep[:], ext_d[:, P - 1:P - 1 + P * (EXT - 1)].rearrange("h (p w) -> p h w", w=EXT - 1)
                         [:, :, 0:TOEP]).then_inc(toep_loaded, 16)
            for j in range(2, AHEAD + 1):
                load_x(j, j)

            def step(i, k):
                load_x(i + AHEAD + 1, k + AHEAD + 1)
                load_xp(i, k)
                if not (isinstance(i, int) and i == 0):
                    store_y(i - 1, k + 1)

            run(sp, step)
            store_y(N - 1, N - 1)
            for p in range(2):
                sp.wait_ge(y_stored[p], 16 * (N // 2))

        @block.gpsimd
        def _(pool):
            nc.gpsimd.memset(ident[:], 0.0).then_inc(ident_zeroed, 1)
            nc.gpsimd.memset(minus_half[:], -0.5).then_inc(ident_zeroed, 1)
            nc.gpsimd.memset(v_t[:], 0.0).then_inc(v_cleared, 1)
            pool.wait_ge(ident_zeroed, 2)
            nc.gpsimd.affine_select(out=ident[:], in_=ident[:], compare_op=ALU.not_equal, fill=1.0, base=0,
                                    pattern=[[-1, P]], channel_multiplier=1).then_inc(ident_ready, 1)
            pool.wait_ge(v_cleared, 1)
            nc.gpsimd.memset(v_t[:].rearrange("p b i h w -> p (b i h) w")[:, :, DH:DH + 1], 1.0).then_inc(v_ones, 1)

            def normalise(j, k):
                p = k % 2
                wait_apart(pool, mv_done, j + 1)
                nc.gpsimd.tensor_scalar(rstd[:, p:p + 1], mean_var[:, p, 1:2], EPS, None, ALU.add)\
                    .then_inc(pool_step, 1)
                wait(pool, pool_step, 2 * j + 1)
                nc.gpsimd.tensor_tensor(rstd[:, p:p + 1], rstd[:, p:p + 1], minus_half[:], ALU.pow)\
                    .then_inc(pool_step, 1)
                wait(pool, pool_step, 2 * j + 2)
                wait_apart(pool, xt_ps, j - 1)
                nc.gpsimd.tensor_scalar(xn[:, p, :], x_t[:, p, :], mean_var[:, p, 0:1], rstd[:, p:p + 1],
                                        ALU.subtract, ALU.mult).then_inc(xn_ready, 1)

            def split(j):
                wait(pool, qk_ready, j + 1)
                wait_apart(pool, t_ps, 4 * j)
                dup = [parts[:, 0, :, 0:2, :], parts[:, 1, :, 0:4:2, :]]
                low = [parts[:, 0, :, 2:4, :], parts[:, 1, :, 1:4:2, :]]
                src = [qk[:, m * D:(m + 1) * D].rearrange("p (h x) -> p h x", x=DH).unsqueeze(1)
                       .broadcast_to([P, 2, HEADS, DH]) for m in range(2)]
                turn = "p h a x -> p a h x"
                for m in range(2):
                    nc.gpsimd.tensor_scalar(dup[m].rearrange(turn).bitcast(F32R), src[m], 1.0, None, ALU.mult)\
                        .then_inc(hi_ready, 1)
                for m in range(2):
                    wait(pool, hi_ready, 2 * j + 1 + m)
                    nc.gpsimd.tensor_tensor(low[m].rearrange(turn).bitcast(F32R), src[m], dup[m].rearrange(turn),
                                            ALU.subtract).then_inc(parts_ready, 1)

            def add_bias(i, k):
                wait(pool, xp_loaded[k % 2], own(i, k))
                wait(pool, y_ready, i - 1)
                nc.gpsimd.tensor_tensor(xb[:, k % 2, :], x_p[:, k % 2, :], b_o[:], ALU.add).then_inc(xb_ready, 1)

            pool.wait_ge(w_loaded, 4 * 16)
            normalise(0, 0)
            for j in range(AHEAD):
                normalise(j + 1, j + 1)
                split(j)

            def step(i, k):
                add_bias(i, k)
                split(i + AHEAD)
                normalise(i + AHEAD + 1, k + AHEAD + 1)

            run(pool, step)

        def t_out(n, k):
            dst = (q_T, k_T)[n // 2]
            at = k % IB * P
            return dst[:, k // IB % 2, n % 2 * 4:n % 2 * 4 + 4, at:at + P]

        T_BANK = [0, 1, 0, 0]
        XT_BANK, QK_BANK, V_BANK, OUT_BANK = 0, 0, 1, 1
        OT_BANK = [0, 1, 1, 0]

        def psum_heads(a):
            return a.rearrange("p (c t) -> p c t", c=4)

        @block.scalar
        def _(act):
            def copy_xn_T(j):
                wait(act, xt_ps, j + 1)
                wait(act, v_ps, j)
                nc.scalar.activation(xn_T[:], M[XT_BANK][:, 0:D].rearrange("p (k t) -> p k t", k=KD), ACT.Copy)\
                    .then_inc(xn_T_ready, 1)

            def copy_t(j, k, n):
                wait(act, t_ps, 4 * j + n + 1)
                wait(act, s_done, 16 * (j - k % IB - IB))
                nc.scalar.activation(t_out(n, k), psum_heads(M[T_BANK[n]][:]), ACT.Copy).then_inc(t_by_act, 1)

            def exp(i, s):
                wait(act, max_done, 16 * i + s + 1)
                q = s % 4
                nc.scalar.activation(e_t[:, q, :], e_t[:, q, :], ACT.Exp, bias=neg_max[:, q:q + 1], scale=-1.0)\
                    .then_inc(exp_done, 1)

            def copy_et(i, s):
                g = s // 4
                wait(act, et_ps, 16 * i + s + 1)
                if s % 4 == 0:
                    wait(act, pv_done, 4 * i + g - 1)
                nc.scalar.activation(e_T[:, g % 2, s % 4, :, :], psum_heads(ET[0][:]), ACT.Copy).then_inc(et_by_act, 1)

            def copy_o(group):
                wait(act, pv_done, group + 1)
                wait(act, ot_ps, group)
                nc.scalar.activation(o_sb[:], O[:, 0:P], ACT.Copy).then_inc(o_copied, 1)

            def copy_o_T(j):
                wait(act, oT_ps, j + 1)
                wait(act, wo_ps, j)
                nc.scalar.activation(o_T[:], M[OUT_BANK][:, 0:D].rearrange("p (k t) -> p k t", k=KD), ACT.Copy)\
                    .then_inc(o_T_ready, 1)

            for j in range(AHEAD):
                copy_xn_T(j)
                for n in (0, 2, 3):
                    copy_t(j, j, n)

            def step(i, k):
                start = isinstance(i, int) and i == 0
                for s in range(16):
                    exp(i, s)
                    if s == 15:
                        copy_t(i + AHEAD, k + AHEAD, 2)
                    if s % 2 == 1 and not (start and s < 3):
                        copy_et(i, s - 3)
                    if s % 4 == 1 and not (start and s < 8):
                        copy_o(4 * i + s // 4 - 2)
                    if s == 2:
                        copy_xn_T(i + AHEAD)
                    if s == 9 and not start:
                        copy_o_T(i - 1)
                    if s == 13:
                        copy_t(i + AHEAD, k + AHEAD, 0)
                    if s == 15:
                        copy_t(i + AHEAD, k + AHEAD, 3)

            run(act, step)
            copy_et(N, -2)
            copy_o(4 * N - 2)
            copy_o(4 * N - 1)
            copy_o_T(N - 1)

        @block.vector
        def _(dve):
            def statistics(j, k):
                wait(dve, x_loaded[k % 2], own(j, k))
                wait(dve, mv_done, j)
                nc.vector.bn_stats(stats[:], x_t[:, k % 2, :]).then_inc(stats_done, 1)
                wait(dve, stats_done, j + 1)
                wait_apart(dve, xn_ready, j - 1)
                nc.vector.bn_aggr(mean_var[:, k % 2, :], stats[:]).then_inc(mv_done, 1)

            def add_qk(j):
                wait(dve, qk_ps, j + 1)
                wait(dve, parts_ready, 2 * j)
                nc.vector.tensor_tensor(qk[:], M[QK_BANK][:], b_qkv[:, 0:2 * D], ALU.add).then_inc(qk_ready, 1)

            def add_v(j, k):
                wait(dve, v_ps, j + 1)
                wait(dve, pv_done, 4 * (j - k % IB - IB))
                nc.vector.tensor_tensor(v_t[:, k // IB % 2, k % IB, :, 0:DH],
                                        M[V_BANK][:, 0:D].rearrange("p (h x) -> p h x", x=DH),
                                        b_qkv[:, 2 * D:3 * D].rearrange("p (h x) -> p h x", x=DH), ALU.add)\
                    .then_inc(v_ready, 1)

            def copy_t(j, k, n):
                wait(dve, t_ps, 4 * j + n + 1)
                wait(dve, s_done, 16 * (j - k % IB - IB))
                nc.vector.tensor_copy(t_out(n, k), psum_heads(M[T_BANK[n]][:])).then_inc(t_by_dve, 1)

            def add_bias(i, k, s):
                n = 16 * i + s
                at = SEQ - P - k % IB * P
                wait(dve, s_done, n + 1)
                wait_apart(dve, et_ps, n - 3)
                nc.vector.tensor_tensor_reduce(out=e_t[:, s % 4, :], in0=S[(k * 16 + s) % 3][:],
                                               in1=toep[:, s, at:at + SEQ], scale=1.0, scalar=3.0e38, op0=ALU.add,
                                               op1=ALU.min, accum_out=neg_max[:, s % 4:s % 4 + 1])\
                    .then_inc(max_done, 1)

            def copy_et(i, s):
                g = s // 4
                wait(dve, et_ps, 16 * i + s + 1)
                if s % 4 == 1:
                    wait(dve, pv_done, 4 * i + g - 1)
                nc.vector.tensor_copy(e_T[:, g % 2, s % 4, :, :], psum_heads(ET[1][:])).then_inc(et_by_dve, 1)

            def normalise(group, gk):
                heads = M[OT_BANK[gk % 4]][:, 0:P].rearrange("p (h w) -> p h w", w=VW)
                wait(dve, ot_ps, group + 1)
                wait(dve, norm_done, group)
                nc.vector.reciprocal(rec[:], heads[:, :, DH]).then_inc(rec_done, 1)
                wait(dve, rec_done, group + 1)
                at = gk % 4 * 4 * DH
                nc.vector.tensor_tensor(o_t[:, gk // 4 % 2, at:at + 4 * DH].rearrange("p (h x) -> p h x", x=DH),
                                        heads[:, :, 0:DH], rec[:].unsqueeze(2).broadcast_to([P, 4, DH]), ALU.mult)\
                    .then_inc(norm_done, 1)

            def add_residual(j, k):
                wait(dve, wo_ps, j + 1)
                wait(dve, xb_ready, j + 1)
                wait(dve, y_stored[k % 2], own(j, k) - 16)
                nc.vector.tensor_tensor(y_t[:, k % 2, :], M[OUT_BANK][:, 0:D], xb[:, k % 2, :], ALU.add)\
                    .then_inc(y_ready, 1)

            dve.wait_ge(w_loaded, 4 * 16)
            dve.wait_ge(v_ones, 1)
            nc.vector.tensor_scalar(w_qkv[:, :, 0:D], w_qkv[:, :, 0:D], -1.0 / DH ** 0.5, None, ALU.mult)\
                .then_inc(wq_scaled, 1)
            nc.vector.tensor_scalar(b_qkv[:, 0:D], b_qkv[:, 0:D], -1.0 / DH ** 0.5, None, ALU.mult)\
                .then_inc(wq_scaled, 1)
            dve.wait_ge(wq_scaled, 2)
            statistics(0, 0)
            for j in range(AHEAD):
                statistics(j + 1, j + 1)
                add_qk(j)
                add_v(j, j)
                copy_t(j, j, 1)
            dve.wait_ge(toep_loaded, 16)

            def step(i, k):
                start = isinstance(i, int) and i == 0
                for s in range(16):
                    add_bias(i, k, s)
                    if s == 14:
                        copy_t(i + AHEAD, k + AHEAD, 1)
                    if s % 2 == 0 and not (start and s < 4):
                        copy_et(i, s - 3)
                    if s % 4 == 3 and not (start and s < 8):
                        g = s // 4 - 2
                        if g == 0:
                            wait(dve, oT_ps, i - 1)
                        normalise(4 * i + g, 4 * k + g)
                    if s == 4:
                        add_qk(i + AHEAD)
                    if s == 6:
                        add_v(i + AHEAD, k + AHEAD)
                    if s == 11 and not start:
                        add_residual(i - 1, k + 1)
                    if s == 15:
                        statistics(i + AHEAD + 1, k + AHEAD + 1)

            run(dve, step)
            copy_et(N, -3)
            copy_et(N, -1)
            normalise(4 * N - 2, 4 * BODY - 2)
            normalise(4 * N - 1, 4 * BODY - 1)
            add_residual(N - 1, BODY - 1)

        @block.tensor
        def _(pe):
            def transpose_x(j, k):
                wait(pe, xn_ready, j + 1)
                wait(pe, t_by_act, 3 * j)
                for c in range(KD):
                    last = nc.tensor.transpose(M[XT_BANK][:, c * P:(c + 1) * P], xn[:, k % 2, c * P:(c + 1) * P],
                                               ident[:])
                last.then_inc(xt_ps, 1)

            def project_qk(j):
                wait(pe, xn_T_ready, j + 1)
                for c in range(KD):
                    last = nc.tensor.matmul(M[QK_BANK][:], xn_T[:, c, :], w_qkv[:, c, 0:2 * D],
                                            start=c == 0, stop=c == KD - 1)
                last.then_inc(qk_ps, 1)

            def project_v(j, group):
                wait(pe, norm_done, group)
                wait(pe, t_by_dve, j)
                for c in range(KD):
                    last = nc.tensor.matmul(M[V_BANK][:, 0:D], xn_T[:, c, :], w_qkv[:, c, 2 * D:3 * D],
                                            start=c == 0, stop=c == KD - 1)
                last.then_inc(v_ps, 1)

            def transpose_parts(j, n, group):
                wait(pe, parts_ready, 2 * (j + 1))
                if n == 0:
                    wait(pe, qk_ready, j + 1)
                    wait(pe, norm_done, group)
                elif n == 1:
                    wait(pe, v_ready, j + 1)
                    wait(pe, y_ready, j - AHEAD)
                elif n == 2:
                    wait(pe, t_by_act, 3 * j + 1)
                else:
                    wait(pe, t_by_act, 3 * j + 2)
                for c in range(4):
                    m = n % 2 * 4 + c
                    last = nc.tensor.transpose(M[T_BANK[n]][:, c * P:(c + 1) * P],
                                               parts[:, n // 2, 2 * m:2 * m + 2, :, :]
                                               .rearrange("p h a x -> p (h a x)"), ident[:])
                last.then_inc(t_ps, 1)

            def scores(i, k, s):
                n = 16 * i + s
                wait(pe, max_done, n - 2)
                if s == 0 and k % IB == 0:
                    wait(pe, t_by_act, 3 * (i + IB))
                    wait(pe, t_by_dve, i + IB)
                lo, at = s % 2 * 64, k % IB * P
                nc.tensor.matmul(S[(k * 16 + s) % 3][:], q_T[lo:lo + 64, k // IB % 2, s // 2, at:at + P],
                                 k_T[lo:lo + 64, k // IB % 2, s // 2, :], start=True, stop=True).then_inc(s_done, 1)

            def transpose_e(i, s):
                n = 16 * i + s
                wait(pe, exp_done, n + 1)
                wait(pe, et_by_dve if s % 2 else et_by_act, 8 * i + s // 2)
                for c in range(IB):
                    last = nc.tensor.transpose(ET[s % 2][:, c * P:(c + 1) * P], e_t[:, s % 4, c * P:(c + 1) * P],
                                               ident[:])
                last.then_inc(et_ps, 1)

            def values(group, gk):
                wait(pe, et_by_act, 2 * (group + 1))
                wait(pe, et_by_dve, 2 * (group + 1))
                wait(pe, o_copied, group)
                b = gk // (4 * IB) % 2
                for c in range(IB):
                    for q in range(4):
                        last = nc.tensor.matmul(O[q * VW:(q + 1) * VW, 0:P], v_t[:, b, c, gk % 4 * 4 + q, :],
                                                e_T[:, gk % 2, q, c, :], start=c == 0, stop=c == IB - 1)
                last.then_inc(pv_done, 1)

            def transpose_o(group, gk, i):
                wait(pe, o_copied, group + 1)
                g = gk % 4
                if g == 0:
                    wait(pe, norm_done, group)
                elif g == 1:
                    wait(pe, t_by_dve, i + AHEAD + 1)
                elif g == 2:
                    wait(pe, norm_done, group)
                else:
                    wait(pe, qk_ready, i + AHEAD + 1)
                nc.tensor.transpose(M[OT_BANK[g]][:, 0:P], o_sb[:], ident[:]).then_inc(ot_ps, 1)

            def transpose_out(j, k, bank_free):
                wait(pe, norm_done, 4 * (j + 1))
                bank_free()
                for c in range(KD):
                    last = nc.tensor.transpose(M[OUT_BANK][:, c * P:(c + 1) * P], o_t[:, k % 2, c * P:(c + 1) * P],
                                               ident[:])
                last.then_inc(oT_ps, 1)

            def output(j):
                wait(pe, o_T_ready, j + 1)
                for c in range(KD):
                    last = nc.tensor.matmul(M[OUT_BANK][:, 0:D], o_T[:, c, :], w_o[:, c, :],
                                            start=c == 0, stop=c == KD - 1)
                last.then_inc(wo_ps, 1)

            pe.wait_ge(ident_ready, 1)
            pe.wait_ge(wq_scaled, 2)
            for j in range(AHEAD):
                transpose_x(j, j)
                project_qk(j)
                project_v(j, 0)
                for n in range(4):
                    transpose_parts(j, n, 0)

            def step(i, k):
                start = isinstance(i, int) and i == 0
                m = i + AHEAD
                for s in range(16):
                    scores(i, k, s)
                    if s % 4 == 0 and not (start and s < 8):
                        values(4 * i + s // 4 - 2, 4 * k + s // 4 - 2)
                    if s == 1:
                        transpose_x(m, k + AHEAD)
                    if s % 4 == 2 and not (start and s < 8):
                        transpose_o(4 * i + s // 4 - 2, 4 * k + s // 4 - 2, i)
                    if s == 3:
                        project_qk(m)
                    if s == 5:
                        project_v(m, 4 * i - 1)
                    if s == 8 and not start:
                        transpose_out(i - 1, k + 1, lambda: wait(pe, v_ready, m + 1))
                    if s == 10 and not start:
                        output(i - 1)
                    if s == 12:
                        transpose_parts(m, 0, 4 * i + 1)
                    if s == 13:
                        transpose_parts(m, 1, 0)
                    if s == 14:
                        transpose_parts(m, 2, 0)
                    if s == 15:
                        transpose_parts(m, 3, 0)
                    if not (start and s < 3):
                        transpose_e(i, s - 3)

            run(pe, step)
            for s in (-3, -2, -1):
                transpose_e(N, s)
            values(4 * N - 2, 4 * BODY - 2)
            transpose_o(4 * N - 2, 4 * BODY - 2, N)
            values(4 * N - 1, 4 * BODY - 1)
            transpose_o(4 * N - 1, 4 * BODY - 1, N - 1)
            transpose_out(N - 1, 1, lambda: None)
            output(N - 1)

    nc.clear_and_free_semaphores(sems)
    nc.all_engine_barrier()


I32 = mybir.dt.int32
U32 = mybir.dt.uint32

E = 8
TOP = 2
FF = 512
KF = FF // P
SLOT_TILES = TOP * TILES + E
ALL_TILES = TILES + SLOT_TILES


def pairs(eng, step):
    for p in range(2):
        step(0, p)
    with eng.Fori(1, TILES // 2) as h:
        for p in range(2):
            step(h, p)


def build_ffn(nc, tag, x_in, Wg, Ws1, Ws3, Ws2, We1, We3, We2, x_out, rows_d, y_d, zero_fill):
    with ExitStack() as ctx:
        def sb(name, shape, dt=F32):
            return ctx.enter_context(nc.sbuf_tensor(tag + name, shape, dt))

        def sem(name):
            return ctx.enter_context(nc.semaphore(tag + name))

        ident = sb("ident", [P, P])
        w_up = sb("w_up", [P, E + 1, KD, 2 * FF])
        w_down = sb("w_down", [P, E + 1, KF, D])
        logits = sb("logits", [P, TILES, E])
        slots = sb("slots", [P, TILES, TOP], U32)
        mix = sb("mix", [P, TILES, TOP])
        tile_expert = sb("tile_expert", [1, ALL_TILES], I32)
        consts_ready = sem("consts_ready")
        w_loaded = sem("w_loaded")
        shared_loaded = sem("shared_loaded")

        with ExitStack() as c1:
            def sb1(name, shape, dt=F32):
                return c1.enter_context(nc.sbuf_tensor(tag + name, shape, dt))

            def sem1(name):
                return c1.enter_context(nc.semaphore(tag + name))

            w_g = sb1("w_g", [P, KD, E])
            zeros = sb1("zeros", [P, 2, D])
            minus_half = sb1("minus_half", [P, 1])
            x_t = sb1("x_t", [P, 2, D])
            stats = sb1("stats", [P, 6])
            mean_var = sb1("mean_var", [P, 2, 2])
            rstd = sb1("rstd", [P, 2])
            xn = sb1("xn", [P, 2, D])
            xn_T = sb1("xn_T", [P, 2, KD, P])
            XT = [c1.enter_context(nc.psum_tensor(tag + f"xt{i}", [P, 512], F32)) for i in range(2)]
            GL = [c1.enter_context(nc.psum_tensor(tag + f"gl{i}", [P, 512], F32)) for i in range(2)]
            wg_loaded = sem1("wg_loaded")
            x_loaded = [sem1(f"x_loaded{p}") for p in range(2)]
            stats_done = sem1("stats_done")
            mv_done = sem1("mv_done")
            pool_step = sem1("pool_step")
            xn_ready = sem1("xn_ready")
            xn_stored = [sem1(f"xn_stored{p}") for p in range(2)]
            xt_ps = sem1("xt_ps")
            xn_T_ready = sem1("xn_T_ready")
            gl_ps = sem1("gl_ps")
            gl_copied = sem1("gl_copied")
            zero_filled = sem1("zero_filled")
            block = c1.enter_context(nc.Block())

            @block.sync
            def _(sp):
                sp.dma_start(w_g[:], Wg.rearrange("(k p) n -> p k n", p=P)).then_inc(wg_loaded, 16)

                def step(h, p):
                    j = 2 * h + p
                    wait(sp, xn_ready, j - 1)
                    sp.dma_start(x_t[:, p, :], x_in[bass.ts(j, P), :]).then_inc(x_loaded[p], 16)

                pairs(sp, step)

            @block.scalar
            def _(act):
                def load_w(e, w1, w3, w2, loaded):
                    act.dma_start(w_up[:, e, :, 0:FF], w1.rearrange("(k p) n -> p k n", p=P)).then_inc(loaded, 16)
                    act.dma_start(w_up[:, e, :, FF:2 * FF], w3.rearrange("(k p) n -> p k n", p=P))\
                        .then_inc(loaded, 16)
                    act.dma_start(w_down[:, e, :, :], w2.rearrange("(k p) n -> p k n", p=P)).then_inc(loaded, 16)

                load_w(E, Ws1, Ws3, Ws2, shared_loaded)
                for e in range(E):
                    load_w(e, We1[e], We3[e], We2[e], w_loaded)
                if zero_fill:
                    act.wait_ge(consts_ready, 3)
                    with act.Fori(0, SLOT_TILES // 2) as q:
                        act.dma_start(rows_d[bass.ds(TILES * P + q * 2 * P, 2 * P), :]
                                      .rearrange("(a p) n -> p a n", p=P), zeros[:]).then_inc(zero_filled, 16)

                def step(h, p):
                    j = 2 * h + p
                    wait(act, xt_ps, j + 1)
                    wait(act, gl_ps, j - 1)
                    nc.scalar.activation(xn_T[:, p, :, :], XT[p][:, 0:D].rearrange("p (k t) -> p k t", k=KD),
                                         ACT.Copy).then_inc(xn_T_ready, 1)

                pairs(act, step)
                if zero_fill:
                    act.wait_ge(zero_filled, 16 * (SLOT_TILES // 2))

            @block.gpsimd
            def _(pool):
                nc.gpsimd.memset(ident[:], 0.0).then_inc(consts_ready, 1)
                nc.gpsimd.memset(minus_half[:], -0.5).then_inc(consts_ready, 1)
                nc.gpsimd.memset(zeros[:], 0.0).then_inc(consts_ready, 1)
                pool.wait_ge(consts_ready, 3)
                nc.gpsimd.affine_select(out=ident[:], in_=ident[:], compare_op=ALU.not_equal, fill=1.0, base=0,
                                        pattern=[[-1, P]], channel_multiplier=1).then_inc(consts_ready, 1)

                def step(h, p):
                    j = 2 * h + p
                    wait_apart(pool, mv_done, j + 1)
                    nc.gpsimd.tensor_scalar(rstd[:, p:p + 1], mean_var[:, p, 1:2], EPS, None, ALU.add)\
                        .then_inc(pool_step, 1)
                    wait(pool, pool_step, 2 * j + 1)
                    nc.gpsimd.tensor_tensor(rstd[:, p:p + 1], rstd[:, p:p + 1], minus_half[:], ALU.pow)\
                        .then_inc(pool_step, 1)
                    wait(pool, pool_step, 2 * j + 2)
                    wait(pool, xt_ps, j - 1)
                    wait_apart(pool, xn_stored[p], 16 * h)
                    nc.gpsimd.tensor_scalar(xn[:, p, :], x_t[:, p, :], mean_var[:, p, 0:1], rstd[:, p:p + 1],
                                            ALU.subtract, ALU.mult).then_inc(xn_ready, 1)
                    wait(pool, xn_ready, j + 1)
                    pool.dma_start(rows_d[bass.ts(j, P), :], xn[:, p, :]).then_inc(xn_stored[p], 16)

                pairs(pool, step)
                for p in range(2):
                    pool.wait_ge(xn_stored[p], 16 * (TILES // 2))

            @block.vector
            def _(dve):
                def step(h, p):
                    j = 2 * h + p
                    wait(dve, x_loaded[p], 16 * h + 16)
                    wait(dve, mv_done, j)
                    nc.vector.bn_stats(stats[:], x_t[:, p, :]).then_inc(stats_done, 1)
                    wait(dve, stats_done, j + 1)
                    wait_apart(dve, xn_ready, j - 1)
                    nc.vector.bn_aggr(mean_var[:, p, :], stats[:]).then_inc(mv_done, 1)
                    if p:
                        for q in range(2):
                            wait(dve, gl_ps, 2 * h + q + 1)
                            nc.vector.tensor_copy(logits[:, 2 * h + q, :], GL[q][:, 0:E]).then_inc(gl_copied, 1)

                pairs(dve, step)

            @block.tensor
            def _(pe):
                pe.wait_ge(consts_ready, 4)
                pe.wait_ge(wg_loaded, 16)

                def step(h, p):
                    j = 2 * h + p
                    wait(pe, xn_ready, j + 1)
                    wait(pe, xn_T_ready, j)
                    for k in range(KD):
                        last = nc.tensor.transpose(XT[p][:, k * P:(k + 1) * P], xn[:, p, k * P:(k + 1) * P], ident[:])
                    last.then_inc(xt_ps, 1)
                    wait(pe, xn_T_ready, j + 1)
                    wait(pe, gl_copied, 2 * h)
                    for k in range(KD):
                        last = nc.tensor.matmul(GL[p][:, 0:E], xn_T[:, p, k, :], w_g[:, k, :],
                                                start=k == 0, stop=k == KD - 1)
                    last.then_inc(gl_ps, 1)

                pairs(pe, step)

        with ExitStack() as c2:
            def sb2(name, shape, dt=F32):
                return c2.enter_context(nc.sbuf_tensor(tag + name, shape, dt))

            def sem2(name):
                return c2.enter_context(nc.semaphore(tag + name))

            def pb2(name):
                return c2.enter_context(nc.psum_tensor(tag + name, [P, 512], F32))

            below = sb2("below", [P, P])
            ones = sb2("ones", [P, P])
            rank8 = sb2("rank8", [P, E])
            rank8_i = sb2("rank8_i", [P, E], I32)
            tile_no = sb2("tile_no", [1, SLOT_TILES])
            tile_no_i = sb2("tile_no_i", [1, SLOT_TILES], I32)
            gates = sb2("gates", [P, TILES, E])
            top = sb2("top", [P, TOP, TILES])
            pick = sb2("pick", [P, TILES, E])
            first = sb2("first", [P, TILES])
            hot = sb2("hot", [P, TOP, TILES, E])
            mask = sb2("mask", [P, TILES, E])
            total = sb2("total", [P, 2, TILES, E])
            ends = sb2("ends", [P, 2, E])
            n_tiles = sb2("n_tiles", [P, E])
            n_int = sb2("n_int", [P, E], I32)
            slot = sb2("slot", [P, TILES, E])
            picked = sb2("picked", [P, TILES, E])
            slot_f = sb2("slot_f", [P, TOP, TILES])
            tile_ge = sb2("tile_ge", [1, SLOT_TILES, E - 1])
            tile_e_f = sb2("tile_e_f", [1, SLOT_TILES])
            idx = sb2("idx", [P, 2, TOP], U32)
            x_sc = sb2("x_sc", [P, 2, D])
            x_t = sb2("x_t2", [P, 2, D])
            x_T = sb2("x_T", [P, 2, KD, P])
            gate = sb2("gate", [P, 2, FF])
            hid = sb2("hid", [P, 2, FF])
            hid_T = sb2("hid_T", [P, 2, KF, P])
            y_t = sb2("y_t", [P, 2, D])
            A = [pb2(f"a{i}") for i in range(2)]
            B = [pb2(f"b{i}") for i in range(2)]
            X = pb2("x")
            H = pb2("h")
            Y = [pb2(f"y{i}") for i in range(2)]

            route_consts = sem2("route_consts")
            gates_ready = sem2("gates_ready")
            chain = sem2("chain")
            mask_ready = sem2("mask_ready")
            counts_ps = sem2("counts_ps")
            routed = sem2("routed")
            idx_ready = sem2("idx_ready")
            sc_loaded = [sem2(f"sc_loaded{p}") for p in range(2)]
            scattered = [sem2(f"scattered{p}") for p in range(2)]
            x_loaded = [sem2(f"x_loaded2{p}") for p in range(2)]
            x_ps = sem2("x_ps")
            x_T_ready = sem2("x_T_ready")
            a_ps = sem2("a_ps")
            b_ps = sem2("b_ps")
            gate_ready = sem2("gate_ready")
            hid_ready = sem2("hid_ready")
            h_ps = sem2("h_ps")
            hid_T_ready = sem2("hid_T_ready")
            y_ps = sem2("y_ps")
            y_ready = sem2("y_ready")
            y_stored = [sem2(f"y_stored{p}") for p in range(2)]
            block = c2.enter_context(nc.Block())
            PAIRS = ALL_TILES // 2

            @block.sync
            def _(sp):
                def load_x(t, p):
                    wait(sp, x_ps, t - 1)
                    sp.dma_start(x_t[:, p, :], rows_d[bass.ts(t, P), :]).then_inc(x_loaded[p], 16)

                def store_y(t, p):
                    wait(sp, y_ready, t + 1)
                    sp.dma_start(y_d[bass.ts(t, P), :], y_t[:, p, :]).then_inc(y_stored[p], 16)

                load_x(0, 0)
                load_x(1, 1)
                with sp.Fori(1, TILES // 2) as h:
                    for p in range(2):
                        load_x(2 * h + p, p)
                        store_y(2 * h + p - 2, p)
                for p in range(2):
                    sp.wait_ge(scattered[p], 16 * TOP * (TILES // 2))
                with sp.Fori(TILES // 2, PAIRS) as h:
                    for p in range(2):
                        load_x(2 * h + p, p)
                        store_y(2 * h + p - 2, p)
                for p in range(2):
                    store_y(ALL_TILES - 2 + p, p)
                for p in range(2):
                    sp.wait_ge(y_stored[p], 16 * PAIRS)

            @block.gpsimd
            def _(pool):
                nc.gpsimd.memset(ones[:], 1.0).then_inc(route_consts, 1)
                nc.gpsimd.memset(below[:], 1.0).then_inc(route_consts, 1)
                nc.gpsimd.iota(rank8_i[:], pattern=[[-1, E]], base=E, channel_multiplier=0).then_inc(route_consts, 1)
                nc.gpsimd.iota(tile_no_i[:], pattern=[[1, SLOT_TILES]], base=0, channel_multiplier=0)\
                    .then_inc(route_consts, 1)
                pool.wait_ge(route_consts, 4)
                nc.gpsimd.affine_select(out=below[:], in_=below[:], compare_op=ALU.is_gt, fill=0.0, base=0,
                                        pattern=[[1, P]], channel_multiplier=-1).then_inc(route_consts, 1)
                nc.gpsimd.tensor_copy(rank8[:], rank8_i[:]).then_inc(route_consts, 1)
                nc.gpsimd.tensor_copy(tile_no[:], tile_no_i[:]).then_inc(route_consts, 1)
                pool.wait_ge(routed, 1)

                def scatter(h, p):
                    if p == 0:
                        for q in range(2):
                            wait(pool, scattered[q], 16 * TOP * h)
                            pool.dma_start(x_sc[:, q, :], rows_d[bass.ts(2 * h + q, P), :]).then_inc(sc_loaded[q], 16)
                            nc.gpsimd.tensor_copy(idx[:, q, :], slots[:, 2 * h + q, :]).then_inc(idx_ready, 1)
                    wait(pool, sc_loaded[p], 16 * h + 16)
                    wait_apart(pool, idx_ready, 2 * h + 2)
                    for k in range(TOP):
                        pool.indirect_dma_start(out=rows_d[:, :],
                                                out_offset=bass.IndirectOffsetOnAxis(ap=idx[:, p, k:k + 1], axis=0),
                                                in_=x_sc[:, p, :], in_offset=None).then_inc(scattered[p], 16)

                pairs(pool, scatter)
                for p in range(2):
                    pool.wait_ge(scattered[p], 16 * TOP * (TILES // 2))

            @block.scalar
            def _(act):
                nc.scalar.activation(gates[:], logits[:], ACT.Sigmoid).then_inc(gates_ready, 1)

                def copy_x_T(t, p):
                    wait(act, x_ps, t + 1)
                    wait(act, b_ps, t - 1)
                    nc.scalar.activation(x_T[:, p, :, :], X[:, 0:D].rearrange("p (k t) -> p k t", k=KD), ACT.Copy)\
                        .then_inc(x_T_ready, 1)

                def silu(t, p):
                    wait(act, a_ps, t + 1)
                    wait(act, hid_ready, t - 1)
                    nc.scalar.activation(gate[:, p, :], A[p][:], ACT.Silu).then_inc(gate_ready, 1)

                def copy_hid_T(t, p):
                    wait(act, h_ps, t + 1)
                    wait(act, y_ps, t - 1)
                    nc.scalar.activation(hid_T[:, p, :, :], H[:].rearrange("p (k t) -> p k t", k=KF), ACT.Copy)\
                        .then_inc(hid_T_ready, 1)

                def step(t, p, start=False, end=False):
                    silu(t, p)
                    if not start:
                        copy_hid_T(t - 1, 1 - p)
                    if not end:
                        copy_x_T(t + 1, 1 - p)

                copy_x_T(0, 0)
                step(0, 0, start=True)
                step(1, 1)
                with act.Fori(1, PAIRS - 1) as h:
                    step(2 * h, 0)
                    step(2 * h + 1, 1)
                step(ALL_TILES - 2, 0)
                step(ALL_TILES - 1, 1, end=True)
                copy_hid_T(ALL_TILES - 1, 1)

            @block.vector
            def _(dve):
                links = [0]

                def link(instruction):
                    links[0] += 1
                    instruction.then_inc(chain, 1)
                    dve.wait_ge(chain, links[0])

                def over_experts(a):
                    return a.unsqueeze(2).broadcast_to([P, TILES, E])

                dve.wait_ge(gates_ready, 1)
                dve.wait_ge(route_consts, 7)
                for k in range(TOP):
                    link(nc.vector.tensor_reduce(top[:, k, :], gates[:], AX.X, ALU.max))
                    link(nc.vector.tensor_tensor(pick[:], gates[:], over_experts(top[:, k, :]), ALU.is_equal))
                    link(nc.vector.tensor_tensor(pick[:], pick[:], rank8[:].unsqueeze(1).broadcast_to([P, TILES, E]),
                                                 ALU.mult))
                    link(nc.vector.tensor_reduce(first[:], pick[:], AX.X, ALU.max))
                    link(nc.vector.tensor_tensor(hot[:, k, :, :], pick[:], over_experts(first[:]), ALU.is_equal))
                    if k + 1 < TOP:
                        link(nc.vector.scalar_tensor_tensor(gates[:], hot[:, k, :, :], -2.0, gates[:], ALU.mult,
                                                            ALU.add))
                nc.vector.tensor_tensor(mask[:], hot[:, 0, :, :], hot[:, 1, :, :], ALU.add).then_inc(mask_ready, 1)
                link(nc.vector.tensor_tensor(first[:], top[:, 0, :], top[:, 1, :], ALU.add))
                link(nc.vector.reciprocal(first[:], first[:]))
                for k in range(TOP):
                    link(nc.vector.tensor_tensor(mix[:, :, k], top[:, k, :], first[:], ALU.mult))
                dve.wait_ge(counts_ps, 1)
                within, of_tile = A[0], B[0]
                link(nc.vector.tensor_copy(total[:, 0, :, :], of_tile[:, 0:TILES * E].rearrange("p (t e) -> p t e", e=E)))
                at, d = 0, 1
                while d < TILES:
                    link(nc.vector.tensor_copy(total[:, 1 - at, 0:d, :], total[:, at, 0:d, :]))
                    link(nc.vector.tensor_tensor(total[:, 1 - at, d:TILES, :], total[:, at, d:TILES, :],
                                                 total[:, at, 0:TILES - d, :], ALU.add))
                    at, d = 1 - at, 2 * d
                link(nc.vector.tensor_scalar(n_tiles[:], total[:, at, TILES - 1, :], float(P - 1), None, ALU.add))
                link(nc.vector.tensor_copy(n_int[:], n_tiles[:]))
                link(nc.vector.tensor_scalar(n_int[:], n_int[:], P.bit_length() - 1, None, ALU.arith_shift_right))
                link(nc.vector.tensor_copy(n_tiles[:], n_int[:]))
                link(nc.vector.tensor_copy(ends[:, 0, :], n_tiles[:]))
                be, d = 0, 1
                while d < E:
                    link(nc.vector.tensor_copy(ends[:, 1 - be, 0:d], ends[:, be, 0:d]))
                    link(nc.vector.tensor_tensor(ends[:, 1 - be, d:E], ends[:, be, d:E], ends[:, be, 0:E - d], ALU.add))
                    be, d = 1 - be, 2 * d
                link(nc.vector.tensor_tensor(n_tiles[:], ends[:, be, :], n_tiles[:], ALU.subtract))
                link(nc.vector.tensor_scalar(n_tiles[:], n_tiles[:], float(P), float(TILES * P), ALU.mult, ALU.add))
                link(nc.vector.tensor_tensor(slot[:], total[:, at, :, :],
                                             of_tile[:, 0:TILES * E].rearrange("p (t e) -> p t e", e=E), ALU.subtract))
                link(nc.vector.tensor_tensor(slot[:], slot[:],
                                             within[:, 0:TILES * E].rearrange("p (t e) -> p t e", e=E), ALU.add))
                link(nc.vector.tensor_tensor(slot[:], slot[:], n_tiles[:].unsqueeze(1).broadcast_to([P, TILES, E]),
                                             ALU.add))
                for k in range(TOP):
                    link(nc.vector.tensor_tensor(picked[:], slot[:], hot[:, k, :, :], ALU.mult))
                    link(nc.vector.tensor_reduce(slot_f[:, k, :], picked[:], AX.X, ALU.add))
                    link(nc.vector.tensor_copy(slots[:, :, k], slot_f[:, k, :]))
                link(nc.vector.tensor_tensor(tile_ge[:], tile_no[:].unsqueeze(2).broadcast_to([1, SLOT_TILES, E - 1]),
                                             ends[0:1, be, 0:E - 1].unsqueeze(1)
                                             .broadcast_to([1, SLOT_TILES, E - 1]), ALU.is_ge))
                link(nc.vector.tensor_reduce(tile_e_f[:], tile_ge[:], AX.X, ALU.add))
                link(nc.vector.memset(tile_expert[:, 0:TILES], E))
                nc.vector.tensor_copy(tile_expert[:, TILES:ALL_TILES], tile_e_f[:]).then_inc(routed, 1)

                def gate_by_up(t, p):
                    wait(dve, gate_ready, t + 1)
                    wait(dve, b_ps, t + 1)
                    wait(dve, h_ps, t - 1)
                    nc.vector.tensor_tensor(hid[:, p, :], gate[:, p, :], B[p][:], ALU.mult).then_inc(hid_ready, 1)

                def copy_y(t, p):
                    wait(dve, y_ps, t + 1)
                    wait(dve, y_stored[p], 8 * (t - p))
                    nc.vector.tensor_copy(y_t[:, p, :], Y[p][:, 0:D]).then_inc(y_ready, 1)

                gate_by_up(0, 0)
                gate_by_up(1, 1)
                with dve.Fori(1, PAIRS) as h:
                    for p in range(2):
                        copy_y(2 * h + p - 2, p)
                        gate_by_up(2 * h + p, p)
                copy_y(ALL_TILES - 2, 0)
                copy_y(ALL_TILES - 1, 1)

            @block.tensor
            def _(pe):
                pe.wait_ge(route_consts, 7)
                pe.wait_ge(mask_ready, 1)
                nc.tensor.matmul(A[0][:, 0:TILES * E], below[:], mask[:].rearrange("p t e -> p (t e)"),
                                 start=True, stop=True)
                nc.tensor.matmul(B[0][:, 0:TILES * E], ones[:], mask[:].rearrange("p t e -> p (t e)"),
                                 start=True, stop=True).then_inc(counts_ps, 1)

                def transpose_x(t, p):
                    wait(pe, x_loaded[p], 8 * (t - p) + 16)
                    wait(pe, x_T_ready, t)
                    for k in range(KD):
                        last = nc.tensor.transpose(X[:, k * P:(k + 1) * P], x_t[:, p, k * P:(k + 1) * P], ident[:])
                    last.then_inc(x_ps, 1)

                def up(t, p, e, out, col, done):
                    for k in range(KD):
                        last = nc.tensor.matmul(out[p][:], x_T[:, p, k, :], w_up[:, e, k, col:col + FF],
                                                start=k == 0, stop=k == KD - 1)
                    last.then_inc(done, 1)

                def transpose_hid(t, p):
                    wait(pe, hid_ready, t + 1)
                    wait(pe, hid_T_ready, t)
                    for k in range(KF):
                        last = nc.tensor.transpose(H[:, k * P:(k + 1) * P], hid[:, p, k * P:(k + 1) * P], ident[:])
                    last.then_inc(h_ps, 1)

                def down(t, p, e):
                    wait(pe, hid_T_ready, t + 1)
                    wait(pe, y_ready, t - 1)
                    for k in range(KF):
                        last = nc.tensor.matmul(Y[p][:, 0:D], hid_T[:, p, k, :], w_down[:, e, k, :],
                                                start=k == 0, stop=k == KF - 1)
                    last.then_inc(y_ps, 1)

                def step(t, p, e, e_before, start=False, end=False):
                    wait(pe, x_T_ready, t + 1)
                    wait(pe, hid_ready, t - 1)
                    up(t, p, e, A, 0, a_ps)
                    if not start:
                        transpose_hid(t - 1, 1 - p)
                    up(t, p, e, B, FF, b_ps)
                    if not end:
                        transpose_x(t + 1, 1 - p)
                    if not start:
                        down(t - 1, 1 - p, e_before)

                def expert_of(t):
                    return pe.value_load(tile_expert[0:1, bass.ds(t, 1)], min_val=0, max_val=E)

                pe.wait_ge(shared_loaded, 3 * 16)
                pe.wait_ge(routed, 1)
                transpose_x(0, 0)
                step(0, 0, E, E, start=True)
                step(1, 1, E, E)
                with pe.Fori(1, TILES // 2) as h:
                    step(2 * h, 0, E, E)
                    step(2 * h + 1, 1, E, E)
                pe.wait_ge(w_loaded, 3 * 16 * E)
                with pe.Fori(TILES // 2, PAIRS - 1) as h:
                    e_before, e0, e1 = expert_of(2 * h - 1), expert_of(2 * h), expert_of(2 * h + 1)
                    step(2 * h, 0, e0, e_before)
                    step(2 * h + 1, 1, e1, e0)
                e_before, e0, e1 = [expert_of(ALL_TILES - k) for k in (3, 2, 1)]
                step(ALL_TILES - 2, 0, e0, e_before)
                step(ALL_TILES - 1, 1, e1, e0, end=True)
                transpose_hid(ALL_TILES - 1, 1)
                down(ALL_TILES - 1, 1, e1)

        with ExitStack() as c3:
            def sb3(name, shape, dt=F32):
                return c3.enter_context(nc.sbuf_tensor(tag + name, shape, dt))

            def sem3(name):
                return c3.enter_context(nc.semaphore(tag + name))

            idx = sb3("idx3", [P, 2, TOP], U32)
            share = sb3("share", [P, 2, TOP])
            x_t = sb3("x_t3", [P, 2, D])
            y_s = sb3("y_s", [P, 2, D])
            y_r = sb3("y_r", [P, 2, TOP, D])
            acc = sb3("acc", [P, 2, D])
            acc2 = sb3("acc2", [P, 2, D])
            out_t = sb3("out_t", [P, 2, D])
            idx_ready = sem3("idx_ready3")
            loaded = [sem3(f"loaded3{p}") for p in range(2)]
            gathered = [sem3(f"gathered{p}") for p in range(2)]
            part_done = sem3("part_done")
            out_ready = sem3("out_ready")
            stored = [sem3(f"stored3{p}") for p in range(2)]
            block = c3.enter_context(nc.Block())

            @block.sync
            def _(sp):
                def step(h, p):
                    wait(sp, out_ready, 2 * h)
                    sp.dma_start(x_t[:, p, :], x_in[bass.ts(2 * h + p, P), :]).then_inc(loaded[p], 16)
                    sp.dma_start(y_s[:, p, :], y_d[bass.ts(2 * h + p, P), :]).then_inc(loaded[p], 16)

                pairs(sp, step)

            @block.scalar
            def _(act):
                def step(h, p):
                    wait(act, out_ready, 2 * h + p + 1)
                    act.dma_start(x_out[bass.ts(2 * h + p, P), :], out_t[:, p, :]).then_inc(stored[p], 16)

                pairs(act, step)
                for p in range(2):
                    act.wait_ge(stored[p], 16 * (TILES // 2))

            @block.gpsimd
            def _(pool):
                def step(h, p):
                    wait(pool, out_ready, 2 * h)
                    wait(pool, gathered[p], 2 * 16 * h)
                    nc.gpsimd.tensor_copy(idx[:, p, :], slots[:, 2 * h + p, :]).then_inc(idx_ready, 1)
                    nc.gpsimd.tensor_copy(share[:, p, :], mix[:, 2 * h + p, :]).then_inc(idx_ready, 1)
                    wait_apart(pool, idx_ready, 4 * h + 2 * p + 2)
                    for k in range(TOP):
                        pool.indirect_dma_start(out=y_r[:, p, k, :], out_offset=None, in_=y_d[:, :],
                                                in_offset=bass.IndirectOffsetOnAxis(ap=idx[:, p, k:k + 1], axis=0))\
                            .then_inc(gathered[p], 16)

                pairs(pool, step)

            @block.vector
            def _(dve):
                def step(h, p):
                    j = 2 * h + p
                    wait(dve, loaded[p], 32 * h + 32)
                    wait(dve, gathered[p], 32 * h + 32)
                    wait(dve, idx_ready, 2 * j + 2)
                    nc.vector.scalar_tensor_tensor(acc[:, p, :], y_r[:, p, 0, :], share[:, p, 0:1], y_s[:, p, :],
                                                   ALU.mult, ALU.add).then_inc(part_done, 1)
                    wait(dve, part_done, 2 * j + 1)
                    nc.vector.scalar_tensor_tensor(acc2[:, p, :], y_r[:, p, 1, :], share[:, p, 1:2], acc[:, p, :],
                                                   ALU.mult, ALU.add).then_inc(part_done, 1)
                    wait(dve, part_done, 2 * j + 2)
                    wait(dve, stored[p], 16 * h)
                    nc.vector.scalar_tensor_tensor(out_t[:, p, :], acc2[:, p, :], 1.0 / (1 + TOP), x_t[:, p, :],
                                                   ALU.mult, ALU.add).then_inc(out_ready, 1)

                pairs(dve, step)


def build_network(nc, x, a_w, b_w, f_w, out):
    def dram(name, shape):
        return nc.dram_tensor(name, shape, F32).ap()

    x1, x2, x3 = [dram(name, (T, D)) for name in ("after_a", "after_f1", "after_b")]
    v_d = dram("a_values", (T + 2 * P, D))
    rs_d = dram("a_row_sums", (TILES * 4, SEQ))
    rows_d = dram("ffn_rows", (ALL_TILES * P, D))
    y_d = dram("ffn_outputs", (ALL_TILES * P, D))
    ext_d = dram("bias_rows", (HEADS, P * EXT))
    Wq, bq, Wk, bk, Wv, bv, Wo, bo = a_w
    W_qkv, b_qkv, W_out, b_out, rel_bias = b_w
    with ExitStack() as ctx:
        ext_sb = ctx.enter_context(nc.sbuf_tensor("ext_sb", [HEADS, EXT], F32))
        ext_stored = ctx.enter_context(nc.semaphore("ext_stored"))
        build_bias_rows(nc, rel_bias, ext_sb, ext_d, ext_stored)
        build_attention_a(nc, x, Wq, bq, Wk, bk, Wv, bv, Wo, bo, x1, v_d, rs_d)
        build_ffn(nc, "f1_", x1, *f_w, x2, rows_d, y_d, True)
        build_attention_b(nc, x2, W_qkv, b_qkv, W_out, b_out, x3, ext_d, ext_stored)
        build_ffn(nc, "f2_", x3, *f_w, out, rows_d, y_d, False)


A_NAMES = ["L0_attn_a_" + n for n in ("Wq", "bq", "Wk", "bk", "Wv", "bv", "Wo", "bo")]
B_NAMES = ["L0_attn_b_" + n for n in ("W_qkv", "b_qkv", "W_out", "b_out", "rel_bias")]
F_NAMES = ["L0_ffn_" + n for n in ("Wg", "Ws1", "Ws3", "Ws2", "We1", "We3", "We2")]


def kernel(**inputs):
    import numpy as np
    import concourse.bacc as bacc
    from concourse.bass_utils import run_bass_kernel_spmd

    nc = bacc.Bacc("TRN2", target_bir_lowering=False, num_devices=1)
    x = np.ascontiguousarray(inputs["L0_attn_a_X_embed"])
    arrays = {"in_x": x.reshape(T, D)}
    for name in A_NAMES + B_NAMES + F_NAMES:
        arrays["in_" + name] = np.ascontiguousarray(inputs[name])
    aps = {name: nc.dram_tensor(name, a.shape, mybir.dt.from_np(a.dtype), kind="ExternalInput").ap()
           for name, a in arrays.items()}
    out = nc.dram_tensor("out_x", (T, D), F32, kind="ExternalOutput").ap()
    build_network(nc, aps["in_x"], [aps["in_" + n] for n in A_NAMES], [aps["in_" + n] for n in B_NAMES],
                  [aps["in_" + n] for n in F_NAMES], out)
    r = run_bass_kernel_spmd(nc, [arrays], core_ids=[0])
    return r.results[0]["out_x"].reshape(x.shape)
```

```python
import concourse.bass as bass
from concourse import mybir
from contextlib import ExitStack

F32 = mybir.dt.float32
F32R = mybir.dt.float32r
ALU = mybir.AluOpType
ACT = mybir.ActivationFunctionType
AX = mybir.AxisListType

P = 128
D = 256
KD = D // P
HEADS = 16
DH = D // HEADS
T = 4096
TILES = T // P
EPS = 1e-5


def wait(eng, sem, value):
    if not isinstance(value, int) or value > 0:
        eng.wait_ge(sem, value)


def wait_apart(eng, sem, value):
    wait(eng, sem, value)
    if not isinstance(value, int):
        eng.nop(nofuse=True)


def build_attention_a(nc, x_in, Wq, bq, Wk, bk, Wv, bv, Wo, bo, x_out, v_d, rs_d, slot_rows, ext_sb, ext_d):
    HT = 4
    R = P // HT
    L = R * HEADS
    G = 4
    EXT_COPIES = P // TILES
    SCALE = 1.0 / D
    with ExitStack() as ctx:
        def sb(name, shape, dt=F32):
            return ctx.enter_context(nc.sbuf_tensor("aa_" + name, shape, dt))

        def pb(name):
            return ctx.enter_context(nc.psum_tensor("aa_" + name, [P, 512], F32))

        sems = []

        def sem(name):
            sems.append(nc.alloc_semaphore("aa_" + name))
            return sems[-1]

        ident = sb("ident", [P, P])
        ident_r = sb("ident_r", [P, P], F32R)
        w_qkv = sb("w_qkv", [P, KD, 3 * D])
        w_o = sb("w_o", [P, KD, D])
        b_qkv = sb("b_qkv", [P, 3 * D])
        b_o = sb("b_o", [P, D])
        minus_half = sb("minus_half", [P, 1])
        x_t = sb("x_t", [P, 2, D])
        stats = sb("stats", [P, 6])
        mean_var = sb("mean_var", [P, 2, 2])
        rstd = sb("rstd", [P, 2])
        xn = sb("xn", [P, 2, D])
        xn_T = sb("xn_T", [P, 2, KD, P])
        qk = sb("qk", [P, 2, 2 * D])
        v_t = sb("v_t", [P, 2, D])
        parts = sb("parts", [P, 2, HEADS, 8, DH])
        qk_T = sb("qk_T", [P, 2, HT, HEADS, R], F32R)
        k_T = sb("k_T", [64, 2, HT, HEADS * R], F32R)
        neg_max = sb("neg_max", [P, 8])
        e_t = sb("e_t", [P, 2, HT, L])
        den = sb("den", [P, 2, HT])
        inv = sb("inv", [P, 2, HT])
        rs_sb = sb("rs_sb", [P, L])
        rs_t = sb("rs_t", [P, 2, HEADS])
        v_p = sb("v_p", [P, 2, D])
        x_p = sb("x_p", [P, 2, D])
        xb = sb("xb", [P, 2, D])
        o_t = sb("o_t", [P, 2, D])
        o_T = sb("o_T", [P, KD, P])
        y_t = sb("y_t", [P, 2, D])
        S = [pb(f"s{i}") for i in range(4)]
        M = [pb(f"m{i}") for i in range(3)]
        RS = pb("rs")

        blank = sb("blank", [P, D + 2])
        blank_no = sb("blank_no", [P, 1], mybir.dt.int32)
        blank_zeroed = sem("blank_zeroed")
        blank_ready = sem("blank_ready")
        blanks_filled = sem("blanks_filled")
        ext_stored = sem("ext_stored")
        w_loaded = sem("w_loaded")
        wq_scaled = sem("wq_scaled")
        ident_zeroed = sem("ident_zeroed")
        ident_ready = sem("ident_ready")
        x_loaded = [sem(f"x_loaded{p}") for p in range(2)]
        stats_done = sem("stats_done")
        mv_done = sem("mv_done")
        pool_step = sem("pool_step")
        xn_ready = sem("xn_ready")
        xt_ps = sem("xt_ps")
        xn_T_ready = sem("xn_T_ready")
        qk_ps = sem("qk_ps")
        v_ps = sem("v_ps")
        qk_ready = sem("qk_ready")
        v_ready = sem("v_ready")
        v_stored = [sem(f"v_stored{p}") for p in range(2)]
        hi_ready = sem("hi_ready")
        parts_ready = sem("parts_ready")
        t_ps = sem("t_ps")
        t_by_act = sem("t_by_act")
        t_by_dve = sem("t_by_dve")
        k_T_moved = [sem(f"k_T_moved{p}") for p in range(2)]
        s_done = sem("s_done")
        max_done = sem("max_done")
        exp_done = sem("exp_done")
        inv_done = sem("inv_done")
        rs_done = sem("rs_done")
        rs_copied = sem("rs_copied")
        rs_stored = sem("rs_stored")
        post_loaded = [sem(f"post_loaded{p}") for p in range(2)]
        xb_ready = sem("xb_ready")
        out_ready = sem("out_ready")
        ot_ps = sem("ot_ps")
        o_T_ready = sem("o_T_ready")
        wo_ps = sem("wo_ps")
        y_ready = sem("y_ready")
        y_stored = [sem(f"y_stored{p}") for p in range(2)]

        block = ctx.enter_context(nc.Block())


        def run(eng, step):
            step(0, 0, 0)
            step(1, 1, 0)
            with eng.Fori(1, TILES // 2) as h:
                step(2 * h, 0, h)
                step(2 * h + 1, 1, h)

        def has(i, back):
            return not isinstance(i, int) or i >= back

        PE_R = {0: -2, 4: -1, 8: 0, 12: 1}
        PE_OT, PE_WO, PE_XT, PE_QK, PE_V = 1, 3, 5, (11, 13), 14
        PE_T = {6: 0, 7: 1, 9: 2, 10: 3}
        ACT_OT, ACT_RS, ACT_XT = 0, 3, 4
        ACT_T = {5: 0, 8: 2}
        DVE_INV = {3: -1, 7: 0, 11: 1, 15: 2}
        DVE_Y, DVE_STATS, DVE_QK, DVE_V = 4, 9, 14, 15
        DVE_T = {8: 1, 11: 3}

        @block.sync
        def _(sp):
            def load_x(j, p, h):
                tile = j % TILES if isinstance(j, int) else sp.snap(j % TILES, min_val=0, max_val=TILES - 1)
                wait(sp, xn_ready, j - 1)
                sp.dma_start(x_t[:, p, :], x_in[bass.ts(tile, P), :]).then_inc(x_loaded[p], 16)

            def store_v(j, p, h):
                wait(sp, v_ready, j + 1)
                sp.dma_start(v_d[bass.ts(j, P), :], v_t[:, p, :]).then_inc(v_stored[p], 16)

            def move_k(j, p, h):
                wait(sp, t_by_act, 2 * j + 2)
                wait(sp, t_by_dve, 2 * j + 2)
                wait(sp, s_done, 16 * (j - 1))
                sp.dma_start(k_T[:, p, :, :].bitcast(F32), qk_T[64:P, p, :, :, :].rearrange("p e c r -> p e (c r)").bitcast(F32)).then_inc(k_T_moved[p], 16)

            def post_loads(j, p, h):
                wait(sp, rs_copied, j + 1)
                sp.dma_start(rs_d[bass.ts(j, HT), :], rs_sb[0:P - R + 1:R, :])\
                    .then_inc(rs_stored, 16)
                wait(sp, out_ready, j - 1)
                wait_apart(sp, xb_ready, j - 1)
                wait(sp, v_stored[p], 16 * (h + 1))
                sp.dma_start(v_p[:, p, :], v_d[bass.ts(j, P), :]).then_inc(post_loaded[p], 16)
                sp.dma_start(x_p[:, p, :], x_in[bass.ts(j, P), :]).then_inc(post_loaded[p], 16)
                wait(sp, rs_stored, 16 * (j + 1))
                sp.dma_start(rs_t[:, p, :], rs_d.rearrange("e (r c) -> (e r) c", c=HEADS)[bass.ts(j, P), :])\
                    .then_inc(post_loaded[p], 16)

            def store_y(j, p, h):
                wait(sp, y_ready, j + 1)
                sp.dma_start(x_out[bass.ts(j, P), :], y_t[:, p, :]).then_inc(y_stored[p], 16)

            for w, part in ((Wq, 0), (Wk, 1), (Wv, 2)):
                sp.dma_start(w_qkv[:, :, part * D:(part + 1) * D], w.rearrange("(k p) n -> p k n", p=P))\
                    .then_inc(w_loaded, 16)
            for b, part in ((bq, 0), (bk, 1), (bv, 2)):
                sp.dma_start(b_qkv[:, part * D:(part + 1) * D], b.partition_broadcast(P)).then_inc(w_loaded, 16)
            sp.dma_start(w_o[:], Wo.rearrange("(k p) n -> p k n", p=P)).then_inc(w_loaded, 16)
            sp.dma_start(b_o[:], bo.partition_broadcast(P)).then_inc(w_loaded, 16)
            load_x(0, 0, 0)
            load_x(1, 1, 0)
            load_x(2, 0, 1)
            sp.wait_ge(blank_ready, 1)
            fill_tiles = slot_rows[0].shape[0] // P
            for rows_d in slot_rows:
                sp.dma_start(rows_d[2 * TILES * P:fill_tiles * P, :].rearrange("(a p) n -> p a n", p=P),
                             blank[:].unsqueeze(1).broadcast_to([P, fill_tiles - 2 * TILES, D + 2]))\
                    .then_inc(blanks_filled, 16)
            store_v(0, 0, 0)
            store_v(1, 1, 0)
            move_k(0, 0, 0)

            def step(i, p, h):
                load_x(i + 3, 1 - p, h + 1 + p)
                if has(i, 1):
                    post_loads(i - 1, 1 - p, h - 1 + p)
                if has(i, 2):
                    store_y(i - 2, p, h - 1)
                move_k(i + 1, 1 - p, h + p)
                store_v(i + 2, p, h + 1)
                for rows_d in slot_rows:
                    sp.dma_start(rows_d[bass.ts(i, 2 * P), :].rearrange("(a p) n -> p a n", p=P),
                                 blank[:].unsqueeze(1).broadcast_to([P, 2, D + 2])).then_inc(blanks_filled, 16)
                sp.dma_start(ext_d.rearrange("h (p w) -> h p w", p=P)[:, bass.ts(i, EXT_COPIES), :],
                             ext_sb[:].unsqueeze(1).broadcast_to([HEADS, EXT_COPIES, ext_sb.shape[1]]))\
                    .then_inc(ext_stored, 16)

            run(sp, step)
            post_loads(TILES - 1, 1, TILES // 2 - 1)
            store_y(TILES - 2, 0, TILES // 2 - 1)
            store_y(TILES - 1, 1, TILES // 2 - 1)
            sp.wait_ge(blanks_filled, 16 * len(slot_rows) * (TILES + 1))
            sp.wait_ge(ext_stored, 16 * TILES)
            for p in range(2):
                sp.wait_ge(y_stored[p], 16 * (TILES // 2))
                sp.wait_ge(v_stored[p], 16 * (TILES // 2 + 1))

        @block.gpsimd
        def _(pool):
            nc.gpsimd.memset(blank[:], 0.0).then_inc(blank_zeroed, 1)
            nc.gpsimd.iota(blank_no[:], pattern=[[0, 1]], base=T, channel_multiplier=1).then_inc(blank_zeroed, 1)
            pool.wait_ge(blank_zeroed, 2)
            nc.gpsimd.tensor_copy(blank[:, D:D + 1], blank_no[:]).then_inc(blank_ready, 1)
            nc.gpsimd.memset(ident[:], 0.0).then_inc(ident_zeroed, 1)
            pool.wait_ge(ident_zeroed, 1)
            nc.gpsimd.affine_select(out=ident[:], in_=ident[:], compare_op=ALU.not_equal, fill=1.0, base=0,
                                    pattern=[[-1, P]], channel_multiplier=1).then_inc(ident_ready, 1)
            pool.wait_ge(ident_ready, 1)
            nc.gpsimd.tensor_copy(ident_r[:], ident[:]).then_inc(ident_ready, 1)
            nc.gpsimd.memset(minus_half[:], -0.5).then_inc(ident_zeroed, 1)
            pool.wait_ge(ident_zeroed, 2)

            def normalise(j, p, h):
                wait_apart(pool, mv_done, j + 1)
                nc.gpsimd.tensor_scalar(rstd[:, p:p + 1], mean_var[:, p, 1:2], EPS, None, ALU.add)\
                    .then_inc(pool_step, 1)
                wait(pool, pool_step, 2 * j + 1)
                nc.gpsimd.tensor_tensor(rstd[:, p:p + 1], rstd[:, p:p + 1], minus_half[:], ALU.pow)\
                    .then_inc(pool_step, 1)
                wait(pool, pool_step, 2 * j + 2)
                wait_apart(pool, xt_ps, j - 1)
                nc.gpsimd.tensor_scalar(xn[:, p, :], x_t[:, p, :], mean_var[:, p, 0:1], rstd[:, p:p + 1],
                                        ALU.subtract, ALU.mult).then_inc(xn_ready, 1)

            def split(j, p, h):
                wait(pool, qk_ready, j + 1)
                wait_apart(pool, t_ps, 4 * (j - 1))
                for m, hi, lo in ((0, slice(0, 2), slice(2, 4)), (1, slice(4, 8, 2), slice(5, 8, 2))):
                    src = qk[:, p, m * D:(m + 1) * D].rearrange("p (c x) -> p c x", x=DH).unsqueeze(1)\
                        .broadcast_to([P, 2, HEADS, DH])
                    nc.gpsimd.tensor_scalar(parts[:, p, :, hi, :].rearrange("p c a x -> p a c x").bitcast(F32R), src, 1.0, None, ALU.mult)\
                        .then_inc(hi_ready, 1)
                for m, hi, lo in ((0, slice(0, 2), slice(2, 4)), (1, slice(4, 8, 2), slice(5, 8, 2))):
                    src = qk[:, p, m * D:(m + 1) * D].rearrange("p (c x) -> p c x", x=DH).unsqueeze(1)\
                        .broadcast_to([P, 2, HEADS, DH])
                    wait(pool, hi_ready, 2 * j + 1 + m)
                    nc.gpsimd.tensor_tensor(parts[:, p, :, lo, :].rearrange("p c a x -> p a c x").bitcast(F32R), src, parts[:, p, :, hi, :].rearrange("p c a x -> p a c x"),
                                            ALU.subtract).then_inc(parts_ready, 1)

            def weigh(j, p, h):
                wait(pool, post_loaded[p], 48 * (h + 1))
                wait(pool, y_ready, j - 1)
                nc.gpsimd.tensor_tensor(xb[:, p, :], x_p[:, p, :], b_o[:], ALU.add).then_inc(xb_ready, 1)
                wait(pool, ot_ps, j - 1)
                nc.gpsimd.tensor_tensor(o_t[:, p, :].rearrange("p (c x) -> p c x", x=DH),
                                        v_p[:, p, :].rearrange("p (c x) -> p c x", x=DH),
                                        rs_t[:, p, :].unsqueeze(2).broadcast_to([P, HEADS, DH]),
                                        ALU.mult).then_inc(out_ready, 1)

            pool.wait_ge(w_loaded, 8 * 16)
            normalise(0, 0, 0)
            normalise(1, 1, 0)
            split(0, 0, 0)
            normalise(2, 0, 1)
            split(1, 1, 0)

            def step(i, p, h):
                if has(i, 1):
                    weigh(i - 1, 1 - p, h - 1 + p)
                normalise(i + 3, 1 - p, h + 1 + p)
                split(i + 2, p, h + 1)

            run(pool, step)
            weigh(TILES - 1, 1, TILES // 2 - 1)

        def t_out(p, n):
            return qk_T[:, p, :, 4 * n:4 * n + 4, :].rearrange("p e c r -> p c e r")

        T_BANK = [0, 2, 0, 1]
        XT_BANK, QK_BANK, V_BANK, OT_BANK, WO_BANK = 1, 2, 0, 1, 1

        @block.scalar
        def _(act):
            def copy_xn_T(j, p, h):
                wait(act, xt_ps, j + 1)
                wait(act, v_ps, j - 1)
                nc.scalar.activation(xn_T[:, p, :, :], M[XT_BANK][:, 0:D].rearrange("p (k t) -> p k t", k=KD),
                                     ACT.Copy).then_inc(xn_T_ready, 1)

            def copy_t(j, p, n):
                wait(act, t_ps, 4 * j + n + 1)
                wait(act, s_done, 16 * (j - 1))
                wait(act, k_T_moved[p], 16 * ((j - p) // 2) if isinstance(j, int) else k_moves(j, p))
                nc.scalar.activation(t_out(p, n), M[T_BANK[n]][:].rearrange("p (c e r) -> p c e r", c=4, e=HT), ACT.Copy)\
                    .then_inc(t_by_act, 1)

            def exp(i, p, g, e):
                n = 16 * i + 4 * g + e
                wait(act, max_done, n + 1)
                if e == 0:
                    wait(act, rs_done, 4 * i + g - 1)
                nc.scalar.activation(e_t[:, g % 2, e, :], S[e][:], ACT.Exp, bias=neg_max[:, 4 * (g % 2) + e:4 * (g % 2) + e + 1],
                                     scale=-1.0, accum_out=den[:, g % 2, e:e + 1]).then_inc(exp_done, 1)

            def copy_rs(j):
                wait(act, rs_done, 4 * (j + 1))
                wait(act, rs_stored, 16 * j)
                nc.scalar.activation(rs_sb[:].rearrange("p (r c) -> p r c", c=HEADS),
                                     RS[:].rearrange("p (c r) -> p r c", c=HEADS), ACT.Copy).then_inc(rs_copied, 1)

            def copy_o_T(j):
                wait(act, ot_ps, j + 1)
                wait(act, wo_ps, j)
                nc.scalar.activation(o_T[:], M[OT_BANK][:, 0:D].rearrange("p (k t) -> p k t", k=KD), ACT.Copy)\
                    .then_inc(o_T_ready, 1)

            def k_moves(j, p):
                return 8 * (j - p)

            copy_xn_T(0, 0, 0)
            copy_xn_T(1, 1, 0)
            copy_t(0, 0, 0)
            copy_t(0, 0, 2)

            def step(i, p, h):
                for s in range(16):
                    exp(i, p, s // 4, s % 4)
                    if s == ACT_OT and has(i, 2):
                        copy_o_T(i - 2)
                    if s == ACT_RS and has(i, 1):
                        copy_rs(i - 1)
                    if s == ACT_XT:
                        copy_xn_T(i + 2, p, h + 1)
                    if s in ACT_T:
                        copy_t(i + 1, 1 - p, ACT_T[s])

            run(act, step)
            copy_o_T(TILES - 2)
            copy_rs(TILES - 1)
            copy_o_T(TILES - 1)

        @block.vector
        def _(dve):
            def statistics(j, p):
                wait(dve, x_loaded[p], 16 * (j // 2 + 1) if isinstance(j, int) else 8 * (j - p) + 16)
                wait(dve, mv_done, j)
                nc.vector.bn_stats(stats[:], x_t[:, p, :]).then_inc(stats_done, 1)
                wait(dve, stats_done, j + 1)
                wait_apart(dve, xn_ready, j - 1)
                nc.vector.bn_aggr(mean_var[:, p, :], stats[:]).then_inc(mv_done, 1)

            def add_qk(j, p):
                wait(dve, qk_ps, j + 1)
                wait(dve, parts_ready, 2 * (j - 1))
                nc.vector.tensor_tensor(qk[:, p, :], M[QK_BANK][:], b_qkv[:, 0:2 * D], ALU.add).then_inc(qk_ready, 1)

            def add_v(j, p):
                wait(dve, v_ps, j + 1)
                wait(dve, v_stored[p], 16 * (j // 2) if isinstance(j, int) else 8 * (j - p))
                nc.vector.tensor_tensor(v_t[:, p, :], M[V_BANK][:, 0:D], b_qkv[:, 2 * D:3 * D], ALU.add)\
                    .then_inc(v_ready, 1)

            def copy_t(j, p, n):
                wait(dve, t_ps, 4 * j + n + 1)
                wait(dve, s_done, 16 * (j - 1))
                wait(dve, k_T_moved[p], 16 * (j // 2) if isinstance(j, int) else 8 * (j - p))
                nc.vector.tensor_copy(t_out(p, n), M[T_BANK[n]][:].rearrange("p (c e r) -> p c e r", c=4, e=HT))\
                    .then_inc(t_by_dve, 1)

            def maximum(i, g, e):
                wait(dve, s_done, 16 * i + 4 * g + e + 1)
                nc.vector.tensor_reduce(neg_max[:, 4 * (g % 2) + e:4 * (g % 2) + e + 1], S[e][:], AX.X, ALU.min)\
                    .then_inc(max_done, 1)

            def invert(group, gp):
                wait(dve, exp_done, 4 * (group + 1))
                nc.vector.reciprocal(inv[:, gp, :], den[:, gp, :]).then_inc(inv_done, 1)

            def add_residual(j, p):
                wait(dve, wo_ps, j + 1)
                wait(dve, xb_ready, j + 1)
                wait(dve, y_stored[p], 16 * (j // 2) if isinstance(j, int) else 8 * (j - p))
                nc.vector.tensor_tensor(y_t[:, p, :], M[WO_BANK][:, 0:D], xb[:, p, :], ALU.add).then_inc(y_ready, 1)

            dve.wait_ge(w_loaded, 8 * 16)
            nc.vector.tensor_scalar(w_qkv[:, :, 0:D], w_qkv[:, :, 0:D], -SCALE, None, ALU.mult).then_inc(wq_scaled, 1)
            nc.vector.tensor_scalar(b_qkv[:, 0:D], b_qkv[:, 0:D], -SCALE, None, ALU.mult).then_inc(wq_scaled, 1)
            dve.wait_ge(wq_scaled, 2)
            statistics(0, 0)
            statistics(1, 1)
            add_qk(0, 0)
            add_v(0, 0)
            statistics(2, 0)
            add_qk(1, 1)
            add_v(1, 1)
            copy_t(0, 0, 1)
            copy_t(0, 0, 3)

            def step(i, p, h):
                for s in range(16):
                    maximum(i, s // 4, s % 4)
                    if s in DVE_INV and has(4 * i, -DVE_INV[s]):
                        invert(4 * i + DVE_INV[s], DVE_INV[s] % 2)
                    if s == DVE_Y and has(i, 2):
                        add_residual(i - 2, p)
                    if s in DVE_T:
                        copy_t(i + 1, 1 - p, DVE_T[s])
                    if s == DVE_STATS:
                        statistics(i + 3, 1 - p)
                    if s == DVE_QK:
                        add_qk(i + 2, p)
                    if s == DVE_V:
                        add_v(i + 2, p)

            run(dve, step)
            invert(4 * TILES - 1, 1)
            add_residual(TILES - 2, 0)
            add_residual(TILES - 1, 1)

        @block.tensor
        def _(pe):
            def transpose_x(j, p):
                wait(pe, xn_ready, j + 1)
                wait(pe, y_ready, j - 3)
                wait(pe, xn_T_ready, j)
                for k in range(KD):
                    last = nc.tensor.transpose(M[XT_BANK][:, k * P:(k + 1) * P], xn[:, p, k * P:(k + 1) * P], ident[:])
                last.then_inc(xt_ps, 1)

            def project_qk(j, p, k):
                if k == 0:
                    wait(pe, xn_T_ready, j + 1)
                    wait(pe, t_by_dve, 2 * (j - 1) + 1 if not isinstance(j, int) or j >= 2 else 0)
                    wait(pe, qk_ready, j)
                product = nc.tensor.matmul(M[QK_BANK][:], xn_T[:, p, k, :], w_qkv[:, k, 0:2 * D],
                                           start=k == 0, stop=k == KD - 1)
                if k == KD - 1:
                    product.then_inc(qk_ps, 1)

            def project_v(j, p):
                wait(pe, t_by_act, 2 * j if not isinstance(j, int) or j >= 2 else 0)
                wait(pe, v_ready, j)
                for k in range(KD):
                    last = nc.tensor.matmul(M[V_BANK][:, 0:D], xn_T[:, p, k, :], w_qkv[:, k, 2 * D:3 * D],
                                            start=k == 0, stop=k == KD - 1)
                last.then_inc(v_ps, 1)

            def transpose_parts(j, p, n):
                wait(pe, parts_ready, 2 * (j + 1))
                start = isinstance(j, int) and j == 0
                if n == 0:
                    wait(pe, v_ready, j + 1 + start)
                elif n == 1:
                    wait(pe, qk_ready, j + 1 + start)
                elif n == 2:
                    wait(pe, t_by_act, 2 * j + 1)
                else:
                    wait(pe, xn_T_ready, j + 2)
                for c in range(4):
                    last = nc.tensor.transpose(M[T_BANK[n]][:, c * P:(c + 1) * P].bitcast(F32R),
                                               parts[:, p, 4 * n + c, :, :].rearrange("p a x -> p (a x)")
                                               .bitcast(F32R), ident_r[:])
                last.then_inc(t_ps, 1)

            def scores(i, p, g, e):
                n = 16 * i + 4 * g + e
                wait(pe, exp_done, n - 3)
                nc.tensor.matmul(S[e][:], k_T[:, p, e, g * P:(g + 1) * P],
                                 qk_T[0:64, p, e, :, :].rearrange("p c r -> p (c r)"), start=True, stop=True).then_inc(s_done, 1)

            def row_sums(i, group, g):
                wait(pe, inv_done, group + 1)
                if g == 0:
                    wait(pe, rs_copied, i)
                for e in range(4):
                    last = nc.tensor.matmul(RS[e * R:(e + 1) * R, :], inv[:, g % 2, e:e + 1].broadcast_to([P, R]),
                                            e_t[:, g % 2, e, :], start=g == 0, stop=g == 3)
                last.then_inc(rs_done, 1)

            def transpose_o(j, p):
                wait(pe, out_ready, j + 1)
                if isinstance(j, int) and j >= TILES - 2:
                    wait(pe, t_by_dve, 2 * (TILES + 1))
                    wait(pe, y_ready, j)
                for k in range(KD):
                    last = nc.tensor.transpose(M[OT_BANK][:, k * P:(k + 1) * P], o_t[:, p, k * P:(k + 1) * P], ident[:])
                last.then_inc(ot_ps, 1)

            def output(j, p):
                wait(pe, o_T_ready, j + 1)
                for k in range(KD):
                    last = nc.tensor.matmul(M[WO_BANK][:, 0:D], o_T[:, k, :], w_o[:, k, :],
                                            start=k == 0, stop=k == KD - 1)
                last.then_inc(wo_ps, 1)

            pe.wait_ge(ident_ready, 2)
            pe.wait_ge(wq_scaled, 2)
            transpose_x(0, 0)
            transpose_x(1, 1)
            for j in range(2):
                for k in range(KD):
                    project_qk(j, j, k)
                project_v(j, j)
            for n in range(4):
                transpose_parts(0, 0, n)

            def step(i, p, h):
                for s in range(16):
                    if s == 0:
                        wait(pe, k_T_moved[p], 8 * (i - p) + 16)
                    scores(i, p, s // 4, s % 4)
                    if s in PE_R and has(4 * i, -PE_R[s]):
                        g = PE_R[s] % 4
                        row_sums(i, 4 * i + PE_R[s], g)
                    if s == PE_OT and has(i, 2):
                        transpose_o(i - 2, p)
                    if s == PE_WO and has(i, 2):
                        output(i - 2, p)
                    if s == PE_XT:
                        transpose_x(i + 2, p)
                    if s in PE_T:
                        transpose_parts(i + 1, 1 - p, PE_T[s])
                    if s in PE_QK:
                        project_qk(i + 2, p, PE_QK.index(s))
                    if s == PE_V:
                        project_v(i + 2, p)

            run(pe, step)
            transpose_o(TILES - 2, 0)
            output(TILES - 2, 0)
            row_sums(TILES, 4 * TILES - 2, 2)
            row_sums(TILES, 4 * TILES - 1, 3)
            transpose_o(TILES - 1, 1)
            output(TILES - 1, 1)

    nc.clear_and_free_semaphores(sems)
    nc.all_engine_barrier()


MAX_REL = 256
SEQ = 512
BATCHES = T // SEQ
IB = SEQ // P
EXT = SEQ + P - 1 + SEQ - P
TOEP = 2 * SEQ - P


def build_bias_rows(nc, rel_bias, ext_sb):
    NR = 2 * MAX_REL + 1
    LO = EXT // 2 - MAX_REL
    with ExitStack() as ctx:
        def sb(name, shape):
            return ctx.enter_context(nc.sbuf_tensor("rb_" + name, shape, F32))

        def sem(name):
            return ctx.enter_context(nc.semaphore("rb_" + name))

        r_t = sb("r_t", [P, NR // P, HEADS])
        r_last = sb("r_last", [1, HEADS])
        minus_flip = sb("minus_flip", [P, P])
        minus_one = sb("minus_one", [1, 1])
        flipped = ctx.enter_context(nc.psum_tensor("rb_flipped", [P, 512], F32))
        last_ps = ctx.enter_context(nc.psum_tensor("rb_last_ps", [P, 512], F32))
        loaded = sem("loaded")
        zeroed = sem("zeroed")
        flip_ready = sem("flip_ready")
        flip_ps = sem("flip_ps")
        mid_ready = sem("mid_ready")
        ext_ready = sem("ext_ready")
        block = ctx.enter_context(nc.Block())

        @block.sync
        def _(sp):
            sp.dma_start(r_t[:], rel_bias[0:NR - 1, :].rearrange("(a p) h -> p a h", p=P)).then_inc(loaded, 16)
            sp.dma_start(r_last[:], rel_bias[NR - 1:NR, :]).then_inc(loaded, 16)
            sp.wait_ge(ext_ready, 2)

        @block.gpsimd
        def _(pool):
            nc.gpsimd.memset(minus_flip[:], 0.0).then_inc(zeroed, 1)
            nc.gpsimd.memset(minus_one[:], -1.0).then_inc(flip_ready, 1)
            pool.wait_ge(zeroed, 1)
            nc.gpsimd.affine_select(out=minus_flip[:], in_=minus_flip[:], compare_op=ALU.not_equal, fill=-1.0,
                                    base=-(P - 1), pattern=[[1, P]], channel_multiplier=1).then_inc(flip_ready, 1)

        @block.tensor
        def _(pe):
            pe.wait_ge(loaded, 32)
            pe.wait_ge(flip_ready, 2)
            for a in range(NR // P):
                at = (NR // P - 1 - a) * P
                nc.tensor.matmul(flipped[0:HEADS, at:at + P], r_t[:, a, :], minus_flip[:], start=True, stop=True)
            nc.tensor.matmul(last_ps[0:HEADS, 0:1], r_last[:], minus_one[:], start=True, stop=True)\
                .then_inc(flip_ps, 1)

        @block.vector
        def _(dve):
            dve.wait_ge(flip_ps, 1)
            nc.vector.tensor_copy(ext_sb[:, LO + 1:LO + NR], flipped[0:HEADS, 0:NR - 1]).then_inc(mid_ready, 1)
            nc.vector.tensor_copy(ext_sb[:, 0:LO + 1], last_ps[0:HEADS, 0:1].broadcast_to([HEADS, LO + 1]))\
                .then_inc(ext_ready, 1)
            dve.wait_ge(mid_ready, 1)
            nc.vector.tensor_copy(ext_sb[:, LO + NR:EXT],
                                  ext_sb[:, LO + NR - 1:LO + NR].broadcast_to([HEADS, EXT - LO - NR]))\
                .then_inc(ext_ready, 1)


def build_attention_b(nc, x_in, W_qkv, b_qkv_d, W_out, b_out, x_out, ext_d):
    N = TILES
    with ExitStack() as ctx:
        def sb(name, shape, dt=F32):
            return ctx.enter_context(nc.sbuf_tensor("ab_" + name, shape, dt))

        def pb(name):
            return ctx.enter_context(nc.psum_tensor("ab_" + name, [P, 512], F32))

        sems = []

        def sem(name):
            sems.append(nc.alloc_semaphore("ab_" + name))
            return sems[-1]

        VW = 32
        ident_r = sb("ident_r", [P, P], F32R)
        ident = ident_r[:].bitcast(F32)
        w_qkv = sb("w_qkv", [P, KD, 3 * D])
        w_o = sb("w_o", [P, KD, D])
        b_qkv = sb("b_qkv", [P, 3 * D])
        b_o = sb("b_o", [P, D])
        minus_half = sb("minus_half", [P, 1])
        toep = sb("toep", [P, HEADS, TOEP])
        x_t = sb("x_t", [P, 2, D])
        stats = sb("stats", [P, 6])
        mean_var = sb("mean_var", [P, 2, 2])
        rstd = sb("rstd", [P, 2])
        xn = sb("xn", [P, 2, D])
        xn_T = sb("xn_T", [P, 2, KD, P])
        qk = sb("qk", [P, 2 * D])
        parts = sb("parts", [P, 2, HEADS, 4, DH])
        q_T = sb("q_T", [P, 2, HEADS // 2, SEQ], F32R)
        k_T = sb("k_T", [P, 2, HEADS // 2, SEQ], F32R)
        v_t = sb("v_t", [P, 2, IB, HEADS, VW])
        neg_max = sb("neg_max", [P, 8])
        e_t = sb("e_t", [P, 8, SEQ])
        e_T = sb("e_T", [P, 2, 4, IB, P])
        o_sb = sb("o_sb", [P, 2, HEADS // 4, P])
        rec = sb("rec", [P, HEADS])
        o_t = sb("o_t", [P, 2, D])
        o_T = sb("o_T", [P, KD, P])
        x_p = sb("x_p", [P, 2, D])
        y_t = sb("y_t", [P, 2, D])
        S = [pb(f"s{i}") for i in range(3)]
        ET = [pb(f"et{i}") for i in range(2)]
        O = pb("o")
        M = [pb(f"m{i}") for i in range(2)]

        w_loaded = sem("w_loaded")
        toep_loaded = [sem(f"toep_loaded{q}") for q in range(4)]
        wq_scaled = sem("wq_scaled")
        ident_zeroed = sem("ident_zeroed")
        ident_ready = sem("ident_ready")
        v_cleared = sem("v_cleared")
        v_ones = sem("v_ones")
        x_loaded = [sem(f"x_loaded{p}") for p in range(2)]
        xp_loaded = [sem(f"xp_loaded{p}") for p in range(2)]
        stats_done = sem("stats_done")
        mv_done = sem("mv_done")
        pool_step = sem("pool_step")
        xn_ready = sem("xn_ready")
        xt_ps = sem("xt_ps")
        xn_T_ready = sem("xn_T_ready")
        qk_ps = sem("qk_ps")
        v_ps = sem("v_ps")
        qk_ready = sem("qk_ready")
        v_ready = sem("v_ready")
        hi_ready = sem("hi_ready")
        parts_ready = sem("parts_ready")
        t_ps = sem("t_ps")
        t_by_act = sem("t_by_act")
        t_by_dve = sem("t_by_dve")
        s_done = sem("s_done")
        max_done = sem("max_done")
        exp_done = sem("exp_done")
        et_ps = sem("et_ps")
        et_by_act = sem("et_by_act")
        et_by_dve = sem("et_by_dve")
        pv_done = sem("pv_done")
        o_copied = sem("o_copied")
        ot_ps = sem("ot_ps")
        rec_done = sem("rec_done")
        norm_done = sem("norm_done")
        oT_ps = sem("oT_ps")
        o_T_ready = sem("o_T_ready")
        wo_ps = sem("wo_ps")
        xb_ready = sem("xb_ready")
        y_ready = sem("y_ready")
        y_stored = [sem(f"y_stored{p}") for p in range(2)]
        block = ctx.enter_context(nc.Block())
        AHEAD = IB
        BODY = 2 * IB

        def run(eng, step):
            for k in range(BODY):
                step(k, k)
            with eng.Fori(1, N // BODY) as u:
                for k in range(BODY):
                    step(BODY * u + k, k)

        def has(i, back):
            return not isinstance(i, int) or i >= back

        LAG = 5
        PE_QK, PE_OUT, PE_XT, PE_WO, PE_OT, PE_V = 2, 3, 5, 6, 7, 9
        PE_T = {10: 0, 12: 1, 13: 2, 15: 3}
        PE_PV, ACT_O = 11, 12
        ACT_OUT, ACT_XT = 3, 5
        ACT_T = {10: 0, 13: 2, 15: 3}
        DVE_STATS, DVE_QK, DVE_Y, DVE_O, DVE_V, DVE_T1 = 1, 3, 7, 8, 10, 13

        def group_of(s, first):
            return (s - first) // 4 if (s - first) % 4 == 0 else None

        def own(j, k):
            return 8 * (j - k % 2) + 16

        @block.sync
        def _(sp):
            def load_x(j, k):
                tile = j % N if isinstance(j, int) else sp.snap(j % N, min_val=0, max_val=N - 1)
                wait(sp, xn_ready, j - 1)
                sp.dma_start(x_t[:, k % 2, :], x_in[bass.ts(tile, P), :]).then_inc(x_loaded[k % 2], 16)

            def load_xp(i, k):
                wait(sp, y_ready, i - 1)
                sp.dma_start(x_p[:, k % 2, :], x_in[bass.ts(i, P), :]).then_inc(xp_loaded[k % 2], 16)

            def store_y(j, k):
                wait(sp, y_ready, j + 1)
                sp.dma_start(x_out[bass.ts(j, P), :], y_t[:, k % 2, :]).then_inc(y_stored[k % 2], 16)

            sp.dma_start(w_qkv[:], W_qkv.rearrange("(k p) n -> p k n", p=P)).then_inc(w_loaded, 16)
            sp.dma_start(b_qkv[:], b_qkv_d.partition_broadcast(P)).then_inc(w_loaded, 16)
            sp.dma_start(w_o[:], W_out.rearrange("(k p) n -> p k n", p=P)).then_inc(w_loaded, 16)
            sp.dma_start(b_o[:], b_out.partition_broadcast(P)).then_inc(w_loaded, 16)
            for j in range(3):
                load_x(j, j)
            skewed = ext_d[:, P - 1:P - 1 + P * (EXT - 1)].rearrange("h (p w) -> p h w", w=EXT - 1)
            for h in range(0, HEADS, 2):
                sp.dma_start(toep[:, h:h + 2, :], skewed[:, h:h + 2, 0:TOEP]).then_inc(toep_loaded[h // 4], 16)
                if h // 2 < 4:
                    load_x(3 + h // 2, 3 + h // 2)

            def step(i, k):
                load_x(i + AHEAD + 3, k + AHEAD + 3)
                if has(i, 1):
                    load_xp(i - 1, k + BODY - 1)
                if has(i, 3):
                    store_y(i - 3, k + BODY - 3)

            run(sp, step)
            load_xp(N - 1, N - 1)
            store_y(N - 3, N - 3)
            store_y(N - 2, N - 2)
            store_y(N - 1, N - 1)
            for p in range(2):
                sp.wait_ge(y_stored[p], 16 * (N // 2))

        @block.gpsimd
        def _(pool):
            unity = o_t[:, 0, 0:P]
            nc.gpsimd.memset(unity, 0.0).then_inc(ident_zeroed, 1)
            nc.gpsimd.memset(minus_half[:], -0.5).then_inc(ident_zeroed, 1)
            nc.gpsimd.memset(v_t[:], 0.0).then_inc(v_cleared, 1)
            pool.wait_ge(ident_zeroed, 2)
            nc.gpsimd.affine_select(out=unity, in_=unity, compare_op=ALU.not_equal, fill=1.0, base=0,
                                    pattern=[[-1, P]], channel_multiplier=1).then_inc(ident_ready, 1)
            pool.wait_ge(ident_ready, 1)
            nc.gpsimd.tensor_copy(ident_r[:], unity).then_inc(ident_ready, 1)
            pool.wait_ge(v_cleared, 1)
            nc.gpsimd.memset(v_t[:].rearrange("p b i h w -> p (b i h) w")[:, :, DH:DH + 1], 1.0).then_inc(v_ones, 1)

            def normalise(j, k):
                p = k % 2
                wait_apart(pool, mv_done, j + 1)
                nc.gpsimd.tensor_scalar(rstd[:, p:p + 1], mean_var[:, p, 1:2], EPS, None, ALU.add)\
                    .then_inc(pool_step, 1)
                wait(pool, pool_step, 2 * j + 1)
                nc.gpsimd.tensor_tensor(rstd[:, p:p + 1], rstd[:, p:p + 1], minus_half[:], ALU.pow)\
                    .then_inc(pool_step, 1)
                wait(pool, pool_step, 2 * j + 2)
                wait_apart(pool, xt_ps, j - 1)
                nc.gpsimd.tensor_scalar(xn[:, p, :], x_t[:, p, :], mean_var[:, p, 0:1], rstd[:, p:p + 1],
                                        ALU.subtract, ALU.mult).then_inc(xn_ready, 1)

            def split(j):
                wait(pool, qk_ready, j + 1)
                wait_apart(pool, t_ps, 4 * j)
                dup = [parts[:, 0, :, 0:2, :], parts[:, 1, :, 0:4:2, :]]
                low = [parts[:, 0, :, 2:4, :], parts[:, 1, :, 1:4:2, :]]
                src = [qk[:, m * D:(m + 1) * D].rearrange("p (h x) -> p h x", x=DH).unsqueeze(1)
                       .broadcast_to([P, 2, HEADS, DH]) for m in range(2)]
                turn = "p h a x -> p a h x"
                for m in range(2):
                    nc.gpsimd.tensor_scalar(dup[m].rearrange(turn).bitcast(F32R), src[m], 1.0, None, ALU.mult)\
                        .then_inc(hi_ready, 1)
                for m in range(2):
                    wait(pool, hi_ready, 2 * j + 1 + m)
                    nc.gpsimd.tensor_tensor(low[m].rearrange(turn).bitcast(F32R), src[m], dup[m].rearrange(turn),
                                            ALU.subtract).then_inc(parts_ready, 1)

            def add_bias(i, k):
                wait(pool, xp_loaded[k % 2], own(i, k))
                nc.gpsimd.tensor_tensor(x_p[:, k % 2, :], x_p[:, k % 2, :], b_o[:], ALU.add).then_inc(xb_ready, 1)

            pool.wait_ge(w_loaded, 4 * 16)
            normalise(0, 0)
            for j in range(AHEAD):
                normalise(j + 1, j + 1)
                split(j)
            normalise(AHEAD + 1, AHEAD + 1)

            def step(i, k):
                split(i + AHEAD)
                if has(i, 2):
                    add_bias(i - 2, k + BODY - 2)
                normalise(i + AHEAD + 2, k + AHEAD + 2)

            run(pool, step)
            add_bias(N - 2, N - 2)
            add_bias(N - 1, N - 1)

        def t_out(n, k):
            dst = (q_T, k_T)[n // 2]
            at = k % IB * P
            return dst[:, k // IB % 2, n % 2 * 4:n % 2 * 4 + 4, at:at + P]

        T_BANK = [0, 1, 0, 1]
        QK, XT, OT = M[0], M[0][:, 0:D], M[0]
        OUT_T, WO, V = [M[1][:, 0:D]] * 3

        def psum_heads(a):
            return a.rearrange("p (c t) -> p c t", c=4)

        @block.scalar
        def _(act):
            def copy_xn_T(j, k):
                wait(act, xt_ps, j + 1)
                wait(act, v_ps, j - 1)
                nc.scalar.activation(xn_T[:, k % 2, :, :], XT.rearrange("p (k t) -> p k t", k=KD), ACT.Copy)\
                    .then_inc(xn_T_ready, 1)

            def copy_t(j, k, n):
                wait(act, t_ps, 4 * j + n + 1)
                wait(act, s_done, 16 * (j - k % IB - IB))
                nc.scalar.activation(t_out(n, k), psum_heads(M[T_BANK[n]][:]), ACT.Copy).then_inc(t_by_act, 1)

            def exp(i, s):
                wait(act, max_done, 16 * i + s + 1)
                q = s % 8
                nc.scalar.activation(e_t[:, q, :], e_t[:, q, :], ACT.Exp, bias=neg_max[:, q:q + 1], scale=-1.0)\
                    .then_inc(exp_done, 1)

            def copy_et(i, s):
                g = s // 4
                wait(act, et_ps, 16 * i + s + 1)
                if s % 4 == 0:
                    wait(act, pv_done, 4 * i + g - 1)
                nc.scalar.activation(e_T[:, g % 2, s % 4, :, :], psum_heads(ET[0][:]), ACT.Copy).then_inc(et_by_act, 1)

            def copy_o(i, g, k):
                wait(act, pv_done, 4 * i + g + 1)
                if g % 4 == 0:
                    wait(act, ot_ps, i + g // 4 - 1)
                nc.scalar.activation(o_sb[:, (k + g // 4) % 2, g % 4, :], O[:, 0:P], ACT.Copy).then_inc(o_copied, 1)

            def copy_o_T(j):
                wait(act, oT_ps, j + 1)
                wait(act, wo_ps, j)
                nc.scalar.activation(o_T[:], OUT_T.rearrange("p (k t) -> p k t", k=KD), ACT.Copy)\
                    .then_inc(o_T_ready, 1)

            for j in range(AHEAD):
                copy_xn_T(j, j)
                for n in (0, 2, 3):
                    copy_t(j, j, n)

            copy_xn_T(AHEAD, AHEAD)

            def step(i, k):
                for s in range(16):
                    if (s - LAG) % 2 == 0 and has(16 * i + s, LAG):
                        copy_et(i, s - LAG)
                    g = group_of(s, ACT_O)
                    if g is not None and has(4 * i + g, 0):
                        copy_o(i, g, k)
                    exp(i, s)
                    if s == ACT_OUT and has(i, 3):
                        copy_o_T(i - 3)
                    if s == ACT_XT:
                        copy_xn_T(i + AHEAD + 1, k + AHEAD + 1)
                    if s in ACT_T:
                        copy_t(i + AHEAD, k + AHEAD, ACT_T[s])

            run(act, step)
            copy_et(N, -4)
            copy_et(N, -2)
            for g in (-3, -2, -1):
                copy_o(N, g, N)
            for j in range(N - 3, N):
                copy_o_T(j)

        @block.vector
        def _(dve):
            def statistics(j, k):
                wait(dve, x_loaded[k % 2], own(j, k))
                wait(dve, mv_done, j)
                nc.vector.bn_stats(stats[:], x_t[:, k % 2, :]).then_inc(stats_done, 1)
                wait(dve, stats_done, j + 1)
                wait_apart(dve, xn_ready, j - 1)
                nc.vector.bn_aggr(mean_var[:, k % 2, :], stats[:]).then_inc(mv_done, 1)

            def add_qk(j):
                wait(dve, qk_ps, j + 1)
                wait(dve, parts_ready, 2 * j)
                nc.vector.tensor_tensor(qk[:], QK[:], b_qkv[:, 0:2 * D], ALU.add).then_inc(qk_ready, 1)

            def add_v(j, k):
                wait(dve, v_ps, j + 1)
                wait(dve, pv_done, 4 * (j - k % IB - IB))
                nc.vector.tensor_tensor(v_t[:, k // IB % 2, k % IB, :, 0:DH],
                                        V.rearrange("p (h x) -> p h x", x=DH),
                                        b_qkv[:, 2 * D:3 * D].rearrange("p (h x) -> p h x", x=DH), ALU.add)\
                    .then_inc(v_ready, 1)

            def copy_t(j, k, n):
                wait(dve, t_ps, 4 * j + n + 1)
                wait(dve, s_done, 16 * (j - k % IB - IB))
                nc.vector.tensor_copy(t_out(n, k), psum_heads(M[T_BANK[n]][:])).then_inc(t_by_dve, 1)

            def add_bias(i, k, s):
                n = 16 * i + s
                at = SEQ - P - k % IB * P
                wait(dve, s_done, n + 1)
                wait_apart(dve, et_ps, n - 7)
                nc.vector.tensor_tensor_reduce(out=e_t[:, s % 8, :], in0=S[(k * 16 + s) % 3][:],
                                               in1=toep[:, s, at:at + SEQ], scale=1.0, scalar=3.0e38, op0=ALU.add,
                                               op1=ALU.min, accum_out=neg_max[:, s % 8:s % 8 + 1])\
                    .then_inc(max_done, 1)

            def copy_et(i, s):
                g = s // 4
                wait(dve, et_ps, 16 * i + s + 1)
                if s % 4 == 1:
                    wait(dve, pv_done, 4 * i + g - 1)
                nc.vector.tensor_copy(e_T[:, g % 2, s % 4, :, :], psum_heads(ET[1][:])).then_inc(et_by_dve, 1)

            def divide(j, k):
                groups = OT[:].rearrange("p (h w) -> p h w", w=VW)
                wait(dve, ot_ps, j + 1)
                wait(dve, norm_done, j)
                nc.vector.reciprocal(rec[:], groups[:, :, DH]).then_inc(rec_done, 1)
                wait(dve, rec_done, j + 1)
                wait(dve, oT_ps, j - 1)
                nc.vector.tensor_tensor(o_t[:, k % 2, :].rearrange("p (h x) -> p h x", x=DH), groups[:, :, 0:DH],
                                        rec[:].unsqueeze(2).broadcast_to([P, HEADS, DH]), ALU.mult)\
                    .then_inc(norm_done, 1)

            def add_residual(j, k):
                wait(dve, wo_ps, j + 1)
                wait(dve, xb_ready, j + 1)
                wait(dve, y_stored[k % 2], own(j, k) - 16)
                nc.vector.tensor_tensor(y_t[:, k % 2, :], WO, x_p[:, k % 2, :], ALU.add)\
                    .then_inc(y_ready, 1)

            dve.wait_ge(w_loaded, 4 * 16)
            dve.wait_ge(v_ones, 1)
            nc.vector.tensor_scalar(w_qkv[:, :, 0:D], w_qkv[:, :, 0:D], -1.0 / DH ** 0.5, None, ALU.mult)\
                .then_inc(wq_scaled, 1)
            nc.vector.tensor_scalar(b_qkv[:, 0:D], b_qkv[:, 0:D], -1.0 / DH ** 0.5, None, ALU.mult)\
                .then_inc(wq_scaled, 1)
            dve.wait_ge(wq_scaled, 2)
            statistics(0, 0)
            for j in range(AHEAD):
                statistics(j + 1, j + 1)
                add_qk(j)
                add_v(j, j)
                copy_t(j, j, 1)
            statistics(AHEAD + 1, AHEAD + 1)

            def step(i, k):
                for s in range(16):
                    if isinstance(i, int) and i == 0 and s % 4 == 0:
                        dve.wait_ge(toep_loaded[s // 4], 2 * 16)
                    add_bias(i, k, s)
                    if (s - LAG) % 2 == 0 and has(16 * i + s, LAG + 1):
                        copy_et(i, s - LAG - 1)
                    if s == DVE_O and has(i, 2):
                        divide(i - 2, k)
                    if s == DVE_T1:
                        copy_t(i + AHEAD, k + AHEAD, 1)
                    if s == DVE_QK:
                        add_qk(i + AHEAD)
                    if s == DVE_V:
                        add_v(i + AHEAD, k + AHEAD)
                    if s == DVE_Y and has(i, 3):
                        add_residual(i - 3, k + BODY - 3)
                    if s == DVE_STATS:
                        statistics(i + AHEAD + 2, k + AHEAD + 2)

            run(dve, step)
            for s in (-5, -3, -1):
                copy_et(N, s)
            for j in (N - 2, N - 1):
                divide(j, j)
            for j in range(N - 3, N):
                add_residual(j, j)

        @block.tensor
        def _(pe):
            def transpose_x(j, k):
                wait(pe, xn_ready, j + 1)
                if isinstance(j, int) and j <= AHEAD:
                    wait(pe, t_by_act, 3 * j - 1)
                else:
                    wait(pe, qk_ready, j)
                for c in range(KD):
                    last = nc.tensor.transpose(XT[:, c * P:(c + 1) * P], xn[:, k % 2, c * P:(c + 1) * P], ident[:])
                last.then_inc(xt_ps, 1)

            def project_qk(j, k):
                wait(pe, xn_T_ready, j + 1)
                wait(pe, t_by_act, 3 * j - 1)
                for c in range(KD):
                    last = nc.tensor.matmul(QK[:], xn_T[:, k % 2, c, :], w_qkv[:, c, 0:2 * D],
                                            start=c == 0, stop=c == KD - 1)
                last.then_inc(qk_ps, 1)

            def project_v(j, k):
                wait(pe, t_by_act, 3 * j)
                wait(pe, y_ready, j - AHEAD - 2)
                for c in range(KD):
                    last = nc.tensor.matmul(V, xn_T[:, k % 2, c, :], w_qkv[:, c, 2 * D:3 * D],
                                            start=c == 0, stop=c == KD - 1)
                last.then_inc(v_ps, 1)

            def transpose_parts(j, n):
                wait(pe, parts_ready, 2 * (j + 1))
                if n == 0:
                    wait(pe, qk_ready, j + 1)
                    if not isinstance(j, int) or j >= AHEAD:
                        wait(pe, xn_T_ready, j + 2)
                    wait(pe, norm_done, j - AHEAD - 1)
                elif n == 1:
                    wait(pe, v_ready, j + 1)
                elif n == 2:
                    wait(pe, t_by_act, 3 * j + 1)
                else:
                    wait(pe, t_by_dve, j + 1)
                for c in range(4):
                    m = n % 2 * 4 + c
                    last = nc.tensor.transpose(M[T_BANK[n]][:, c * P:(c + 1) * P].bitcast(F32R),
                                               parts[:, n // 2, 2 * m:2 * m + 2, :, :]
                                               .rearrange("p h a x -> p (h a x)").bitcast(F32R), ident_r[:])
                last.then_inc(t_ps, 1)

            def scores(i, k, s):
                n = 16 * i + s
                wait(pe, max_done, n - 1 if k == 0 and s < 2 else n - 2)
                if s == 0 and k % IB == 0:
                    wait(pe, t_by_act, 3 * (i + IB))
                    wait(pe, t_by_dve, i + IB)
                lo, at = s % 2 * 64, k % IB * P
                nc.tensor.matmul(S[(k * 16 + s) % 3][:], q_T[lo:lo + 64, k // IB % 2, s // 2, at:at + P],
                                 k_T[lo:lo + 64, k // IB % 2, s // 2, :], start=True, stop=True).then_inc(s_done, 1)

            def transpose_e(i, s):
                n = 16 * i + s
                wait(pe, exp_done, n + 1)
                wait(pe, et_by_dve if s % 2 else et_by_act, 8 * i + s // 2)
                for c in range(IB):
                    last = nc.tensor.transpose(ET[s % 2][:, c * P:(c + 1) * P], e_t[:, s % 8, c * P:(c + 1) * P],
                                               ident[:])
                last.then_inc(et_ps, 1)

            def values(group, gk):
                wait(pe, et_by_act, 2 * (group + 1))
                wait(pe, et_by_dve, 2 * (group + 1))
                wait(pe, o_copied, group)
                b = gk // (4 * IB) % 2
                for c in range(IB):
                    for q in range(4):
                        last = nc.tensor.matmul(O[q * VW:(q + 1) * VW, 0:P], v_t[:, b, c, gk % 4 * 4 + q, :],
                                                e_T[:, gk % 2, q, c, :], start=c == 0, stop=c == IB - 1)
                last.then_inc(pv_done, 1)

            def transpose_o(j, k):
                wait(pe, o_copied, 4 * (j + 1))
                for g in range(HEADS // 4):
                    last = nc.tensor.transpose(OT[:, g * P:(g + 1) * P], o_sb[:, k % 2, g, :], ident[:])
                last.then_inc(ot_ps, 1)

            def transpose_out(j, k):
                wait(pe, norm_done, j + 1)
                for c in range(KD):
                    last = nc.tensor.transpose(OUT_T[:, c * P:(c + 1) * P], o_t[:, k % 2, c * P:(c + 1) * P],
                                               ident[:])
                last.then_inc(oT_ps, 1)

            def output(j):
                wait(pe, o_T_ready, j + 1)
                for c in range(KD):
                    last = nc.tensor.matmul(WO, o_T[:, c, :], w_o[:, c, :], start=c == 0, stop=c == KD - 1)
                last.then_inc(wo_ps, 1)

            pe.wait_ge(ident_ready, 2)
            pe.wait_ge(wq_scaled, 2)
            for j in range(AHEAD):
                transpose_x(j, j)
                project_qk(j, j)
                project_v(j, j)
                for n in range(4):
                    transpose_parts(j, n)
            transpose_x(AHEAD, AHEAD)

            def step(i, k):
                m = i + AHEAD
                for s in range(16):
                    scores(i, k, s)
                    if s == PE_QK:
                        project_qk(m, k + AHEAD)
                    if s == PE_OUT and has(i, 3):
                        wait(pe, t_by_act, 3 * m)
                        transpose_out(i - 3, k + BODY - 3)
                    if s == PE_WO and has(i, 3):
                        output(i - 3)
                    if s == PE_OT and has(i, 2):
                        wait(pe, xn_T_ready, m + 2)
                        transpose_o(i - 2, k)
                    if s == PE_V:
                        project_v(m, k + AHEAD)
                    if s in PE_T:
                        transpose_parts(m, PE_T[s])
                    if s == PE_XT:
                        transpose_x(m + 1, k + AHEAD + 1)
                    g = group_of(s, PE_PV)
                    if g is not None and has(4 * i + g, 0):
                        values(4 * i + g, 4 * (k + BODY) + g)
                    if has(16 * i + s, LAG):
                        transpose_e(i, s - LAG)

            run(pe, step)
            for s in range(-LAG, 0):
                transpose_e(N, s)
            for group in (4 * N - 2, 4 * N - 1):
                values(group, group)
            wait(pe, t_by_act, 3 * (N + AHEAD))
            for j in (N - 2, N - 1):
                wait(pe, norm_done, j)
                transpose_o(j, j)
            for j in range(N - 3, N):
                transpose_out(j, j)
                output(j)
                wait(pe, y_ready, j + 1)

    nc.clear_and_free_semaphores(sems)
    nc.all_engine_barrier()


I32 = mybir.dt.int32
U32 = mybir.dt.uint32

E = 8
TOP = 2
FF = 512
KF = FF // P
SLOT_TILES = TOP * TILES + E
ALL_TILES = TILES + SLOT_TILES
GT = 4
GROUPS = TILES // GT
ROW = D + 2


def pairs(eng, step):
    for p in range(2):
        step(0, p)
    with eng.Fori(1, TILES // 2) as h:
        for p in range(2):
            step(h, p)


def build_ffn(nc, tag, x_in, Wg, Ws1, Ws3, Ws2, We1, We3, We2, x_out, rows_d):
    with ExitStack() as ctx:
        def sb(name, shape, dt=F32):
            return ctx.enter_context(nc.sbuf_tensor(tag + name, shape, dt))

        def sem(name):
            return ctx.enter_context(nc.semaphore(tag + name))

        ident = sb("ident", [P, P])
        w_up = sb("w_up", [P, E + 1, KD, 2 * FF])
        w_down = sb("w_down", [P, E + 1, KF, D])
        xn_all = sb("xn_all", [P, TILES, D])
        logits = sb("logits", [P, TILES, E])
        slots = sb("slots", [P, TILES, TOP], U32)
        labels = sb("labels", [P, TILES, TOP, 2])
        quad_experts = sb("quad_experts", [1, SLOT_TILES // 4], I32)
        consts_ready = sem("consts_ready")
        w_loaded = sem("w_loaded")
        shared_loaded = sem("shared_loaded")

        with ExitStack() as c1:
            def sb1(name, shape, dt=F32):
                return c1.enter_context(nc.sbuf_tensor(tag + name, shape, dt))

            def sem1(name):
                return c1.enter_context(nc.semaphore(tag + name))

            w_g = sb1("w_g", [P, KD, E])
            minus_half = sb1("minus_half", [P, GT])
            x_t = sb1("x_t", [P, 4, GT, D])
            stats = sb1("stats", [P, GT, 6])
            mean_var = sb1("mean_var", [P, 2, GT, 2])
            rstd = sb1("rstd", [P, 2, GT])
            xn = sb1("xn", [P, 2, GT, D])
            xn_T = sb1("xn_T", [P, 2, GT, KD, P])
            XT = [c1.enter_context(nc.psum_tensor(tag + f"xt{i}", [P, 512], F32)) for i in range(4)]
            GL = [c1.enter_context(nc.psum_tensor(tag + f"gl{i}", [P, 512], F32)) for i in range(2)]
            wg_loaded = sem1("wg_loaded")
            x_loaded = [sem1(f"x_loaded{r}") for r in range(4)]
            stats_done = sem1("stats_done")
            mv_done = sem1("mv_done")
            pool_step = sem1("pool_step")
            xn_ready = sem1("xn_ready")
            xn_kept = sem1("xn_kept")
            xt_ps = sem1("xt_ps")
            xn_T_ready = sem1("xn_T_ready")
            gl_ps = sem1("gl_ps")
            gl_copied = sem1("gl_copied")
            block = c1.enter_context(nc.Block())

            @block.sync
            def _(sp):
                sp.dma_start(w_g[:], Wg.rearrange("(k p) n -> p k n", p=P)).then_inc(wg_loaded, 16)

                def load_x(g, r):
                    wait(sp, xn_ready, g - 3)
                    sp.dma_start(x_t[:, r, :, :], x_in[bass.ts(g, GT * P), :].rearrange("(a p) n -> p a n", p=P))\
                        .then_inc(x_loaded[r], 16)

                for r in range(4):
                    load_x(r, r)
                def load_w(e, w1, w3, w2, loaded):
                    sp.dma_start(w_up[:, e, :, 0:FF], w1.rearrange("(k p) n -> p k n", p=P)).then_inc(loaded, 16)
                    sp.dma_start(w_up[:, e, :, FF:2 * FF], w3.rearrange("(k p) n -> p k n", p=P)).then_inc(loaded, 16)
                    sp.dma_start(w_down[:, e, :, :], w2.rearrange("(k p) n -> p k n", p=P)).then_inc(loaded, 16)

                with sp.Fori(1, GROUPS // 4) as m:
                    for r in range(4):
                        load_x(4 * m + r, r)
                load_w(E, Ws1, Ws3, Ws2, shared_loaded)
                for e in range(E):
                    load_w(e, We1[e], We3[e], We2[e], w_loaded)

            @block.gpsimd
            def _(pool):
                nc.gpsimd.memset(ident[:], 0.0).then_inc(consts_ready, 1)
                nc.gpsimd.memset(minus_half[:], -0.5).then_inc(consts_ready, 1)
                pool.wait_ge(consts_ready, 2)
                nc.gpsimd.affine_select(out=ident[:], in_=ident[:], compare_op=ALU.not_equal, fill=1.0, base=0,
                                        pattern=[[-1, P]], channel_multiplier=1).then_inc(consts_ready, 1)

                def step(g, p):
                    wait_apart(pool, mv_done, GT * g + GT)
                    nc.gpsimd.tensor_scalar(rstd[:, p, :], mean_var[:, p, :, 1], EPS, None, ALU.add)\
                        .then_inc(pool_step, 1)
                    wait(pool, pool_step, 2 * g + 1)
                    nc.gpsimd.tensor_tensor(rstd[:, p, :], rstd[:, p, :], minus_half[:], ALU.pow)\
                        .then_inc(pool_step, 1)

                step(0, 0)
                step(1, 1)
                with pool.Fori(1, GROUPS // 2) as h:
                    for p in range(2):
                        step(2 * h + p, p)

            @block.vector
            def _(dve):
                def mean_and_var(g, r):
                    p = r % 2
                    wait(dve, x_loaded[r], 4 * (g - r) + 16)
                    wait(dve, mv_done, GT * g)
                    for i in range(GT):
                        nc.vector.bn_stats(stats[:, i, :], x_t[:, r, i, :]).then_inc(stats_done, 1)
                    wait_apart(dve, stats_done, GT * g + GT)
                    for i in range(GT):
                        nc.vector.bn_aggr(mean_var[:, p, i, :], stats[:, i, :]).then_inc(mv_done, 1)

                def normalise(g, r):
                    p = r % 2
                    wait_apart(dve, mv_done, GT * g + GT)
                    wait(dve, pool_step, 2 * g + 2)
                    wait(dve, xn_kept, g - 1)
                    wait(dve, xt_ps, 2 * g - 2)
                    for i in range(GT):
                        last = nc.vector.tensor_scalar(xn[:, p, i, :], x_t[:, r, i, :], mean_var[:, p, i, 0:1],
                                                       rstd[:, p, i:i + 1], ALU.subtract, ALU.mult)
                    last.then_inc(xn_ready, 1)

                mean_and_var(0, 0)
                for r in range(1, 4):
                    mean_and_var(r, r)
                    normalise(r - 1, r - 1)
                with dve.Fori(1, GROUPS // 4) as m:
                    for r in range(4):
                        mean_and_var(4 * m + r, r)
                        normalise(4 * m + r - 1, (r - 1) % 4)
                normalise(GROUPS - 1, 3)

            @block.scalar
            def _(act):
                def step(g, p, start=False):
                    wait(act, xn_ready, g + 1)
                    nc.scalar.activation(xn_all[:, bass.ds(GT * g, GT), :], xn[:, p, :, :], ACT.Copy)\
                        .then_inc(xn_kept, 1)
                    for q in range(2):
                        wait(act, xt_ps, 2 * g + q + 1)
                        wait(act, gl_ps, g - 1)
                        nc.scalar.activation(xn_T[:, p, 2 * q:2 * q + 2, :, :],
                                             XT[2 * p + q][:].rearrange("p (a k t) -> p a k t", a=2, k=KD), ACT.Copy)\
                            .then_inc(xn_T_ready, 1)
                    if not start:
                        copy_logits(g - 1, 1 - p)

                def copy_logits(g, p):
                    wait(act, gl_ps, g + 1)
                    nc.scalar.activation(logits[:, bass.ds(GT * g, GT), :],
                                         GL[p][:, 0:GT * E].rearrange("p (a e) -> p a e", a=GT), ACT.Copy)\
                        .then_inc(gl_copied, 1)

                step(0, 0, start=True)
                step(1, 1)
                with act.Fori(1, GROUPS // 2) as h:
                    for p in range(2):
                        step(2 * h + p, p)
                copy_logits(GROUPS - 1, 1)

            @block.tensor
            def _(pe):
                def transpose_xn(g, p):
                    wait(pe, xn_ready, g + 1)
                    for q in range(2):
                        wait(pe, xn_T_ready, 2 * g + q - 3)
                        for i in range(2):
                            for k in range(KD):
                                last = nc.tensor.transpose(XT[2 * p + q][:, (i * KD + k) * P:(i * KD + k + 1) * P],
                                                           xn[:, p, 2 * q + i, k * P:(k + 1) * P], ident[:])
                        last.then_inc(xt_ps, 1)

                def gate_logits(g, p):
                    wait(pe, xn_T_ready, 2 * g + 2)
                    wait(pe, gl_copied, g - 1)
                    for i in range(GT):
                        for k in range(KD):
                            last = nc.tensor.matmul(GL[p][:, i * E:(i + 1) * E], xn_T[:, p, i, k, :], w_g[:, k, :],
                                                    start=k == 0, stop=k == KD - 1)
                    last.then_inc(gl_ps, 1)

                pe.wait_ge(consts_ready, 3)
                pe.wait_ge(wg_loaded, 16)
                transpose_xn(0, 0)
                transpose_xn(1, 1)
                gate_logits(0, 0)
                with pe.Fori(1, GROUPS // 2) as h:
                    for p in range(2):
                        transpose_xn(2 * h + p, p)
                        gate_logits(2 * h + p - 1, 1 - p)
                gate_logits(GROUPS - 1, 1)

        with ExitStack() as c2:
            def sb2(name, shape, dt=F32):
                return c2.enter_context(nc.sbuf_tensor(tag + name, shape, dt))

            def sem2(name):
                return c2.enter_context(nc.semaphore(tag + name))

            def pb2(name):
                return c2.enter_context(nc.psum_tensor(tag + name, [P, 512], F32))

            below = sb2("below", [P, P])
            ones = sb2("ones", [P, P])
            rank8 = sb2("rank8", [P, E])
            rank8_i = sb2("rank8_i", [P, E], I32)
            tile_no = sb2("tile_no", [1, SLOT_TILES])
            tile_no_i = sb2("tile_no_i", [1, SLOT_TILES], I32)
            gates = sb2("gates", [P, TILES, E])
            top = sb2("top", [P, TOP, TILES])
            pick = sb2("pick", [P, TILES, E])
            first = sb2("first", [P, TILES])
            hot = sb2("hot", [P, TOP, TILES, E])
            mask = sb2("mask", [P, TILES, E])
            total = sb2("total", [P, 2, TILES, E])
            ends = sb2("ends", [P, 2, E])
            n_tiles = sb2("n_tiles", [P, E])
            n_int = sb2("n_int", [P, E], I32)
            slot = sb2("slot", [P, TILES, E])
            picked = sb2("picked", [P, TILES, E])
            slot_f = sb2("slot_f", [P, TOP, TILES])
            tile_ge = sb2("tile_ge", [1, SLOT_TILES, E - 1])
            tile_e_f = sb2("tile_e_f", [1, 4 + SLOT_TILES])
            quad_f = sb2("quad_f", [1, SLOT_TILES // 4])
            token_no = sb2("token_no", [P, TILES], I32)
            idx = sb2("idx", [P, 4, TOP], U32)
            idx_add = sb2("idx_add", [P, 2, 1], U32)
            x_r = sb2("x_r", [P, 2, D])
            x_t = sb2("x_t2", [P, 4, TOP, ROW])
            x_T = sb2("x_T", [P, 2, KD, P])
            gate = sb2("gate", [P, 2, FF])
            hid = sb2("hid", [P, 2, FF])
            hid_T = sb2("hid_T", [P, 2, KF, P])
            y_t = sb2("y_t", [P, 2, D])
            A = [pb2(f"a{i}") for i in range(2)]
            B = [pb2(f"b{i}") for i in range(2)]
            X = pb2("x")
            H = pb2("h")
            Y = [pb2(f"y{i}") for i in range(2)]

            route_consts = sem2("route_consts")
            gates_ready = sem2("gates_ready")
            chain = sem2("chain")
            mask_ready = sem2("mask_ready")
            counts_ps = sem2("counts_ps")
            routed = sem2("routed")
            idx_ready = sem2("idx_ready")
            row_copied = sem2("row_copied")
            scattered = [sem2(f"scattered{r}") for r in range(4)]
            x_loaded = [sem2(f"x_loaded2{r}") for r in range(4)]
            x_ps = sem2("x_ps")
            x_T_ready = sem2("x_T_ready")
            a_ps = sem2("a_ps")
            b_ps = sem2("b_ps")
            gate_ready = sem2("gate_ready")
            hid_ready = sem2("hid_ready")
            h_ps = sem2("h_ps")
            hid_T_ready = sem2("hid_T_ready")
            y_ps = sem2("y_ps")
            y_ready = sem2("y_ready")
            x_r_loaded = [sem2(f"x_r_loaded{p}") for p in range(2)]
            x_r_stored = [sem2(f"x_r_stored{p}") for p in range(2)]
            spare_stored = sem2("spare_stored")
            labelled = sem2("labelled")
            idx_add_ready = sem2("idx_add_ready")
            added = sem2("added")
            block = c2.enter_context(nc.Block())
            PAIRS = ALL_TILES // 2
            QUADS = ALL_TILES // 4

            @block.sync
            def _(sp):
                def load_residual(t, p):
                    wait(sp, x_r_stored[p], 8 * (t - p))
                    sp.dma_start(x_r[:, p, :], x_in[bass.ts(t, P), :]).then_inc(x_r_loaded[p], 16)

                def store_sum(t, p):
                    wait(sp, y_ready, t + 1)
                    sp.dma_start(x_out[bass.ts(t, P), :], x_r[:, p, :]).then_inc(x_r_stored[p], 16)

                def load_x(t, r):
                    fixed = isinstance(t, int)
                    slot_tile = t - TILES if fixed else sp.snap(t - TILES)
                    passed = t - 3 if fixed else sp.snap(t - 3)
                    slots_passed = slot_tile - 3 if fixed else sp.snap(t - TILES - 3)
                    wait_apart(sp, idx_add_ready, slots_passed)
                    wait_apart(sp, x_ps, passed)
                    if not fixed:
                        wait_apart(sp, y_ready, passed)
                    sp.dma_start(x_t[:, r, 0, :], rows_d[bass.ts(slot_tile, P), :]).then_inc(x_loaded[r], 16)

                load_residual(0, 0)
                load_residual(1, 1)
                store_sum(0, 0)
                sp.dma_start(x_out[T:T + P, :], x_r[:, 0, :]).then_inc(spare_stored, 16)
                sp.wait_ge(spare_stored, 16)
                load_residual(2, 0)
                store_sum(1, 1)
                load_residual(3, 1)
                with sp.Fori(2, TILES // 2) as h:
                    for p in range(2):
                        store_sum(2 * h + p - 2, p)
                        load_residual(2 * h + p, p)
                for r in range(4):
                    sp.wait_ge(scattered[r], 16 * TOP * (TILES // 4))
                for r in range(4):
                    load_x(TILES + r, r)
                store_sum(TILES - 2, 0)
                store_sum(TILES - 1, 1)
                with sp.Fori(TILES // 4 + 1, QUADS) as m:
                    for r in range(4):
                        load_x(4 * m + r, r)

            @block.gpsimd
            def _(pool):
                nc.gpsimd.memset(ones[:], 1.0).then_inc(route_consts, 1)
                nc.gpsimd.memset(below[:], 1.0).then_inc(route_consts, 1)
                nc.gpsimd.iota(rank8_i[:], pattern=[[-1, E]], base=E, channel_multiplier=0).then_inc(route_consts, 1)
                nc.gpsimd.iota(tile_no_i[:], pattern=[[1, SLOT_TILES]], base=0, channel_multiplier=0)\
                    .then_inc(route_consts, 1)
                nc.gpsimd.iota(token_no[:], pattern=[[P, TILES]], base=0, channel_multiplier=1)\
                    .then_inc(route_consts, 1)
                pool.wait_ge(route_consts, 5)
                nc.gpsimd.affine_select(out=below[:], in_=below[:], compare_op=ALU.is_gt, fill=0.0, base=0,
                                        pattern=[[1, P]], channel_multiplier=-1).then_inc(route_consts, 1)
                nc.gpsimd.tensor_copy(rank8[:], rank8_i[:]).then_inc(route_consts, 1)
                nc.gpsimd.tensor_copy(tile_no[:], tile_no_i[:]).then_inc(route_consts, 1)
                nc.gpsimd.tensor_copy(labels[:, :, :, 0], token_no[:].unsqueeze(2).broadcast_to([P, TILES, TOP]))\
                    .then_inc(route_consts, 1)

                def copy_row(t, r):
                    wait(pool, x_ps, t - 3)
                    wait(pool, scattered[r], 4 * TOP * (t - r))
                    nc.gpsimd.tensor_copy(x_t[:, r, :, 0:D], xn_all[:, bass.ds(t, 1), :].broadcast_to([P, TOP, D]))\
                        .then_inc(row_copied, 1)

                def scatter(t, r):
                    wait(pool, scattered[r], 4 * TOP * (t - r))
                    nc.gpsimd.tensor_copy(x_t[:, r, :, D:ROW], labels[:, bass.ds(t, 1), :, :]
                                          .rearrange("p a k n -> p (a k) n")).then_inc(labelled, 1)
                    nc.gpsimd.tensor_copy(idx[:, r, :], slots[:, t, :]).then_inc(idx_ready, 1)
                    wait(pool, row_copied, t + 1)
                    wait(pool, labelled, t + 1)
                    wait_apart(pool, idx_ready, t + 1)
                    for k in range(TOP):
                        pool.indirect_dma_start(out=rows_d[:, :],
                                                out_offset=bass.IndirectOffsetOnAxis(ap=idx[:, r, k:k + 1], axis=0),
                                                in_=x_t[:, r, k, :], in_offset=None).then_inc(scattered[r], 16)

                for r in range(4):
                    copy_row(r, r)
                pool.wait_ge(routed, 1)
                for r in range(4):
                    scatter(r, r)
                with pool.Fori(1, TILES // 4) as m:
                    for r in range(4):
                        copy_row(4 * m + r, r)
                        scatter(4 * m + r, r)
                for r in range(4):
                    pool.wait_ge(scattered[r], 16 * TOP * (TILES // 4))

                def add_y(t, r):
                    wait_apart(pool, x_loaded[r], 4 * (t - TILES - r) + 16)
                    nc.gpsimd.tensor_copy(idx_add[:, r % 2, :], x_t[:, r, 0, D:D + 1]).then_inc(idx_add_ready, 1)
                    wait(pool, idx_add_ready, t - TILES + 1)
                    wait(pool, y_ready, t + 1)
                    wait_apart(pool, added, 16 * (t - TILES))
                    pool.indirect_dma_start(out=x_out[:, :], in_=y_t[:, r % 2, :], in_offset=None, compute_op=ALU.add,
                                            out_offset=bass.IndirectOffsetOnAxis(ap=idx_add[:, r % 2, :], axis=0))\
                        .then_inc(added, 16)

                for p in range(2):
                    pool.wait_ge(x_r_stored[p], 16 * (TILES // 2))
                pool.wait_ge(spare_stored, 16)
                for r in range(4):
                    add_y(TILES + r, r)
                with pool.Fori(TILES // 4 + 1, QUADS) as m:
                    for r in range(4):
                        add_y(4 * m + r, r)
                pool.wait_ge(added, 16 * SLOT_TILES)

            @block.scalar
            def _(act):
                nc.scalar.activation(gates[:], logits[:], ACT.Sigmoid).then_inc(gates_ready, 1)

                def copy_x_T(t, p):
                    wait(act, x_ps, t + 1)
                    wait(act, b_ps, t - 1)
                    nc.scalar.activation(x_T[:, p, :, :], X[:, 0:D].rearrange("p (k t) -> p k t", k=KD), ACT.Copy)\
                        .then_inc(x_T_ready, 1)

                def silu(t, p):
                    wait(act, a_ps, t + 1)
                    wait(act, hid_ready, t - 1)
                    nc.scalar.activation(gate[:, p, :], A[p][:], ACT.Silu).then_inc(gate_ready, 1)

                def copy_hid_T(t, p):
                    wait(act, h_ps, t + 1)
                    wait(act, y_ps, t - 1)
                    nc.scalar.activation(hid_T[:, p, :, :], H[:].rearrange("p (k t) -> p k t", k=KF), ACT.Copy)\
                        .then_inc(hid_T_ready, 1)

                def step(t, p, start=False, end=False):
                    silu(t, p)
                    if not start:
                        copy_hid_T(t - 1, 1 - p)
                    if not end:
                        copy_x_T(t + 1, 1 - p)

                copy_x_T(0, 0)
                step(0, 0, start=True)
                step(1, 1)
                with act.Fori(1, PAIRS - 1) as h:
                    step(2 * h, 0)
                    step(2 * h + 1, 1)
                step(ALL_TILES - 2, 0)
                step(ALL_TILES - 1, 1, end=True)
                copy_hid_T(ALL_TILES - 1, 1)

            @block.vector
            def _(dve):
                links = [0]

                def link(instruction):
                    links[0] += 1
                    instruction.then_inc(chain, 1)
                    dve.wait_ge(chain, links[0])

                def over_experts(a):
                    return a.unsqueeze(2).broadcast_to([P, TILES, E])

                dve.wait_ge(gates_ready, 1)
                dve.wait_ge(route_consts, 9)
                for k in range(TOP):
                    link(nc.vector.tensor_reduce(top[:, k, :], gates[:], AX.X, ALU.max))
                    link(nc.vector.tensor_tensor(pick[:], gates[:], over_experts(top[:, k, :]), ALU.is_equal))
                    link(nc.vector.tensor_tensor(pick[:], pick[:], rank8[:].unsqueeze(1).broadcast_to([P, TILES, E]),
                                                 ALU.mult))
                    link(nc.vector.tensor_reduce(first[:], pick[:], AX.X, ALU.max))
                    link(nc.vector.tensor_tensor(hot[:, k, :, :], pick[:], over_experts(first[:]), ALU.is_equal))
                    if k + 1 < TOP:
                        link(nc.vector.scalar_tensor_tensor(gates[:], hot[:, k, :, :], -2.0, gates[:], ALU.mult,
                                                            ALU.add))
                nc.vector.tensor_tensor(mask[:], hot[:, 0, :, :], hot[:, 1, :, :], ALU.add).then_inc(mask_ready, 1)
                link(nc.vector.tensor_tensor(first[:], top[:, 0, :], top[:, 1, :], ALU.add))
                link(nc.vector.reciprocal(first[:], first[:]))
                for k in range(TOP):
                    link(nc.vector.scalar_tensor_tensor(labels[:, :, k, 1], top[:, k, :], 1.0 / (1 + TOP), first[:],
                                                        ALU.mult, ALU.mult))
                dve.wait_ge(counts_ps, 1)
                within, of_tile = A[0], B[0]
                link(nc.vector.tensor_copy(total[:, 0, :, :], of_tile[:, 0:TILES * E].rearrange("p (t e) -> p t e", e=E)))
                at, d = 0, 1
                while d < TILES:
                    link(nc.vector.tensor_copy(total[:, 1 - at, 0:d, :], total[:, at, 0:d, :]))
                    link(nc.vector.tensor_tensor(total[:, 1 - at, d:TILES, :], total[:, at, d:TILES, :],
                                                 total[:, at, 0:TILES - d, :], ALU.add))
                    at, d = 1 - at, 2 * d
                link(nc.vector.tensor_scalar(n_tiles[:], total[:, at, TILES - 1, :], float(P - 1), None, ALU.add))
                link(nc.vector.tensor_copy(n_int[:], n_tiles[:]))
                link(nc.vector.tensor_scalar(n_int[:], n_int[:], P.bit_length() - 1, None, ALU.arith_shift_right))
                link(nc.vector.tensor_copy(n_tiles[:], n_int[:]))
                link(nc.vector.tensor_copy(ends[:, 0, :], n_tiles[:]))
                be, d = 0, 1
                while d < E:
                    link(nc.vector.tensor_copy(ends[:, 1 - be, 0:d], ends[:, be, 0:d]))
                    link(nc.vector.tensor_tensor(ends[:, 1 - be, d:E], ends[:, be, d:E], ends[:, be, 0:E - d], ALU.add))
                    be, d = 1 - be, 2 * d
                link(nc.vector.tensor_tensor(n_tiles[:], ends[:, be, :], n_tiles[:], ALU.subtract))
                link(nc.vector.tensor_scalar(n_tiles[:], n_tiles[:], float(P), None, ALU.mult))
                link(nc.vector.tensor_tensor(slot[:], total[:, at, :, :],
                                             of_tile[:, 0:TILES * E].rearrange("p (t e) -> p t e", e=E), ALU.subtract))
                link(nc.vector.tensor_tensor(slot[:], slot[:],
                                             within[:, 0:TILES * E].rearrange("p (t e) -> p t e", e=E), ALU.add))
                link(nc.vector.tensor_tensor(slot[:], slot[:], n_tiles[:].unsqueeze(1).broadcast_to([P, TILES, E]),
                                             ALU.add))
                for k in range(TOP):
                    link(nc.vector.tensor_tensor(picked[:], slot[:], hot[:, k, :, :], ALU.mult))
                    link(nc.vector.tensor_reduce(slot_f[:, k, :], picked[:], AX.X, ALU.add))
                    link(nc.vector.tensor_copy(slots[:, :, k], slot_f[:, k, :]))
                link(nc.vector.tensor_tensor(tile_ge[:], tile_no[:].unsqueeze(2).broadcast_to([1, SLOT_TILES, E - 1]),
                                             ends[0:1, be, 0:E - 1].unsqueeze(1)
                                             .broadcast_to([1, SLOT_TILES, E - 1]), ALU.is_ge))
                link(nc.vector.tensor_reduce(tile_e_f[:, 1:1 + SLOT_TILES], tile_ge[:], AX.X, ALU.add))
                link(nc.vector.memset(tile_e_f[:, 0:1], 0.0))
                link(nc.vector.tensor_copy(quad_f[:], tile_e_f[:, 4:4 + SLOT_TILES:4]))
                for i in range(3, -1, -1):
                    link(nc.vector.scalar_tensor_tensor(quad_f[:], quad_f[:], float(E), tile_e_f[:, i:i + SLOT_TILES - 3:4],
                                                        ALU.mult, ALU.add))
                nc.vector.tensor_copy(quad_experts[:], quad_f[:]).then_inc(routed, 1)

                def gate_by_up(t, p):
                    wait(dve, gate_ready, t + 1)
                    wait(dve, b_ps, t + 1)
                    wait(dve, h_ps, t - 1)
                    nc.vector.tensor_tensor(hid[:, p, :], gate[:, p, :], B[p][:], ALU.mult).then_inc(hid_ready, 1)

                def weigh_y(t, r):
                    wait(dve, y_ps, t + 1)
                    wait(dve, added, 16 * (t - TILES - 1))
                    nc.vector.tensor_scalar(y_t[:, r % 2, :], Y[r % 2][:, 0:D], x_t[:, r, 0, D + 1:ROW], None, ALU.mult)\
                        .then_inc(y_ready, 1)

                def add_residual(t, r):
                    p = r % 2
                    wait(dve, y_ps, t + 1)
                    wait(dve, x_r_loaded[p], 8 * (t - p) + 16)
                    nc.vector.scalar_tensor_tensor(x_r[:, p, :], Y[p][:, 0:D], 1.0 / (1 + TOP), x_r[:, p, :],
                                                   ALU.mult, ALU.add).then_inc(y_ready, 1)

                gate_by_up(0, 0)
                gate_by_up(1, 1)
                with dve.Fori(0, TILES // 4) as m:
                    for r in range(4):
                        add_residual(4 * m + r, r)
                        gate_by_up(4 * m + r + 2, r % 2)
                for r in range(4):
                    weigh_y(TILES + r, r)
                    gate_by_up(TILES + r + 2, r % 2)
                with dve.Fori(TILES // 4 + 1, QUADS - 1) as m:
                    for r in range(4):
                        weigh_y(4 * m + r, r)
                        gate_by_up(4 * m + r + 2, r % 2)
                for r in range(4):
                    weigh_y(ALL_TILES - 4 + r, r)
                    if r < 2:
                        gate_by_up(ALL_TILES - 2 + r, r)

            @block.tensor
            def _(pe):
                pe.wait_ge(route_consts, 9)
                pe.wait_ge(mask_ready, 1)
                nc.tensor.matmul(A[0][:, 0:TILES * E], below[:], mask[:].rearrange("p t e -> p (t e)"),
                                 start=True, stop=True)
                nc.tensor.matmul(B[0][:, 0:TILES * E], ones[:], mask[:].rearrange("p t e -> p (t e)"),
                                 start=True, stop=True).then_inc(counts_ps, 1)

                def transpose_x(t, r, shared):
                    wait(pe, x_T_ready, t)
                    if shared:
                        wait(pe, row_copied, t + 1)
                    else:
                        wait(pe, x_loaded[r], 4 * (t - TILES - r) + 16)
                    for k in range(KD):
                        last = nc.tensor.transpose(X[:, k * P:(k + 1) * P], x_t[:, r, 0, k * P:(k + 1) * P], ident[:])
                    last.then_inc(x_ps, 1)

                def up(t, p, e, out, col, done):
                    for k in range(KD):
                        last = nc.tensor.matmul(out[p][:], x_T[:, p, k, :], w_up[:, e, k, col:col + FF],
                                                start=k == 0, stop=k == KD - 1)
                    last.then_inc(done, 1)

                def transpose_hid(t, p):
                    wait(pe, hid_ready, t + 1)
                    wait(pe, hid_T_ready, t)
                    for k in range(KF):
                        last = nc.tensor.transpose(H[:, k * P:(k + 1) * P], hid[:, p, k * P:(k + 1) * P], ident[:])
                    last.then_inc(h_ps, 1)

                def down(t, p, e):
                    wait(pe, hid_T_ready, t + 1)
                    wait(pe, y_ready, t - 1)
                    for k in range(KF):
                        last = nc.tensor.matmul(Y[p][:, 0:D], hid_T[:, p, k, :], w_down[:, e, k, :],
                                                start=k == 0, stop=k == KF - 1)
                    last.then_inc(y_ps, 1)

                def step(t, r, e, e_before, start=False, end=False, next_shared=False):
                    p = r % 2
                    wait(pe, x_T_ready, t + 1)
                    wait(pe, hid_ready, t - 1)
                    up(t, p, e, A, 0, a_ps)
                    if not start:
                        transpose_hid(t - 1, 1 - p)
                    up(t, p, e, B, FF, b_ps)
                    if not end:
                        transpose_x(t + 1, (r + 1) % 4, next_shared)
                    if not start:
                        down(t - 1, 1 - p, e_before)

                def quad(m, e_before=None, end=False):
                    code = pe.value_load(quad_experts[0:1, bass.ds(m - TILES // 4, 1)], min_val=0, max_val=E ** 5 - 1)
                    e = [(code >> (3 * i)) & (E - 1) for i in range(5)]
                    if e_before is not None:
                        e[0] = e_before
                    for r in range(4):
                        step(4 * m + r, r, e[r + 1], e[r], end=end and r == 3)
                    return e[4]

                pe.wait_ge(shared_loaded, 3 * 16)
                pe.wait_ge(routed, 1)
                transpose_x(0, 0, True)
                for r in range(4):
                    step(r, r, E, E, start=r == 0, next_shared=True)
                with pe.Fori(1, TILES // 4 - 1) as m:
                    for r in range(4):
                        step(4 * m + r, r, E, E, next_shared=True)
                for r in range(4):
                    step(TILES - 4 + r, r, E, E, next_shared=r < 3)
                pe.wait_ge(w_loaded, 3 * 16 * E)
                quad(TILES // 4, e_before=E)
                with pe.Fori(TILES // 4 + 1, QUADS - 1) as m:
                    quad(m)
                e_last = quad(QUADS - 1, end=True)
                transpose_hid(ALL_TILES - 1, 1)
                down(ALL_TILES - 1, 1, e_last)


def build_network(nc, x, a_w, b_w, f_w, out):
    def dram(name, shape):
        return nc.dram_tensor(name, shape, F32).ap()

    x1, x2, x3 = [dram(name, (T + P, D)) for name in ("after_a", "after_f1", "after_b")]
    v_d = dram("a_values", (T + 2 * P, D))
    rs_d = dram("a_row_sums", (TILES * 4, SEQ))
    slot_rows = [dram("slot_rows" + n, (SLOT_TILES * P, ROW)) for n in "12"]
    ext_d = dram("bias_rows", (HEADS, P * EXT))
    Wq, bq, Wk, bk, Wv, bv, Wo, bo = a_w
    W_qkv, b_qkv, W_out, b_out, rel_bias = b_w
    with ExitStack() as ctx:
        ext_sb = ctx.enter_context(nc.sbuf_tensor("ext_sb", [HEADS, EXT], F32))
        build_bias_rows(nc, rel_bias, ext_sb)
        build_attention_a(nc, x, Wq, bq, Wk, bk, Wv, bv, Wo, bo, x1, v_d, rs_d, slot_rows, ext_sb, ext_d)
    build_ffn(nc, "f1_", x1, *f_w, x2, slot_rows[0])
    build_attention_b(nc, x2, W_qkv, b_qkv, W_out, b_out, x3, ext_d)
    build_ffn(nc, "f2_", x3, *f_w, out, slot_rows[1])


A_NAMES = ["L0_attn_a_" + n for n in ("Wq", "bq", "Wk", "bk", "Wv", "bv", "Wo", "bo")]
B_NAMES = ["L0_attn_b_" + n for n in ("W_qkv", "b_qkv", "W_out", "b_out", "rel_bias")]
F_NAMES = ["L0_ffn_" + n for n in ("Wg", "Ws1", "Ws3", "Ws2", "We1", "We3", "We2")]


def kernel(**inputs):
    import numpy as np
    import concourse.bacc as bacc
    from concourse.bass_utils import run_bass_kernel_spmd

    nc = bacc.Bacc("TRN2", target_bir_lowering=False, num_devices=1)
    x = np.ascontiguousarray(inputs["L0_attn_a_X_embed"])
    arrays = {"in_x": x.reshape(T, D)}
    for name in A_NAMES + B_NAMES + F_NAMES:
        arrays["in_" + name] = np.ascontiguousarray(inputs[name])
    aps = {name: nc.dram_tensor(name, a.shape, mybir.dt.from_np(a.dtype), kind="ExternalInput").ap()
           for name, a in arrays.items()}
    out = nc.dram_tensor("out_x", (T + P, D), F32, kind="ExternalOutput").ap()
    build_network(nc, aps["in_x"], [aps["in_" + n] for n in A_NAMES], [aps["in_" + n] for n in B_NAMES],
                  [aps["in_" + n] for n in F_NAMES], out)
    r = run_bass_kernel_spmd(nc, [arrays], core_ids=[0])
    return r.results[0]["out_x"][0:T].reshape(x.shape)
```

```python
import concourse.bass as bass
from concourse import mybir
from contextlib import ExitStack

F32 = mybir.dt.float32
F32R = mybir.dt.float32r
ALU = mybir.AluOpType
ACT = mybir.ActivationFunctionType
AX = mybir.AxisListType

P = 128
D = 256
KD = D // P
HEADS = 16
DH = D // HEADS
T = 4096
TILES = T // P
EPS = 1e-5


def wait(eng, sem, value):
    if not isinstance(value, int) or value > 0:
        eng.wait_ge(sem, value)


def wait_apart(eng, sem, value):
    wait(eng, sem, value)
    if not isinstance(value, int):
        eng.nop(nofuse=True)


def build_attention_a(nc, x_in, Wq, bq, Wk, bk, Wv, bv, Wo, bo, x_out, v_d, rs_d, slot_rows, ext_sb, ext_d):
    HT = 4
    R = P // HT
    L = R * HEADS
    G = 4
    EXT_COPIES = P // TILES
    SCALE = 1.0 / D
    with ExitStack() as ctx:
        def sb(name, shape, dt=F32):
            return ctx.enter_context(nc.sbuf_tensor("aa_" + name, shape, dt))

        def pb(name):
            return ctx.enter_context(nc.psum_tensor("aa_" + name, [P, 512], F32))

        sems = []

        def sem(name):
            sems.append(nc.alloc_semaphore("aa_" + name))
            return sems[-1]

        ident = sb("ident", [P, P])
        ident_r = sb("ident_r", [P, P], F32R)
        w_qkv = sb("w_qkv", [P, KD, 3 * D])
        w_o = sb("w_o", [P, KD, D])
        b_qkv = sb("b_qkv", [P, 3 * D])
        b_o = sb("b_o", [P, D])
        minus_half = sb("minus_half", [P, 1])
        x_t = sb("x_t", [P, 2, D])
        stats = sb("stats", [P, 6])
        mean_var = sb("mean_var", [P, 2, 2])
        rstd = sb("rstd", [P, 2])
        xn = sb("xn", [P, 2, D])
        xn_T = sb("xn_T", [P, 2, KD, P])
        qk = sb("qk", [P, 2, 2 * D])
        v_t = sb("v_t", [P, 2, D])
        parts = sb("parts", [P, 2, HEADS, 8, DH])
        qk_T = sb("qk_T", [P, 2, HT, HEADS, R], F32R)
        k_T = sb("k_T", [64, 2, HT, HEADS * R], F32R)
        neg_max = sb("neg_max", [P, 8])
        e_t = sb("e_t", [P, G, HT, L])
        den = sb("den", [P, G, HT])
        inv = sb("inv", [P, G, HT])
        rs_sb = sb("rs_sb", [P, L])
        rs_t = sb("rs_t", [P, 2, HEADS])
        v_p = sb("v_p", [P, 2, D])
        x_p = sb("x_p", [P, 2, D])
        xb = sb("xb", [P, 2, D])
        o_t = sb("o_t", [P, 2, D])
        o_T = sb("o_T", [P, KD, P])
        y_t = sb("y_t", [P, 2, D])
        S = [pb(f"s{i}") for i in range(4)]
        M = [pb(f"m{i}") for i in range(3)]
        RS = pb("rs")

        blank = sb("blank", [P, D + 2])
        blank_no = sb("blank_no", [P, 1], mybir.dt.int32)
        blank_zeroed = sem("blank_zeroed")
        blank_ready = sem("blank_ready")
        blanks_filled = sem("blanks_filled")
        ext_stored = sem("ext_stored")
        w_loaded = sem("w_loaded")
        wq_scaled = sem("wq_scaled")
        ident_zeroed = sem("ident_zeroed")
        ident_ready = sem("ident_ready")
        x_loaded = [sem(f"x_loaded{p}") for p in range(2)]
        stats_done = sem("stats_done")
        mv_done = sem("mv_done")
        pool_step = sem("pool_step")
        xn_ready = sem("xn_ready")
        xt_ps = sem("xt_ps")
        xn_T_ready = sem("xn_T_ready")
        qk_ps = sem("qk_ps")
        v_ps = sem("v_ps")
        qk_ready = sem("qk_ready")
        v_ready = sem("v_ready")
        v_stored = [sem(f"v_stored{p}") for p in range(2)]
        hi_ready = sem("hi_ready")
        parts_ready = sem("parts_ready")
        t_ps = sem("t_ps")
        t_by_act = sem("t_by_act")
        t_by_dve = sem("t_by_dve")
        k_T_moved = [sem(f"k_T_moved{p}") for p in range(2)]
        s_done = sem("s_done")
        max_done = sem("max_done")
        exp_done = sem("exp_done")
        inv_done = sem("inv_done")
        rs_done = sem("rs_done")
        rs_copied = sem("rs_copied")
        rs_stored = sem("rs_stored")
        post_loaded = [sem(f"post_loaded{p}") for p in range(2)]
        xb_ready = sem("xb_ready")
        out_ready = sem("out_ready")
        ot_ps = sem("ot_ps")
        o_T_ready = sem("o_T_ready")
        wo_ps = sem("wo_ps")
        y_ready = sem("y_ready")
        y_stored = [sem(f"y_stored{p}") for p in range(2)]

        block = ctx.enter_context(nc.Block())


        def run(eng, step):
            step(0, 0, 0)
            step(1, 1, 0)
            with eng.Fori(1, TILES // 2) as h:
                step(2 * h, 0, h)
                step(2 * h + 1, 1, h)

        def has(i, back):
            return not isinstance(i, int) or i >= back

        PE_R = {1: -2, 5: -1, 9: 0, 13: 1}
        PE_OT, PE_WO, PE_XT, PE_QK, PE_V = 0, 3, 5, (11, 13), 14
        PE_T = {6: 0, 7: 1, 9: 2, 10: 3}
        ACT_OT, ACT_RS, ACT_XT = 0, 3, 4
        ACT_T = {5: 0, 8: 2}
        DVE_INV = {3: -1, 7: 0, 11: 1, 15: 2}
        DVE_Y, DVE_STATS, DVE_QK, DVE_V = 4, 9, 13, 15
        DVE_T = {8: 1, 11: 3}

        @block.sync
        def _(sp):
            def load_x(j, p, h):
                tile = j % TILES if isinstance(j, int) else sp.snap(j % TILES, min_val=0, max_val=TILES - 1)
                wait(sp, xn_ready, j - 1)
                sp.dma_start(x_t[:, p, :], x_in[bass.ts(tile, P), :]).then_inc(x_loaded[p], 16)

            def store_v(j, p, h):
                wait(sp, v_ready, j + 1)
                sp.dma_start(v_d[bass.ts(j, P), :], v_t[:, p, :]).then_inc(v_stored[p], 16)

            def move_k(j, p, h):
                wait(sp, t_by_act, 2 * j + 2)
                wait(sp, t_by_dve, 2 * j + 2)
                wait(sp, s_done, 16 * (j - 1))
                sp.dma_start(k_T[:, p, :, :].bitcast(F32),
                             qk_T[64:P, p, :, :, :].rearrange("p e c r -> p e (c r)").bitcast(F32))\
                    .then_inc(k_T_moved[p], 16)

            def post_loads(j, p, h):
                wait(sp, rs_copied, j + 1)
                sp.dma_start(rs_d[bass.ts(j, HT), :], rs_sb[0:P - R + 1:R, :])\
                    .then_inc(rs_stored, 16)
                wait(sp, out_ready, j - 1)
                wait_apart(sp, xb_ready, j - 1)
                wait(sp, v_stored[p], 16 * (h + 1))
                sp.dma_start(v_p[:, p, :], v_d[bass.ts(j, P), :]).then_inc(post_loaded[p], 16)
                sp.dma_start(x_p[:, p, :], x_in[bass.ts(j, P), :]).then_inc(post_loaded[p], 16)
                wait(sp, rs_stored, 16 * (j + 1))
                sp.dma_start(rs_t[:, p, :], rs_d.rearrange("e (r c) -> (e r) c", c=HEADS)[bass.ts(j, P), :])\
                    .then_inc(post_loaded[p], 16)

            def store_y(j, p, h):
                wait(sp, y_ready, j + 1)
                sp.dma_start(x_out[bass.ts(j, P), :], y_t[:, p, :]).then_inc(y_stored[p], 16)

            for w, part in ((Wq, 0), (Wk, 1), (Wv, 2)):
                sp.dma_start(w_qkv[:, :, part * D:(part + 1) * D], w.rearrange("(k p) n -> p k n", p=P))\
                    .then_inc(w_loaded, 16)
            for b, part in ((bq, 0), (bk, 1), (bv, 2)):
                sp.dma_start(b_qkv[:, part * D:(part + 1) * D], b.partition_broadcast(P)).then_inc(w_loaded, 16)
            sp.dma_start(w_o[:], Wo.rearrange("(k p) n -> p k n", p=P)).then_inc(w_loaded, 16)
            sp.dma_start(b_o[:], bo.partition_broadcast(P)).then_inc(w_loaded, 16)
            load_x(0, 0, 0)
            load_x(1, 1, 0)
            load_x(2, 0, 1)
            sp.wait_ge(blank_ready, 1)
            fill_tiles = slot_rows[0].shape[0] // P
            for rows_d in slot_rows:
                sp.dma_start(rows_d[2 * TILES * P:fill_tiles * P, :].rearrange("(a p) n -> p a n", p=P),
                             blank[:].unsqueeze(1).broadcast_to([P, fill_tiles - 2 * TILES, D + 2]))\
                    .then_inc(blanks_filled, 16)
            store_v(0, 0, 0)
            store_v(1, 1, 0)
            move_k(0, 0, 0)

            def step(i, p, h):
                load_x(i + 3, 1 - p, h + 1 + p)
                if has(i, 1):
                    post_loads(i - 1, 1 - p, h - 1 + p)
                if has(i, 2):
                    store_y(i - 2, p, h - 1)
                move_k(i + 1, 1 - p, h + p)
                store_v(i + 2, p, h + 1)
                for rows_d in slot_rows:
                    sp.dma_start(rows_d[bass.ts(i, 2 * P), :].rearrange("(a p) n -> p a n", p=P),
                                 blank[:].unsqueeze(1).broadcast_to([P, 2, D + 2])).then_inc(blanks_filled, 16)
                sp.dma_start(ext_d.rearrange("h (p w) -> h p w", p=P)[:, bass.ts(i, EXT_COPIES), :],
                             ext_sb[:].unsqueeze(1).broadcast_to([HEADS, EXT_COPIES, ext_sb.shape[1]]))\
                    .then_inc(ext_stored, 16)

            run(sp, step)
            post_loads(TILES - 1, 1, TILES // 2 - 1)
            store_y(TILES - 2, 0, TILES // 2 - 1)
            store_y(TILES - 1, 1, TILES // 2 - 1)
            sp.wait_ge(blanks_filled, 16 * len(slot_rows) * (TILES + 1))
            sp.wait_ge(ext_stored, 16 * TILES)
            for p in range(2):
                sp.wait_ge(y_stored[p], 16 * (TILES // 2))
                sp.wait_ge(v_stored[p], 16 * (TILES // 2 + 1))

        @block.gpsimd
        def _(pool):
            nc.gpsimd.memset(blank[:], 0.0).then_inc(blank_zeroed, 1)
            nc.gpsimd.iota(blank_no[:], pattern=[[0, 1]], base=T, channel_multiplier=1).then_inc(blank_zeroed, 1)
            pool.wait_ge(blank_zeroed, 2)
            nc.gpsimd.tensor_copy(blank[:, D:D + 1], blank_no[:]).then_inc(blank_ready, 1)
            nc.gpsimd.memset(ident[:], 0.0).then_inc(ident_zeroed, 1)
            pool.wait_ge(ident_zeroed, 1)
            nc.gpsimd.affine_select(out=ident[:], in_=ident[:], compare_op=ALU.not_equal, fill=1.0, base=0,
                                    pattern=[[-1, P]], channel_multiplier=1).then_inc(ident_ready, 1)
            pool.wait_ge(ident_ready, 1)
            nc.gpsimd.tensor_copy(ident_r[:], ident[:]).then_inc(ident_ready, 1)
            nc.gpsimd.memset(minus_half[:], -0.5).then_inc(ident_zeroed, 1)
            pool.wait_ge(ident_zeroed, 2)

            def normalise(j, p, h):
                wait_apart(pool, mv_done, j + 1)
                nc.gpsimd.tensor_scalar(rstd[:, p:p + 1], mean_var[:, p, 1:2], EPS, None, ALU.add)\
                    .then_inc(pool_step, 1)
                wait(pool, pool_step, 2 * j + 1)
                nc.gpsimd.tensor_tensor(rstd[:, p:p + 1], rstd[:, p:p + 1], minus_half[:], ALU.pow)\
                    .then_inc(pool_step, 1)
                wait(pool, pool_step, 2 * j + 2)
                wait_apart(pool, xt_ps, j - 1)
                nc.gpsimd.tensor_scalar(xn[:, p, :], x_t[:, p, :], mean_var[:, p, 0:1], rstd[:, p:p + 1],
                                        ALU.subtract, ALU.mult).then_inc(xn_ready, 1)

            def split(j, p, h):
                wait(pool, qk_ready, j + 1)
                wait_apart(pool, t_ps, 4 * (j - 1))
                for m, hi, lo in ((0, slice(0, 2), slice(2, 4)), (1, slice(4, 8, 2), slice(5, 8, 2))):
                    src = qk[:, p, m * D:(m + 1) * D].rearrange("p (c x) -> p c x", x=DH).unsqueeze(1)\
                        .broadcast_to([P, 2, HEADS, DH])
                    nc.gpsimd.tensor_scalar(parts[:, p, :, hi, :].rearrange("p c a x -> p a c x").bitcast(F32R), src,
                                            1.0, None, ALU.mult)\
                        .then_inc(hi_ready, 1)
                for m, hi, lo in ((0, slice(0, 2), slice(2, 4)), (1, slice(4, 8, 2), slice(5, 8, 2))):
                    src = qk[:, p, m * D:(m + 1) * D].rearrange("p (c x) -> p c x", x=DH).unsqueeze(1)\
                        .broadcast_to([P, 2, HEADS, DH])
                    wait(pool, hi_ready, 2 * j + 1 + m)
                    nc.gpsimd.tensor_tensor(parts[:, p, :, lo, :].rearrange("p c a x -> p a c x").bitcast(F32R), src,
                                            parts[:, p, :, hi, :].rearrange("p c a x -> p a c x"), ALU.subtract).then_inc(parts_ready, 1)

            def weigh(j, p, h):
                wait(pool, post_loaded[p], 48 * (h + 1))
                wait(pool, y_ready, j - 1)
                nc.gpsimd.tensor_tensor(xb[:, p, :], x_p[:, p, :], b_o[:], ALU.add).then_inc(xb_ready, 1)
                wait(pool, ot_ps, j - 1)
                nc.gpsimd.tensor_tensor(o_t[:, p, :].rearrange("p (c x) -> p c x", x=DH),
                                        v_p[:, p, :].rearrange("p (c x) -> p c x", x=DH),
                                        rs_t[:, p, :].unsqueeze(2).broadcast_to([P, HEADS, DH]),
                                        ALU.mult).then_inc(out_ready, 1)

            pool.wait_ge(w_loaded, 8 * 16)
            normalise(0, 0, 0)
            normalise(1, 1, 0)
            split(0, 0, 0)
            normalise(2, 0, 1)
            split(1, 1, 0)

            def step(i, p, h):
                if has(i, 1):
                    weigh(i - 1, 1 - p, h - 1 + p)
                normalise(i + 3, 1 - p, h + 1 + p)
                split(i + 2, p, h + 1)

            run(pool, step)
            weigh(TILES - 1, 1, TILES // 2 - 1)

        def t_out(p, n):
            return qk_T[:, p, :, 4 * n:4 * n + 4, :].rearrange("p e c r -> p c e r")

        T_BANK = [0, 2, 0, 1]
        XT_BANK, QK_BANK, V_BANK, OT_BANK, WO_BANK = 1, 2, 0, 1, 1

        @block.scalar
        def _(act):
            def copy_xn_T(j, p, h):
                wait(act, xt_ps, j + 1)
                wait(act, v_ps, j - 1)
                nc.scalar.activation(xn_T[:, p, :, :], M[XT_BANK][:, 0:D].rearrange("p (k t) -> p k t", k=KD),
                                     ACT.Copy).then_inc(xn_T_ready, 1)

            def copy_t(j, p, n):
                wait(act, t_ps, 4 * j + n + 1)
                wait(act, s_done, 16 * (j - 1))
                wait(act, k_T_moved[p], 16 * ((j - p) // 2) if isinstance(j, int) else k_moves(j, p))
                nc.scalar.activation(t_out(p, n), M[T_BANK[n]][:].rearrange("p (c e r) -> p c e r", c=4, e=HT), ACT.Copy)\
                    .then_inc(t_by_act, 1)

            def exp(i, p, g, e):
                n = 16 * i + 4 * g + e
                wait(act, max_done, n + 1)
                if e == 0:
                    wait(act, rs_done, 4 * (i - 1) + g + 1)
                shift = neg_max[:, 4 * (g % 2) + e:4 * (g % 2) + e + 1]
                nc.scalar.activation(e_t[:, g, e, :], S[e][:], ACT.Exp, bias=shift,
                                     scale=-1.0, accum_out=den[:, g, e:e + 1]).then_inc(exp_done, 1)

            def copy_rs(j):
                wait(act, rs_done, 4 * (j + 1))
                wait(act, rs_stored, 16 * j)
                nc.scalar.activation(rs_sb[:].rearrange("p (r c) -> p r c", c=HEADS),
                                     RS[:].rearrange("p (c r) -> p r c", c=HEADS), ACT.Copy).then_inc(rs_copied, 1)

            def copy_o_T(j):
                wait(act, ot_ps, j + 1)
                wait(act, wo_ps, j)
                nc.scalar.activation(o_T[:], M[OT_BANK][:, 0:D].rearrange("p (k t) -> p k t", k=KD), ACT.Copy)\
                    .then_inc(o_T_ready, 1)

            def k_moves(j, p):
                return 8 * (j - p)

            copy_xn_T(0, 0, 0)
            copy_xn_T(1, 1, 0)
            copy_t(0, 0, 0)
            copy_t(0, 0, 2)

            def step(i, p, h):
                for s in range(16):
                    exp(i, p, s // 4, s % 4)
                    if s == ACT_OT and has(i, 2):
                        copy_o_T(i - 2)
                    if s == ACT_RS and has(i, 1):
                        copy_rs(i - 1)
                    if s == ACT_XT:
                        copy_xn_T(i + 2, p, h + 1)
                    if s in ACT_T:
                        copy_t(i + 1, 1 - p, ACT_T[s])

            run(act, step)
            copy_o_T(TILES - 2)
            copy_rs(TILES - 1)
            copy_o_T(TILES - 1)

        @block.vector
        def _(dve):
            def statistics(j, p):
                wait(dve, x_loaded[p], 16 * (j // 2 + 1) if isinstance(j, int) else 8 * (j - p) + 16)
                wait(dve, mv_done, j)
                nc.vector.bn_stats(stats[:], x_t[:, p, :]).then_inc(stats_done, 1)
                wait(dve, stats_done, j + 1)
                wait_apart(dve, xn_ready, j - 1)
                nc.vector.bn_aggr(mean_var[:, p, :], stats[:]).then_inc(mv_done, 1)

            def add_qk(j, p):
                wait(dve, qk_ps, j + 1)
                wait(dve, parts_ready, 2 * (j - 1))
                nc.vector.tensor_tensor(qk[:, p, :], M[QK_BANK][:], b_qkv[:, 0:2 * D], ALU.add).then_inc(qk_ready, 1)

            def add_v(j, p):
                wait(dve, v_ps, j + 1)
                wait(dve, v_stored[p], 16 * (j // 2) if isinstance(j, int) else 8 * (j - p))
                nc.vector.tensor_tensor(v_t[:, p, :], M[V_BANK][:, 0:D], b_qkv[:, 2 * D:3 * D], ALU.add)\
                    .then_inc(v_ready, 1)

            def copy_t(j, p, n):
                wait(dve, t_ps, 4 * j + n + 1)
                wait(dve, s_done, 16 * (j - 1))
                wait(dve, k_T_moved[p], 16 * (j // 2) if isinstance(j, int) else 8 * (j - p))
                nc.vector.tensor_copy(t_out(p, n), M[T_BANK[n]][:].rearrange("p (c e r) -> p c e r", c=4, e=HT))\
                    .then_inc(t_by_dve, 1)

            def maximum(i, g, e):
                wait(dve, s_done, 16 * i + 4 * g + e + 1)
                nc.vector.tensor_reduce(neg_max[:, 4 * (g % 2) + e:4 * (g % 2) + e + 1], S[e][:], AX.X, ALU.min)\
                    .then_inc(max_done, 1)

            def invert(group, gp):
                wait(dve, exp_done, 4 * (group + 1))
                nc.vector.reciprocal(inv[:, gp, :], den[:, gp, :]).then_inc(inv_done, 1)

            def add_residual(j, p):
                wait(dve, wo_ps, j + 1)
                wait(dve, xb_ready, j + 1)
                wait(dve, y_stored[p], 16 * (j // 2) if isinstance(j, int) else 8 * (j - p))
                nc.vector.tensor_tensor(y_t[:, p, :], M[WO_BANK][:, 0:D], xb[:, p, :], ALU.add).then_inc(y_ready, 1)

            dve.wait_ge(w_loaded, 8 * 16)
            nc.vector.tensor_scalar(w_qkv[:, :, 0:D], w_qkv[:, :, 0:D], -SCALE, None, ALU.mult).then_inc(wq_scaled, 1)
            nc.vector.tensor_scalar(b_qkv[:, 0:D], b_qkv[:, 0:D], -SCALE, None, ALU.mult).then_inc(wq_scaled, 1)
            dve.wait_ge(wq_scaled, 2)
            statistics(0, 0)
            statistics(1, 1)
            add_qk(0, 0)
            add_v(0, 0)
            statistics(2, 0)
            add_qk(1, 1)
            add_v(1, 1)
            copy_t(0, 0, 1)
            copy_t(0, 0, 3)

            def step(i, p, h):
                for s in range(16):
                    maximum(i, s // 4, s % 4)
                    if s in DVE_INV and has(4 * i, -DVE_INV[s]):
                        invert(4 * i + DVE_INV[s], DVE_INV[s] % 4)
                    if s == DVE_Y and has(i, 2):
                        add_residual(i - 2, p)
                    if s in DVE_T:
                        copy_t(i + 1, 1 - p, DVE_T[s])
                    if s == DVE_STATS:
                        statistics(i + 3, 1 - p)
                    if s == DVE_QK:
                        add_qk(i + 2, p)
                    if s == DVE_V:
                        add_v(i + 2, p)

            run(dve, step)
            invert(4 * TILES - 1, 3)
            add_residual(TILES - 2, 0)
            add_residual(TILES - 1, 1)

        @block.tensor
        def _(pe):
            def transpose_x(j, p):
                wait(pe, xn_ready, j + 1)
                wait(pe, y_ready, j - 3)
                wait(pe, xn_T_ready, j)
                for k in range(KD):
                    last = nc.tensor.transpose(M[XT_BANK][:, k * P:(k + 1) * P], xn[:, p, k * P:(k + 1) * P], ident[:])
                last.then_inc(xt_ps, 1)

            def project_qk(j, p, k):
                if k == 0:
                    wait(pe, xn_T_ready, j + 1)
                    wait(pe, t_by_dve, 2 * (j - 1) + 1 if not isinstance(j, int) or j >= 2 else 0)
                    wait(pe, qk_ready, j)
                product = nc.tensor.matmul(M[QK_BANK][:], xn_T[:, p, k, :], w_qkv[:, k, 0:2 * D],
                                           start=k == 0, stop=k == KD - 1)
                if k == KD - 1:
                    product.then_inc(qk_ps, 1)

            def project_v(j, p):
                wait(pe, t_by_act, 2 * j if not isinstance(j, int) or j >= 2 else 0)
                wait(pe, v_ready, j)
                for k in range(KD):
                    last = nc.tensor.matmul(M[V_BANK][:, 0:D], xn_T[:, p, k, :], w_qkv[:, k, 2 * D:3 * D],
                                            start=k == 0, stop=k == KD - 1)
                last.then_inc(v_ps, 1)

            def transpose_parts(j, p, n):
                wait(pe, parts_ready, 2 * (j + 1))
                start = isinstance(j, int) and j == 0
                if n == 0:
                    wait(pe, v_ready, j + 1 + start)
                elif n == 1:
                    wait(pe, qk_ready, j + 1 + start)
                elif n == 2:
                    wait(pe, t_by_act, 2 * j + 1)
                else:
                    wait(pe, xn_T_ready, j + 2)
                for c in range(4):
                    last = nc.tensor.transpose(M[T_BANK[n]][:, c * P:(c + 1) * P].bitcast(F32R),
                                               parts[:, p, 4 * n + c, :, :].rearrange("p a x -> p (a x)")
                                               .bitcast(F32R), ident_r[:])
                last.then_inc(t_ps, 1)

            def scores(i, p, g, e):
                n = 16 * i + 4 * g + e
                wait(pe, exp_done, n - 3)
                nc.tensor.matmul(S[e][:], k_T[:, p, e, g * P:(g + 1) * P],
                                 qk_T[0:64, p, e, :, :].rearrange("p c r -> p (c r)"), start=True, stop=True).then_inc(s_done, 1)

            def row_sums(i, group, g):
                wait(pe, inv_done, group + 1)
                if g == 0:
                    wait(pe, rs_copied, i)
                for e in range(4):
                    last = nc.tensor.matmul(RS[e * R:(e + 1) * R, :], inv[:, g, e:e + 1].broadcast_to([P, R]),
                                            e_t[:, g, e, :], start=g == 0, stop=g == 3)
                last.then_inc(rs_done, 1)

            def transpose_o(j, p):
                wait(pe, out_ready, j + 1)
                if isinstance(j, int) and j >= TILES - 2:
                    wait(pe, t_by_dve, 2 * (TILES + 1))
                    wait(pe, y_ready, j)
                for k in range(KD):
                    last = nc.tensor.transpose(M[OT_BANK][:, k * P:(k + 1) * P], o_t[:, p, k * P:(k + 1) * P], ident[:])
                last.then_inc(ot_ps, 1)

            def output(j, p):
                wait(pe, o_T_ready, j + 1)
                for k in range(KD):
                    last = nc.tensor.matmul(M[WO_BANK][:, 0:D], o_T[:, k, :], w_o[:, k, :],
                                            start=k == 0, stop=k == KD - 1)
                last.then_inc(wo_ps, 1)

            pe.wait_ge(ident_ready, 2)
            pe.wait_ge(wq_scaled, 2)
            transpose_x(0, 0)
            transpose_x(1, 1)
            for j in range(2):
                for k in range(KD):
                    project_qk(j, j, k)
                project_v(j, j)
            for n in range(4):
                transpose_parts(0, 0, n)

            def step(i, p, h):
                for s in range(16):
                    if s == 0:
                        wait(pe, k_T_moved[p], 8 * (i - p) + 16)
                    scores(i, p, s // 4, s % 4)
                    if s in PE_R and has(4 * i, -PE_R[s]):
                        g = PE_R[s] % 4
                        row_sums(i, 4 * i + PE_R[s], g)
                    if s == PE_OT and has(i, 2):
                        transpose_o(i - 2, p)
                    if s == PE_WO and has(i, 2):
                        output(i - 2, p)
                    if s == PE_XT:
                        transpose_x(i + 2, p)
                    if s in PE_T:
                        transpose_parts(i + 1, 1 - p, PE_T[s])
                    if s in PE_QK:
                        project_qk(i + 2, p, PE_QK.index(s))
                    if s == PE_V:
                        project_v(i + 2, p)

            run(pe, step)
            transpose_o(TILES - 2, 0)
            output(TILES - 2, 0)
            row_sums(TILES, 4 * TILES - 2, 2)
            row_sums(TILES, 4 * TILES - 1, 3)
            transpose_o(TILES - 1, 1)
            output(TILES - 1, 1)

    nc.clear_and_free_semaphores(sems)
    nc.all_engine_barrier()


MAX_REL = 256
SEQ = 512
IB = SEQ // P
EXT = SEQ + P - 1 + SEQ - P
TOEP = 2 * SEQ - P


def build_bias_rows(nc, rel_bias, ext_sb):
    NR = 2 * MAX_REL + 1
    LO = EXT // 2 - MAX_REL
    with ExitStack() as ctx:
        def sb(name, shape):
            return ctx.enter_context(nc.sbuf_tensor("rb_" + name, shape, F32))

        def sem(name):
            return ctx.enter_context(nc.semaphore("rb_" + name))

        r_t = sb("r_t", [P, NR // P, HEADS])
        r_last = sb("r_last", [1, HEADS])
        minus_flip = sb("minus_flip", [P, P])
        minus_one = sb("minus_one", [1, 1])
        flipped = ctx.enter_context(nc.psum_tensor("rb_flipped", [P, 512], F32))
        last_ps = ctx.enter_context(nc.psum_tensor("rb_last_ps", [P, 512], F32))
        loaded = sem("loaded")
        zeroed = sem("zeroed")
        flip_ready = sem("flip_ready")
        flip_ps = sem("flip_ps")
        mid_ready = sem("mid_ready")
        ext_ready = sem("ext_ready")
        block = ctx.enter_context(nc.Block())

        @block.sync
        def _(sp):
            sp.dma_start(r_t[:], rel_bias[0:NR - 1, :].rearrange("(a p) h -> p a h", p=P)).then_inc(loaded, 16)
            sp.dma_start(r_last[:], rel_bias[NR - 1:NR, :]).then_inc(loaded, 16)
            sp.wait_ge(ext_ready, 2)

        @block.gpsimd
        def _(pool):
            nc.gpsimd.memset(minus_flip[:], 0.0).then_inc(zeroed, 1)
            nc.gpsimd.memset(minus_one[:], -1.0).then_inc(flip_ready, 1)
            pool.wait_ge(zeroed, 1)
            nc.gpsimd.affine_select(out=minus_flip[:], in_=minus_flip[:], compare_op=ALU.not_equal, fill=-1.0,
                                    base=-(P - 1), pattern=[[1, P]], channel_multiplier=1).then_inc(flip_ready, 1)

        @block.tensor
        def _(pe):
            pe.wait_ge(loaded, 32)
            pe.wait_ge(flip_ready, 2)
            for a in range(NR // P):
                at = (NR // P - 1 - a) * P
                nc.tensor.matmul(flipped[0:HEADS, at:at + P], r_t[:, a, :], minus_flip[:], start=True, stop=True)
            nc.tensor.matmul(last_ps[0:HEADS, 0:1], r_last[:], minus_one[:], start=True, stop=True)\
                .then_inc(flip_ps, 1)

        @block.vector
        def _(dve):
            dve.wait_ge(flip_ps, 1)
            nc.vector.tensor_copy(ext_sb[:, LO + 1:LO + NR], flipped[0:HEADS, 0:NR - 1]).then_inc(mid_ready, 1)
            nc.vector.tensor_copy(ext_sb[:, 0:LO + 1], last_ps[0:HEADS, 0:1].broadcast_to([HEADS, LO + 1]))\
                .then_inc(ext_ready, 1)
            dve.wait_ge(mid_ready, 1)
            nc.vector.tensor_copy(ext_sb[:, LO + NR:EXT],
                                  ext_sb[:, LO + NR - 1:LO + NR].broadcast_to([HEADS, EXT - LO - NR]))\
                .then_inc(ext_ready, 1)


def build_attention_b(nc, x_in, W_qkv, b_qkv_d, W_out, b_out, x_out, ext_d):
    N = TILES
    with ExitStack() as ctx:
        def sb(name, shape, dt=F32):
            return ctx.enter_context(nc.sbuf_tensor("ab_" + name, shape, dt))

        def pb(name):
            return ctx.enter_context(nc.psum_tensor("ab_" + name, [P, 512], F32))

        sems = []

        def sem(name):
            sems.append(nc.alloc_semaphore("ab_" + name))
            return sems[-1]

        VW = 32
        ident_r = sb("ident_r", [P, P], F32R)
        ident = ident_r[:].bitcast(F32)
        w_qkv = sb("w_qkv", [P, KD, 3 * D])
        w_o = sb("w_o", [P, KD, D])
        b_qkv = sb("b_qkv", [P, 3 * D])
        b_o = sb("b_o", [P, D])
        minus_half = sb("minus_half", [P, 1])
        toep = sb("toep", [P, HEADS, TOEP])
        x_t = sb("x_t", [P, 2, D])
        stats = sb("stats", [P, 6])
        mean_var = sb("mean_var", [P, 2, 2])
        rstd = sb("rstd", [P, 2])
        xn = sb("xn", [P, 2, D])
        xn_T = sb("xn_T", [P, 2, KD, P])
        qk = sb("qk", [P, 2 * D])
        parts = sb("parts", [P, 2, HEADS, 4, DH])
        q_T = sb("q_T", [P, 2, HEADS // 2, SEQ], F32R)
        k_T = sb("k_T", [P, 2, HEADS // 2, SEQ], F32R)
        v_t = sb("v_t", [P, 2, IB, HEADS, VW])
        neg_max = sb("neg_max", [P, 8])
        e_t = sb("e_t", [P, 8, SEQ])
        e_T = sb("e_T", [P, 2, 4, IB, P])
        o_sb = sb("o_sb", [P, 2, HEADS // 4, P])
        rec = sb("rec", [P, HEADS])
        o_t = sb("o_t", [P, 2, D])
        o_T = sb("o_T", [P, KD, P])
        x_p = sb("x_p", [P, 2, D])
        y_t = sb("y_t", [P, 2, D])
        S = [pb(f"s{i}") for i in range(3)]
        ET = [pb(f"et{i}") for i in range(2)]
        O = pb("o")
        M = [pb(f"m{i}") for i in range(2)]

        w_loaded = sem("w_loaded")
        toep_loaded = [sem(f"toep_loaded{q}") for q in range(4)]
        wq_scaled = sem("wq_scaled")
        ident_zeroed = sem("ident_zeroed")
        ident_ready = sem("ident_ready")
        v_cleared = sem("v_cleared")
        v_ones = sem("v_ones")
        x_loaded = [sem(f"x_loaded{p}") for p in range(2)]
        xp_loaded = [sem(f"xp_loaded{p}") for p in range(2)]
        stats_done = sem("stats_done")
        mv_done = sem("mv_done")
        pool_step = sem("pool_step")
        xn_ready = sem("xn_ready")
        xt_ps = sem("xt_ps")
        xn_T_ready = sem("xn_T_ready")
        qk_ps = sem("qk_ps")
        v_ps = sem("v_ps")
        qk_ready = sem("qk_ready")
        v_ready = sem("v_ready")
        hi_ready = sem("hi_ready")
        parts_ready = sem("parts_ready")
        t_ps = sem("t_ps")
        t_by_act = sem("t_by_act")
        t_by_dve = sem("t_by_dve")
        s_done = sem("s_done")
        max_done = sem("max_done")
        exp_done = sem("exp_done")
        et_ps = sem("et_ps")
        et_by_act = sem("et_by_act")
        et_by_dve = sem("et_by_dve")
        pv_done = sem("pv_done")
        o_copied = sem("o_copied")
        ot_ps = sem("ot_ps")
        rec_done = sem("rec_done")
        norm_done = sem("norm_done")
        oT_ps = sem("oT_ps")
        o_T_ready = sem("o_T_ready")
        wo_ps = sem("wo_ps")
        xb_ready = sem("xb_ready")
        y_ready = sem("y_ready")
        y_stored = [sem(f"y_stored{p}") for p in range(2)]
        block = ctx.enter_context(nc.Block())
        AHEAD = IB
        BODY = 2 * IB

        def run(eng, step):
            for k in range(BODY):
                step(k, k)
            with eng.Fori(1, N // BODY) as u:
                for k in range(BODY):
                    step(BODY * u + k, k)

        def has(i, back):
            return not isinstance(i, int) or i >= back

        LAG = 5
        PE_QK, PE_OUT, PE_XT, PE_WO, PE_OT, PE_V = 1, 3, 5, 6, 8, 10
        PE_T = {10: 0, 12: 1, 13: 2, 15: 3}
        PE_PV, ACT_O = 11, 12
        ACT_OUT, ACT_XT = 2, 3
        ACT_T = {9: 0, 12: 2, 14: 3}
        DVE_STATS, DVE_QK, DVE_Y, DVE_O, DVE_V, DVE_T1 = 1, 3, 7, 8, 10, 13

        def group_of(s, first):
            return (s - first) // 4 if (s - first) % 4 == 0 else None

        def in_prologue(j):
            return isinstance(j, int) and j < AHEAD

        def qk_of(j):
            return e_T[:, 0, 0, :, :].rearrange("p c t -> p (c t)") if in_prologue(j) and j % 2 else qk[:]

        def parts_of(j):
            lent = e_t[:, 0:4, :].rearrange("p (m a) (b x) -> p m (a b x)", m=2, x=DH)\
                .rearrange("p m (h c x) -> p m h c x", h=HEADS, c=4)
            return lent if in_prologue(j) and j % 2 else parts[:]

        def unsplit(j, m):
            return qk_of(j)[:, m * D:(m + 1) * D].rearrange("p (h x) -> p h x", x=DH).unsqueeze(1)\
                .broadcast_to([P, 2, HEADS, DH])

        def high_part(j, m):
            a = parts_of(j)
            return (a[:, 0, :, 0:2, :], a[:, 1, :, 0:4:2, :])[m].rearrange("p h a x -> p a h x")

        def low_part(j, m):
            a = parts_of(j)
            return (a[:, 0, :, 2:4, :], a[:, 1, :, 1:4:2, :])[m].rearrange("p h a x -> p a h x")

        def own(j, k):
            return 8 * (j - k % 2) + 16

        @block.sync
        def _(sp):
            def load_x(j, k):
                tile = j % N if isinstance(j, int) else sp.snap(j % N, min_val=0, max_val=N - 1)
                wait(sp, xn_ready, j - 1)
                sp.dma_start(x_t[:, k % 2, :], x_in[bass.ts(tile, P), :]).then_inc(x_loaded[k % 2], 16)

            def load_xp(i, k):
                wait(sp, y_ready, i - 1)
                sp.dma_start(x_p[:, k % 2, :], x_in[bass.ts(i, P), :]).then_inc(xp_loaded[k % 2], 16)

            def store_y(j, k):
                wait(sp, y_ready, j + 1)
                sp.dma_start(x_out[bass.ts(j, P), :], y_t[:, k % 2, :]).then_inc(y_stored[k % 2], 16)

            sp.dma_start(w_qkv[:], W_qkv.rearrange("(k p) n -> p k n", p=P)).then_inc(w_loaded, 16)
            sp.dma_start(b_qkv[:], b_qkv_d.partition_broadcast(P)).then_inc(w_loaded, 16)
            sp.dma_start(w_o[:], W_out.rearrange("(k p) n -> p k n", p=P)).then_inc(w_loaded, 16)
            sp.dma_start(b_o[:], b_out.partition_broadcast(P)).then_inc(w_loaded, 16)
            for j in range(3):
                load_x(j, j)
            skewed = ext_d[:, P - 1:P - 1 + P * (EXT - 1)].rearrange("h (p w) -> p h w", w=EXT - 1)
            for h in range(0, HEADS, 2):
                sp.dma_start(toep[:, h:h + 2, :], skewed[:, h:h + 2, 0:TOEP]).then_inc(toep_loaded[h // 4], 16)
                if h // 2 < 4:
                    load_x(3 + h // 2, 3 + h // 2)

            def step(i, k):
                load_x(i + AHEAD + 3, k + AHEAD + 3)
                if has(i, 1):
                    load_xp(i - 1, k + BODY - 1)
                if has(i, 3):
                    store_y(i - 3, k + BODY - 3)

            run(sp, step)
            load_xp(N - 1, N - 1)
            store_y(N - 3, N - 3)
            store_y(N - 2, N - 2)
            store_y(N - 1, N - 1)
            for p in range(2):
                sp.wait_ge(y_stored[p], 16 * (N // 2))

        @block.gpsimd
        def _(pool):
            unity = o_t[:, 0, 0:P]
            nc.gpsimd.memset(unity, 0.0).then_inc(ident_zeroed, 1)
            nc.gpsimd.memset(minus_half[:], -0.5).then_inc(ident_zeroed, 1)
            nc.gpsimd.memset(v_t[:], 0.0).then_inc(v_cleared, 1)
            pool.wait_ge(ident_zeroed, 2)
            nc.gpsimd.affine_select(out=unity, in_=unity, compare_op=ALU.not_equal, fill=1.0, base=0,
                                    pattern=[[-1, P]], channel_multiplier=1).then_inc(ident_ready, 1)
            pool.wait_ge(ident_ready, 1)
            nc.gpsimd.tensor_copy(ident_r[:], unity).then_inc(ident_ready, 1)
            pool.wait_ge(v_cleared, 1)
            nc.gpsimd.memset(v_t[:].rearrange("p b i h w -> p (b i h) w")[:, :, DH:DH + 1], 1.0).then_inc(v_ones, 1)

            def normalise(j, k):
                p = k % 2
                wait_apart(pool, mv_done, j + 1)
                nc.gpsimd.tensor_scalar(rstd[:, p:p + 1], mean_var[:, p, 1:2], EPS, None, ALU.add)\
                    .then_inc(pool_step, 1)
                wait(pool, pool_step, 2 * j + 1)
                nc.gpsimd.tensor_tensor(rstd[:, p:p + 1], rstd[:, p:p + 1], minus_half[:], ALU.pow)\
                    .then_inc(pool_step, 1)
                wait(pool, pool_step, 2 * j + 2)
                wait_apart(pool, xt_ps, j - 1)
                nc.gpsimd.tensor_scalar(xn[:, p, :], x_t[:, p, :], mean_var[:, p, 0:1], rstd[:, p:p + 1],
                                        ALU.subtract, ALU.mult).then_inc(xn_ready, 1)

            def split(j):
                wait(pool, qk_ready, j + 1)
                wait_apart(pool, t_ps, 4 * (j - 1) if in_prologue(j) else 4 * j)
                for m in range(2):
                    nc.gpsimd.tensor_scalar(high_part(j, m).bitcast(F32R), unsplit(j, m), 1.0, None, ALU.mult)\
                        .then_inc(hi_ready, 1)
                if not in_prologue(j):
                    for m in range(2):
                        wait(pool, hi_ready, 2 * j + 1 + m)
                        nc.gpsimd.tensor_tensor(low_part(j, m).bitcast(F32R), unsplit(j, m), high_part(j, m),
                                                ALU.subtract).then_inc(parts_ready, 1)

            def add_bias(i, k):
                wait(pool, xp_loaded[k % 2], own(i, k))
                nc.gpsimd.tensor_tensor(x_p[:, k % 2, :], x_p[:, k % 2, :], b_o[:], ALU.add).then_inc(xb_ready, 1)

            pool.wait_ge(w_loaded, 4 * 16)
            normalise(0, 0)
            for j in range(AHEAD):
                normalise(j + 1, j + 1)
                split(j)
            normalise(AHEAD + 1, AHEAD + 1)

            def step(i, k):
                split(i + AHEAD)
                if has(i, 2):
                    add_bias(i - 2, k + BODY - 2)
                normalise(i + AHEAD + 2, k + AHEAD + 2)

            run(pool, step)
            add_bias(N - 2, N - 2)
            add_bias(N - 1, N - 1)

        def t_out(n, k):
            dst = (q_T, k_T)[n // 2]
            at = k % IB * P
            return dst[:, k // IB % 2, n % 2 * 4:n % 2 * 4 + 4, at:at + P]

        T_BANK = [0, 1, 0, 1]
        OT = M[0]
        OUT_T, WO = [M[1][:, 0:D]] * 2

        def XT(j):
            return (S[0] if in_prologue(j) else M[0])[:, 0:D]

        def QK(j):
            return (S[1] if in_prologue(j) else M[0])[:]

        def V(j):
            return (S[2] if in_prologue(j) else M[1])[:, 0:D]

        def psum_heads(a):
            return a.rearrange("p (c t) -> p c t", c=4)

        @block.scalar
        def _(act):
            def copy_xn_T(j, k):
                wait(act, xt_ps, j + 1)
                wait(act, v_ps, j - 1)
                nc.scalar.activation(xn_T[:, k % 2, :, :], XT(j).rearrange("p (k t) -> p k t", k=KD), ACT.Copy)\
                    .then_inc(xn_T_ready, 1)

            def copy_t(j, k, n):
                wait(act, t_ps, 4 * j + n + 1)
                wait(act, s_done, 16 * (j - k % IB - IB))
                nc.scalar.activation(t_out(n, k), psum_heads(M[T_BANK[n]][:]), ACT.Copy).then_inc(t_by_act, 1)

            def exp(i, s):
                wait(act, max_done, 16 * i + s + 1)
                q = s % 8
                nc.scalar.activation(e_t[:, q, :], e_t[:, q, :], ACT.Exp, bias=neg_max[:, q:q + 1], scale=-1.0)\
                    .then_inc(exp_done, 1)

            def copy_et(i, s):
                g = s // 4
                wait(act, et_ps, 16 * i + s + 1)
                if s % 4 == 0:
                    wait(act, pv_done, 4 * i + g - 1)
                nc.scalar.activation(e_T[:, g % 2, s % 4, :, :], psum_heads(ET[0][:]), ACT.Copy).then_inc(et_by_act, 1)

            def copy_o(i, g, k):
                wait(act, pv_done, 4 * i + g + 1)
                if g % 4 == 0:
                    wait(act, ot_ps, i + g // 4 - 1)
                nc.scalar.activation(o_sb[:, (k + g // 4) % 2, g % 4, :], O[:, 0:P], ACT.Copy).then_inc(o_copied, 1)

            def copy_o_T(j):
                wait(act, oT_ps, j + 1)
                wait(act, wo_ps, j)
                nc.scalar.activation(o_T[:], OUT_T.rearrange("p (k t) -> p k t", k=KD), ACT.Copy)\
                    .then_inc(o_T_ready, 1)

            copy_xn_T(0, 0)
            for j in range(AHEAD):
                if j + 1 < AHEAD:
                    copy_xn_T(j + 1, j + 1)
                for n in (0, 2, 3):
                    copy_t(j, j, n)
            copy_xn_T(AHEAD, AHEAD)

            def step(i, k):
                for s in range(16):
                    if (s - LAG) % 2 == 0 and has(16 * i + s, LAG):
                        copy_et(i, s - LAG)
                    g = group_of(s, ACT_O)
                    if g is not None and has(4 * i + g, 0):
                        copy_o(i, g, k)
                    exp(i, s)
                    if s == ACT_OUT and has(i, 3):
                        copy_o_T(i - 3)
                    if s == ACT_XT:
                        copy_xn_T(i + AHEAD + 1, k + AHEAD + 1)
                    if s in ACT_T:
                        copy_t(i + AHEAD, k + AHEAD, ACT_T[s])

            run(act, step)
            copy_et(N, -4)
            copy_et(N, -2)
            for g in (-3, -2, -1):
                copy_o(N, g, N)
            for j in range(N - 3, N):
                copy_o_T(j)

        @block.vector
        def _(dve):
            def statistics(j, k):
                wait(dve, x_loaded[k % 2], own(j, k))
                wait(dve, mv_done, j)
                nc.vector.bn_stats(stats[:], x_t[:, k % 2, :]).then_inc(stats_done, 1)
                wait(dve, stats_done, j + 1)
                wait_apart(dve, xn_ready, j - 1)
                nc.vector.bn_aggr(mean_var[:, k % 2, :], stats[:]).then_inc(mv_done, 1)

            def add_qk(j):
                wait(dve, qk_ps, j + 1)
                wait(dve, parts_ready, 2 * (j - 1) if in_prologue(j) else 2 * j)
                nc.vector.tensor_tensor(qk_of(j), QK(j), b_qkv[:, 0:2 * D], ALU.add).then_inc(qk_ready, 1)

            def add_v(j, k):
                wait(dve, v_ps, j + 1)
                wait(dve, pv_done, 4 * (j - k % IB - IB))
                nc.vector.tensor_tensor(v_t[:, k // IB % 2, k % IB, :, 0:DH],
                                        V(j).rearrange("p (h x) -> p h x", x=DH),
                                        b_qkv[:, 2 * D:3 * D].rearrange("p (h x) -> p h x", x=DH), ALU.add)\
                    .then_inc(v_ready, 1)

            def copy_t(j, k, n):
                wait(dve, t_ps, 4 * j + n + 1)
                wait(dve, s_done, 16 * (j - k % IB - IB))
                nc.vector.tensor_copy(t_out(n, k), psum_heads(M[T_BANK[n]][:])).then_inc(t_by_dve, 1)

            def add_bias(i, k, s):
                n = 16 * i + s
                at = SEQ - P - k % IB * P
                wait(dve, s_done, n + 1)
                wait_apart(dve, et_ps, n - 7)
                nc.vector.tensor_tensor_reduce(out=e_t[:, s % 8, :], in0=S[(k * 16 + s) % 3][:],
                                               in1=toep[:, s, at:at + SEQ], scale=1.0, scalar=3.0e38, op0=ALU.add,
                                               op1=ALU.min, accum_out=neg_max[:, s % 8:s % 8 + 1])\
                    .then_inc(max_done, 1)

            def copy_et(i, s):
                g = s // 4
                wait(dve, et_ps, 16 * i + s + 1)
                if s % 4 == 1:
                    wait(dve, pv_done, 4 * i + g - 1)
                nc.vector.tensor_copy(e_T[:, g % 2, s % 4, :, :], psum_heads(ET[1][:])).then_inc(et_by_dve, 1)

            def divide(j, k):
                groups = OT[:].rearrange("p (h w) -> p h w", w=VW)
                wait(dve, ot_ps, j + 1)
                wait(dve, norm_done, j)
                nc.vector.reciprocal(rec[:], groups[:, :, DH]).then_inc(rec_done, 1)
                wait(dve, rec_done, j + 1)
                wait(dve, oT_ps, j - 1)
                nc.vector.tensor_tensor(o_t[:, k % 2, :].rearrange("p (h x) -> p h x", x=DH), groups[:, :, 0:DH],
                                        rec[:].unsqueeze(2).broadcast_to([P, HEADS, DH]), ALU.mult)\
                    .then_inc(norm_done, 1)

            def add_residual(j, k):
                wait(dve, wo_ps, j + 1)
                wait(dve, xb_ready, j + 1)
                wait(dve, y_stored[k % 2], own(j, k) - 16)
                nc.vector.tensor_tensor(y_t[:, k % 2, :], WO, x_p[:, k % 2, :], ALU.add)\
                    .then_inc(y_ready, 1)

            dve.wait_ge(w_loaded, 4 * 16)
            dve.wait_ge(v_ones, 1)
            nc.vector.tensor_scalar(w_qkv[:, :, 0:D], w_qkv[:, :, 0:D], -1.0 / DH ** 0.5, None, ALU.mult)\
                .then_inc(wq_scaled, 1)
            nc.vector.tensor_scalar(b_qkv[:, 0:D], b_qkv[:, 0:D], -1.0 / DH ** 0.5, None, ALU.mult)\
                .then_inc(wq_scaled, 1)
            dve.wait_ge(wq_scaled, 2)
            statistics(0, 0)
            for j in range(AHEAD + 1):
                statistics(j + 1, j + 1)
                if j > 0:
                    for m in range(2):
                        wait(dve, hi_ready, 2 * (j - 1) + m + 1)
                        nc.vector.tensor_tensor(low_part(j - 1, m).bitcast(F32R), unsplit(j - 1, m),
                                                high_part(j - 1, m), ALU.subtract).then_inc(parts_ready, 1)
                if j < AHEAD:
                    add_qk(j)
                    add_v(j, j)
                if j > 0:
                    copy_t(j - 1, j - 1, 1)

            def step(i, k):
                for s in range(16):
                    if isinstance(i, int) and i == 0 and s % 4 == 0:
                        dve.wait_ge(toep_loaded[s // 4], 2 * 16)
                    add_bias(i, k, s)
                    if (s - LAG) % 2 == 0 and has(16 * i + s, LAG + 1):
                        copy_et(i, s - LAG - 1)
                    if s == DVE_O and has(i, 2):
                        divide(i - 2, k)
                    if s == DVE_T1:
                        copy_t(i + AHEAD, k + AHEAD, 1)
                    if s == DVE_QK:
                        add_qk(i + AHEAD)
                    if s == DVE_V:
                        add_v(i + AHEAD, k + AHEAD)
                    if s == DVE_Y and has(i, 3):
                        add_residual(i - 3, k + BODY - 3)
                    if s == DVE_STATS:
                        statistics(i + AHEAD + 2, k + AHEAD + 2)

            run(dve, step)
            for s in (-5, -3, -1):
                copy_et(N, s)
            for j in (N - 2, N - 1):
                divide(j, j)
            for j in range(N - 3, N):
                add_residual(j, j)

        @block.tensor
        def _(pe):
            def transpose_x(j, k):
                wait(pe, xn_ready, j + 1)
                if in_prologue(j):
                    wait(pe, xn_T_ready, j)
                elif isinstance(j, int) and j == AHEAD:
                    wait(pe, t_by_act, 3 * j - 1)
                else:
                    wait(pe, qk_ready, j)
                for c in range(KD):
                    last = nc.tensor.transpose(XT(j)[:, c * P:(c + 1) * P], xn[:, k % 2, c * P:(c + 1) * P], ident[:])
                last.then_inc(xt_ps, 1)

            def project_qk(j, k):
                wait(pe, xn_T_ready, j + 1)
                if in_prologue(j):
                    wait(pe, qk_ready, j)
                else:
                    wait(pe, t_by_act, 3 * j - 1)
                for c in range(KD):
                    last = nc.tensor.matmul(QK(j), xn_T[:, k % 2, c, :], w_qkv[:, c, 0:2 * D],
                                            start=c == 0, stop=c == KD - 1)
                last.then_inc(qk_ps, 1)

            def project_v(j, k):
                if in_prologue(j):
                    wait(pe, v_ready, j)
                else:
                    wait(pe, t_by_act, 3 * j)
                wait(pe, y_ready, j - AHEAD - 2)
                for c in range(KD):
                    last = nc.tensor.matmul(V(j), xn_T[:, k % 2, c, :], w_qkv[:, c, 2 * D:3 * D],
                                            start=c == 0, stop=c == KD - 1)
                last.then_inc(v_ps, 1)

            def transpose_parts(j, n):
                wait(pe, parts_ready, 2 * (j + 1))
                if in_prologue(j) and n < 2:
                    wait(pe, t_by_act, 3 * j - 1 + n)
                elif n == 0:
                    wait(pe, qk_ready, j + 1)
                    if not isinstance(j, int) or j >= AHEAD:
                        wait(pe, xn_T_ready, j + 2)
                    wait(pe, norm_done, j - AHEAD - 1)
                elif n == 1:
                    wait(pe, v_ready, j + 1)
                elif n == 2:
                    wait(pe, t_by_act, 3 * j + 1)
                else:
                    wait(pe, t_by_dve, j + 1)
                kind, unit = (F32, ident) if in_prologue(j) and j % 2 else (F32R, ident_r[:])
                for c in range(4):
                    m = n % 2 * 4 + c
                    last = nc.tensor.transpose(M[T_BANK[n]][:, c * P:(c + 1) * P].bitcast(kind),
                                               parts_of(j)[:, n // 2, 2 * m:2 * m + 2, :, :]
                                               .rearrange("p h a x -> p (h a x)").bitcast(kind), unit)
                last.then_inc(t_ps, 1)

            def scores(i, k, s):
                n = 16 * i + s
                wait(pe, max_done, n - 1 if k == 0 and s < 2 else n - 2)
                if s == 0 and k % IB == 0:
                    wait(pe, t_by_act, 3 * (i + IB))
                    wait(pe, t_by_dve, i + IB)
                lo, at = s % 2 * 64, k % IB * P
                nc.tensor.matmul(S[(k * 16 + s) % 3][:], q_T[lo:lo + 64, k // IB % 2, s // 2, at:at + P],
                                 k_T[lo:lo + 64, k // IB % 2, s // 2, :], start=True, stop=True).then_inc(s_done, 1)

            def transpose_e(i, s):
                n = 16 * i + s
                wait(pe, exp_done, n + 1)
                wait(pe, et_by_dve if s % 2 else et_by_act, 8 * i + s // 2)
                for c in range(IB):
                    last = nc.tensor.transpose(ET[s % 2][:, c * P:(c + 1) * P], e_t[:, s % 8, c * P:(c + 1) * P],
                                               ident[:])
                last.then_inc(et_ps, 1)

            def values(group, gk):
                wait(pe, et_by_act, 2 * (group + 1))
                wait(pe, et_by_dve, 2 * (group + 1))
                wait(pe, o_copied, group)
                b = gk // (4 * IB) % 2
                for c in range(IB):
                    for q in range(4):
                        last = nc.tensor.matmul(O[q * VW:(q + 1) * VW, 0:P], v_t[:, b, c, gk % 4 * 4 + q, :],
                                                e_T[:, gk % 2, q, c, :], start=c == 0, stop=c == IB - 1)
                last.then_inc(pv_done, 1)

            def transpose_o(j, k):
                wait(pe, o_copied, 4 * (j + 1))
                for g in range(HEADS // 4):
                    last = nc.tensor.transpose(OT[:, g * P:(g + 1) * P], o_sb[:, k % 2, g, :], ident[:])
                last.then_inc(ot_ps, 1)

            def transpose_out(j, k):
                wait(pe, norm_done, j + 1)
                for c in range(KD):
                    last = nc.tensor.transpose(OUT_T[:, c * P:(c + 1) * P], o_t[:, k % 2, c * P:(c + 1) * P],
                                               ident[:])
                last.then_inc(oT_ps, 1)

            def output(j):
                wait(pe, o_T_ready, j + 1)
                for c in range(KD):
                    last = nc.tensor.matmul(WO, o_T[:, c, :], w_o[:, c, :], start=c == 0, stop=c == KD - 1)
                last.then_inc(wo_ps, 1)

            pe.wait_ge(ident_ready, 2)
            pe.wait_ge(wq_scaled, 2)
            for j in range(AHEAD + 1):
                if j < AHEAD:
                    transpose_x(j, j)
                    project_qk(j, j)
                    project_v(j, j)
                if j > 0:
                    for n in range(4):
                        transpose_parts(j - 1, n)
            transpose_x(AHEAD, AHEAD)
            pe.wait_ge(xn_T_ready, AHEAD)
            pe.wait_ge(qk_ready, AHEAD)
            pe.wait_ge(v_ready, AHEAD)

            def step(i, k):
                m = i + AHEAD
                for s in range(16):
                    scores(i, k, s)
                    if s == PE_QK:
                        project_qk(m, k + AHEAD)
                    if s == PE_OUT and has(i, 3):
                        wait(pe, t_by_act, 3 * m)
                        transpose_out(i - 3, k + BODY - 3)
                    if s == PE_WO and has(i, 3):
                        output(i - 3)
                    if s == PE_OT and has(i, 2):
                        wait(pe, xn_T_ready, m + 2)
                        transpose_o(i - 2, k)
                    if s == PE_V:
                        project_v(m, k + AHEAD)
                    if s in PE_T:
                        transpose_parts(m, PE_T[s])
                    if s == PE_XT:
                        transpose_x(m + 1, k + AHEAD + 1)
                    g = group_of(s, PE_PV)
                    if g is not None and has(4 * i + g, 0):
                        values(4 * i + g, 4 * (k + BODY) + g)
                    if has(16 * i + s, LAG):
                        transpose_e(i, s - LAG)

            run(pe, step)
            for s in range(-LAG, 0):
                transpose_e(N, s)
            for group in (4 * N - 2, 4 * N - 1):
                values(group, group)
            wait(pe, t_by_act, 3 * (N + AHEAD))
            for j in (N - 2, N - 1):
                wait(pe, norm_done, j)
                transpose_o(j, j)
            for j in range(N - 3, N):
                transpose_out(j, j)
                output(j)
                wait(pe, y_ready, j + 1)

    nc.clear_and_free_semaphores(sems)
    nc.all_engine_barrier()


I32 = mybir.dt.int32
U32 = mybir.dt.uint32

E = 8
TOP = 2
FF = 512
KF = FF // P
SLOT_TILES = TOP * TILES + E
ALL_TILES = TILES + SLOT_TILES
GT = 4
GROUPS = TILES // GT
ROW = D + 2


def build_ffn(nc, tag, x_in, Wg, Ws1, Ws3, Ws2, We1, We3, We2, x_out, rows_d):
    with ExitStack() as ctx:
        def sb(name, shape, dt=F32):
            return ctx.enter_context(nc.sbuf_tensor(tag + name, shape, dt))

        def sem(name):
            return ctx.enter_context(nc.semaphore(tag + name))

        ident = sb("ident", [P, P])
        w_up = sb("w_up", [P, E, KD, 2 * FF])
        w_down = sb("w_down", [P, E, KF, D])
        s_up = [sb(f"s_up_{part}", [P, KD, 2 * FF], F32R) for part in ("high", "low")]
        s_down = [sb(f"s_down_{part}", [P, KF, D], F32R) for part in ("high", "low")]
        xn_all = sb("xn_all", [P, TILES, D])
        logits = sb("logits", [P, TILES, E])
        slots = sb("slots", [P, TILES, TOP], U32)
        labels = sb("labels", [P, TILES, TOP, 2])
        quad_experts = sb("quad_experts", [1, SLOT_TILES // 4], I32)
        consts_ready = sem("consts_ready")
        w_loaded = sem("w_loaded")
        shared_loaded = sem("shared_loaded")

        with ExitStack() as c1:
            def sb1(name, shape, dt=F32):
                return c1.enter_context(nc.sbuf_tensor(tag + name, shape, dt))

            def sem1(name):
                return c1.enter_context(nc.semaphore(tag + name))

            w_g = sb1("w_g", [P, KD, E])
            s_up_whole = sb1("s_up_whole", [P, KD, 2 * FF])
            s_down_whole = sb1("s_down_whole", [P, KF, D])
            minus_half = sb1("minus_half", [P, GT])
            x_t = sb1("x_t", [P, 4, GT, D])
            stats = sb1("stats", [P, GT, 6])
            mean_var = sb1("mean_var", [P, 2, GT, 2])
            rstd = sb1("rstd", [P, 2, GT])
            xn = sb1("xn", [P, 2, GT, D])
            xn_T = sb1("xn_T", [P, 2, GT, KD, P])
            XT = [c1.enter_context(nc.psum_tensor(tag + f"xt{i}", [P, 512], F32)) for i in range(4)]
            GL = [c1.enter_context(nc.psum_tensor(tag + f"gl{i}", [P, 512], F32)) for i in range(2)]
            LT = [c1.enter_context(nc.psum_tensor(tag + f"lt{i}", [P, 512], F32)) for i in range(2)]
            gl_sb = sb1("gl_sb", [E, 2, GT * P])
            wg_loaded = sem1("wg_loaded")
            x_loaded = [sem1(f"x_loaded{r}") for r in range(4)]
            stats_done = sem1("stats_done")
            mv_done = sem1("mv_done")
            pool_step = sem1("pool_step")
            xn_ready = sem1("xn_ready")
            xn_kept = sem1("xn_kept")
            xt_ps = sem1("xt_ps")
            xn_T_ready = sem1("xn_T_ready")
            gl_ps = sem1("gl_ps")
            gl_copied = sem1("gl_copied")
            lt_ps = sem1("lt_ps")
            lt_copied = sem1("lt_copied")
            s_high_ready = sem1("s_high_ready")
            block = c1.enter_context(nc.Block())

            @block.sync
            def _(sp):
                sp.dma_start(w_g[:], Wg.rearrange("(k p) n -> p k n", p=P)).then_inc(wg_loaded, 16)

                def load_x(g, r):
                    wait(sp, xn_ready, g - 3)
                    sp.dma_start(x_t[:, r, :, :], x_in[bass.ts(g, GT * P), :].rearrange("(a p) n -> p a n", p=P))\
                        .then_inc(x_loaded[r], 16)

                for r in range(4):
                    load_x(r, r)
                def load_w(up, down, w1, w3, w2, loaded):
                    sp.dma_start(up[:, :, 0:FF], w1.rearrange("(k p) n -> p k n", p=P)).then_inc(loaded, 16)
                    sp.dma_start(up[:, :, FF:2 * FF], w3.rearrange("(k p) n -> p k n", p=P)).then_inc(loaded, 16)
                    sp.dma_start(down, w2.rearrange("(k p) n -> p k n", p=P)).then_inc(loaded, 16)

                load_w(s_up_whole[:], s_down_whole[:], Ws1, Ws3, Ws2, shared_loaded)
                with sp.Fori(1, GROUPS // 4) as m:
                    for r in range(4):
                        load_x(4 * m + r, r)
                for e in range(E):
                    load_w(w_up[:, e, :, :], w_down[:, e, :, :], We1[e], We3[e], We2[e], w_loaded)

            @block.gpsimd
            def _(pool):
                nc.gpsimd.memset(ident[:], 0.0).then_inc(consts_ready, 1)
                nc.gpsimd.memset(minus_half[:], -0.5).then_inc(consts_ready, 1)
                pool.wait_ge(consts_ready, 2)
                nc.gpsimd.affine_select(out=ident[:], in_=ident[:], compare_op=ALU.not_equal, fill=1.0, base=0,
                                        pattern=[[-1, P]], channel_multiplier=1).then_inc(consts_ready, 1)

                def step(g, p):
                    wait_apart(pool, mv_done, GT * g + GT)
                    nc.gpsimd.tensor_scalar(rstd[:, p, :], mean_var[:, p, :, 1], EPS, None, ALU.add)\
                        .then_inc(pool_step, 1)
                    wait(pool, pool_step, 2 * g + 1)
                    nc.gpsimd.tensor_tensor(rstd[:, p, :], rstd[:, p, :], minus_half[:], ALU.pow)\
                        .then_inc(pool_step, 1)

                step(0, 0)
                step(1, 1)
                with pool.Fori(1, GROUPS // 2) as h:
                    for p in range(2):
                        step(2 * h + p, p)

            @block.vector
            def _(dve):
                def mean_and_var(g, r):
                    p = r % 2
                    wait(dve, x_loaded[r], 4 * (g - r) + 16)
                    wait(dve, mv_done, GT * g)
                    for i in range(GT):
                        nc.vector.bn_stats(stats[:, i, :], x_t[:, r, i, :]).then_inc(stats_done, 1)
                    wait_apart(dve, stats_done, GT * g + GT)
                    for i in range(GT):
                        nc.vector.bn_aggr(mean_var[:, p, i, :], stats[:, i, :]).then_inc(mv_done, 1)

                def normalise(g, r):
                    p = r % 2
                    wait_apart(dve, mv_done, GT * g + GT)
                    wait(dve, pool_step, 2 * g + 2)
                    wait(dve, xn_kept, g - 1)
                    wait(dve, xt_ps, 2 * g - 2)
                    for i in range(GT):
                        last = nc.vector.tensor_scalar(xn[:, p, i, :], x_t[:, r, i, :], mean_var[:, p, i, 0:1],
                                                       rstd[:, p, i:i + 1], ALU.subtract, ALU.mult)
                    last.then_inc(xn_ready, 1)

                def copy_logits(g, r):
                    wait(dve, lt_ps, g + 1)
                    nc.vector.tensor_copy(logits[:, bass.ds(GT * g, GT), :],
                                          LT[r % 2][:, 0:GT * E].rearrange("p (a e) -> p a e", a=GT))\
                        .then_inc(lt_copied, 1)

                mean_and_var(0, 0)
                for r in range(1, 4):
                    mean_and_var(r, r)
                    normalise(r - 1, r - 1)
                with dve.Fori(1, GROUPS // 4) as m:
                    for r in range(4):
                        mean_and_var(4 * m + r, r)
                        normalise(4 * m + r - 1, (r - 1) % 4)
                        copy_logits(4 * m + r - 4, r)
                normalise(GROUPS - 1, 3)
                for n, (whole, parts) in enumerate(((s_up_whole, s_up), (s_down_whole, s_down))):
                    wait(dve, s_high_ready, n + 1)
                    nc.vector.tensor_tensor(parts[1][:], whole[:], parts[0][:].bitcast(F32), ALU.subtract)
                for r in range(4):
                    copy_logits(GROUPS - 4 + r, r)


            @block.scalar
            def _(act):
                def step(g, p, start=False):
                    wait(act, xn_ready, g + 1)
                    nc.scalar.activation(xn_all[:, bass.ds(GT * g, GT), :], xn[:, p, :, :], ACT.Copy)\
                        .then_inc(xn_kept, 1)
                    for q in range(2):
                        wait(act, xt_ps, 2 * g + q + 1)
                        wait(act, gl_ps, g - 1)
                        nc.scalar.activation(xn_T[:, p, 2 * q:2 * q + 2, :, :],
                                             XT[2 * p + q][:].rearrange("p (a k t) -> p a k t", a=2, k=KD), ACT.Copy)\
                            .then_inc(xn_T_ready, 1)
                    if not start:
                        copy_gl(g - 1, 1 - p)

                def copy_gl(g, p):
                    wait(act, gl_ps, g + 1)
                    wait(act, lt_ps, g - 1)
                    nc.scalar.activation(gl_sb[:, p, :], GL[p][0:E, :], ACT.Copy).then_inc(gl_copied, 1)

                step(0, 0, start=True)
                step(1, 1)
                with act.Fori(1, GROUPS // 2 - 1) as h:
                    for p in range(2):
                        step(2 * h + p, p)
                act.wait_ge(shared_loaded, 3 * 16)
                for whole, parts in ((s_up_whole, s_up), (s_down_whole, s_down)):
                    nc.scalar.activation(parts[0][:], whole[:], ACT.Copy).then_inc(s_high_ready, 1)
                for p in range(2):
                    step(GROUPS - 2 + p, p)
                copy_gl(GROUPS - 1, 1)

            @block.tensor
            def _(pe):
                def transpose_xn(g, p):
                    wait(pe, xn_ready, g + 1)
                    for q in range(2):
                        wait(pe, xn_T_ready, 2 * g + q - 3)
                        for i in range(2):
                            for k in range(KD):
                                last = nc.tensor.transpose(XT[2 * p + q][:, (i * KD + k) * P:(i * KD + k + 1) * P],
                                                           xn[:, p, 2 * q + i, k * P:(k + 1) * P], ident[:])
                        last.then_inc(xt_ps, 1)

                def gate_logits(g, p):
                    wait(pe, xn_T_ready, 2 * g + 2)
                    wait(pe, gl_copied, g - 1)
                    for k in range(KD):
                        last = nc.tensor.matmul(GL[p][0:E, :], w_g[:, k, :], xn_T[:, p, :, k, :],
                                                start=k == 0, stop=k == KD - 1)
                    last.then_inc(gl_ps, 1)

                def turn_logits(g, p):
                    wait(pe, gl_copied, g + 1)
                    wait_apart(pe, lt_copied, g - 1)
                    for i in range(GT):
                        last = nc.tensor.transpose(LT[p][:, i * E:(i + 1) * E], gl_sb[:, p, i * P:(i + 1) * P],
                                                   ident[0:E, 0:E])
                    last.then_inc(lt_ps, 1)

                pe.wait_ge(consts_ready, 3)
                pe.wait_ge(wg_loaded, 16)
                transpose_xn(0, 0)
                transpose_xn(1, 1)
                gate_logits(0, 0)
                transpose_xn(2, 0)
                gate_logits(1, 1)
                turn_logits(0, 0)
                transpose_xn(3, 1)
                gate_logits(2, 0)
                turn_logits(1, 1)
                with pe.Fori(2, GROUPS // 2) as h:
                    for p in range(2):
                        transpose_xn(2 * h + p, p)
                        gate_logits(2 * h + p - 1, 1 - p)
                        turn_logits(2 * h + p - 2, p)
                gate_logits(GROUPS - 1, 1)
                for p in range(2):
                    turn_logits(GROUPS - 2 + p, p)

        with ExitStack() as c2:
            def sb2(name, shape, dt=F32):
                return c2.enter_context(nc.sbuf_tensor(tag + name, shape, dt))

            def sem2(name):
                return c2.enter_context(nc.semaphore(tag + name))

            def pb2(name):
                return c2.enter_context(nc.psum_tensor(tag + name, [P, 512], F32))

            below = sb2("below", [P, P])
            ones = sb2("ones", [P, P])
            rank8 = sb2("rank8", [P, E])
            rank8_i = sb2("rank8_i", [P, E], I32)
            tile_no = sb2("tile_no", [1, SLOT_TILES])
            tile_no_i = sb2("tile_no_i", [1, SLOT_TILES], I32)
            gates = sb2("gates", [P, TILES, E])
            top = sb2("top", [P, TOP, TILES])
            pick = sb2("pick", [P, TILES, E])
            first = sb2("first", [P, TILES])
            hot = sb2("hot", [P, TOP, TILES, E])
            mask = sb2("mask", [P, TILES, E])
            total = sb2("total", [P, 2, TILES, E])
            ends = sb2("ends", [P, 2, E])
            n_tiles = sb2("n_tiles", [P, E])
            n_int = sb2("n_int", [P, E], I32)
            slot = sb2("slot", [P, TILES, E])
            picked = sb2("picked", [P, TILES, E])
            slot_f = sb2("slot_f", [P, TOP, TILES])
            tile_ge = sb2("tile_ge", [1, SLOT_TILES, E - 1])
            tile_e_f = sb2("tile_e_f", [1, 4 + SLOT_TILES])
            quad_f = sb2("quad_f", [1, SLOT_TILES // 4])
            token_no = sb2("token_no", [P, TILES], I32)
            idx = sb2("idx", [P, 4, TOP], U32)
            idx_add = sb2("idx_add", [P, 2, 1], U32)
            x_r = sb2("x_r", [P, 2, D])
            x_t = sb2("x_t2", [P, 4, TOP, ROW])
            x_T = sb2("x_T", [P, 2, KD, P])
            x_T_parts = [sb2(f"x_T_{part}", [P, 2, KD, P], F32R) for part in ("high", "low")]
            gate = sb2("gate", [P, 2, FF])
            hid = sb2("hid", [P, 2, FF])
            hid_T = sb2("hid_T", [P, 2, KF, P])
            hid_T_parts = [sb2(f"hid_T_{part}", [P, 2, KF, P], F32R) for part in ("high", "low")]
            y_t = sb2("y_t", [P, 2, D])
            A = [pb2(f"a{i}") for i in range(2)]
            B = [pb2(f"b{i}") for i in range(2)]
            X = pb2("x")
            H = pb2("h")
            Y = [pb2(f"y{i}") for i in range(2)]

            route_consts = sem2("route_consts")
            gates_ready = sem2("gates_ready")
            chain = sem2("chain")
            mask_ready = sem2("mask_ready")
            counts_ps = sem2("counts_ps")
            routed = sem2("routed")
            idx_ready = sem2("idx_ready")
            row_copied = sem2("row_copied")
            scattered = [sem2(f"scattered{r}") for r in range(4)]
            x_loaded = [sem2(f"x_loaded2{r}") for r in range(4)]
            x_ps = sem2("x_ps")
            x_T_ready = sem2("x_T_ready")
            x_low_ready = sem2("x_low_ready")
            hid_low_ready = sem2("hid_low_ready")
            a_ps = sem2("a_ps")
            b_ps = sem2("b_ps")
            gate_ready = sem2("gate_ready")
            hid_ready = sem2("hid_ready")
            h_ps = sem2("h_ps")
            hid_T_ready = sem2("hid_T_ready")
            y_ps = sem2("y_ps")
            y_ready = sem2("y_ready")
            x_r_loaded = [sem2(f"x_r_loaded{p}") for p in range(2)]
            x_r_stored = [sem2(f"x_r_stored{p}") for p in range(2)]
            spare_stored = sem2("spare_stored")
            labelled = sem2("labelled")
            idx_add_ready = sem2("idx_add_ready")
            added = sem2("added")
            block = c2.enter_context(nc.Block())
            PAIRS = ALL_TILES // 2
            QUADS = ALL_TILES // 4

            @block.sync
            def _(sp):
                def load_residual(t, p):
                    wait(sp, x_r_stored[p], 8 * (t - p))
                    sp.dma_start(x_r[:, p, :], x_in[bass.ts(t, P), :]).then_inc(x_r_loaded[p], 16)

                def store_sum(t, p):
                    wait(sp, y_ready, t + 1)
                    sp.dma_start(x_out[bass.ts(t, P), :], x_r[:, p, :]).then_inc(x_r_stored[p], 16)

                def load_x(t, r):
                    fixed = isinstance(t, int)
                    slot_tile = t - TILES if fixed else sp.snap(t - TILES)
                    passed = t - 3 if fixed else sp.snap(t - 3)
                    slots_passed = slot_tile - 3 if fixed else sp.snap(t - TILES - 3)
                    wait_apart(sp, idx_add_ready, slots_passed)
                    wait_apart(sp, x_ps, passed)
                    if not fixed:
                        wait_apart(sp, y_ready, passed)
                    sp.dma_start(x_t[:, r, 0, :], rows_d[bass.ts(slot_tile, P), :]).then_inc(x_loaded[r], 16)

                load_residual(0, 0)
                load_residual(1, 1)
                store_sum(0, 0)
                sp.dma_start(x_out[T:T + P, :], x_r[:, 0, :]).then_inc(spare_stored, 16)
                sp.wait_ge(spare_stored, 16)
                load_residual(2, 0)
                store_sum(1, 1)
                load_residual(3, 1)
                with sp.Fori(2, TILES // 2) as h:
                    for p in range(2):
                        store_sum(2 * h + p - 2, p)
                        load_residual(2 * h + p, p)
                for r in range(4):
                    sp.wait_ge(scattered[r], 16 * TOP * (TILES // 4))
                for r in range(4):
                    load_x(TILES + r, r)
                store_sum(TILES - 2, 0)
                store_sum(TILES - 1, 1)
                with sp.Fori(TILES // 4 + 1, QUADS) as m:
                    for r in range(4):
                        load_x(4 * m + r, r)

            @block.gpsimd
            def _(pool):
                nc.gpsimd.memset(ones[:], 1.0).then_inc(route_consts, 1)
                nc.gpsimd.memset(below[:], 1.0).then_inc(route_consts, 1)
                nc.gpsimd.iota(rank8_i[:], pattern=[[-1, E]], base=E, channel_multiplier=0).then_inc(route_consts, 1)
                nc.gpsimd.iota(tile_no_i[:], pattern=[[1, SLOT_TILES]], base=0, channel_multiplier=0)\
                    .then_inc(route_consts, 1)
                nc.gpsimd.iota(token_no[:], pattern=[[P, TILES]], base=0, channel_multiplier=1)\
                    .then_inc(route_consts, 1)
                pool.wait_ge(route_consts, 5)
                nc.gpsimd.affine_select(out=below[:], in_=below[:], compare_op=ALU.is_gt, fill=0.0, base=0,
                                        pattern=[[1, P]], channel_multiplier=-1).then_inc(route_consts, 1)
                nc.gpsimd.tensor_copy(rank8[:], rank8_i[:]).then_inc(route_consts, 1)
                nc.gpsimd.tensor_copy(tile_no[:], tile_no_i[:]).then_inc(route_consts, 1)
                nc.gpsimd.tensor_copy(labels[:, :, :, 0], token_no[:].unsqueeze(2).broadcast_to([P, TILES, TOP]))\
                    .then_inc(route_consts, 1)

                def copy_row(t, r):
                    wait(pool, x_ps, t - 3)
                    wait(pool, scattered[r], 4 * TOP * (t - r))
                    nc.gpsimd.tensor_copy(x_t[:, r, :, 0:D], xn_all[:, bass.ds(t, 1), :].broadcast_to([P, TOP, D]))\
                        .then_inc(row_copied, 1)

                def scatter(t, r):
                    wait(pool, scattered[r], 4 * TOP * (t - r))
                    nc.gpsimd.tensor_copy(x_t[:, r, :, D:ROW], labels[:, bass.ds(t, 1), :, :]
                                          .rearrange("p a k n -> p (a k) n")).then_inc(labelled, 1)
                    nc.gpsimd.tensor_copy(idx[:, r, :], slots[:, t, :]).then_inc(idx_ready, 1)
                    wait(pool, row_copied, t + 1)
                    wait(pool, labelled, t + 1)
                    wait_apart(pool, idx_ready, t + 1)
                    for k in range(TOP):
                        pool.indirect_dma_start(out=rows_d[:, :],
                                                out_offset=bass.IndirectOffsetOnAxis(ap=idx[:, r, k:k + 1], axis=0),
                                                in_=x_t[:, r, k, :], in_offset=None).then_inc(scattered[r], 16)

                for r in range(4):
                    copy_row(r, r)
                pool.wait_ge(routed, 1)
                for r in range(4):
                    scatter(r, r)
                with pool.Fori(1, TILES // 4) as m:
                    for r in range(4):
                        copy_row(4 * m + r, r)
                        scatter(4 * m + r, r)
                for r in range(4):
                    pool.wait_ge(scattered[r], 16 * TOP * (TILES // 4))

                def add_y(t, r):
                    wait_apart(pool, x_loaded[r], 4 * (t - TILES - r) + 16)
                    nc.gpsimd.tensor_copy(idx_add[:, r % 2, :], x_t[:, r, 0, D:D + 1]).then_inc(idx_add_ready, 1)
                    wait(pool, idx_add_ready, t - TILES + 1)
                    wait(pool, y_ready, t + 1)
                    wait_apart(pool, added, 16 * (t - TILES))
                    pool.indirect_dma_start(out=x_out[:, :], in_=y_t[:, r % 2, :], in_offset=None, compute_op=ALU.add,
                                            out_offset=bass.IndirectOffsetOnAxis(ap=idx_add[:, r % 2, :], axis=0))\
                        .then_inc(added, 16)

                for p in range(2):
                    pool.wait_ge(x_r_stored[p], 16 * (TILES // 2))
                pool.wait_ge(spare_stored, 16)
                for r in range(4):
                    add_y(TILES + r, r)
                with pool.Fori(TILES // 4 + 1, QUADS) as m:
                    for r in range(4):
                        add_y(4 * m + r, r)
                pool.wait_ge(added, 16 * SLOT_TILES)

            @block.scalar
            def _(act):
                nc.scalar.activation(gates[:], logits[:], ACT.Sigmoid).then_inc(gates_ready, 1)

                def copy_x_T(t, p, shared):
                    wait(act, x_ps, t + 1)
                    wait(act, b_ps, t - 1)
                    out = x_T_parts[0] if shared else x_T
                    nc.scalar.activation(out[:, p, :, :], X[:, 0:D].rearrange("p (k t) -> p k t", k=KD), ACT.Copy)\
                        .then_inc(x_T_ready, 1)

                def silu(t, p):
                    wait(act, a_ps, t + 1)
                    wait(act, hid_ready, t - 1)
                    nc.scalar.activation(gate[:, p, :], A[p][:], ACT.Silu).then_inc(gate_ready, 1)

                def copy_hid_T(t, p, shared):
                    wait(act, h_ps, t + 1)
                    wait(act, y_ps, t - 1)
                    out = hid_T_parts[0] if shared else hid_T
                    nc.scalar.activation(out[:, p, :, :], H[:].rearrange("p (k t) -> p k t", k=KF), ACT.Copy)\
                        .then_inc(hid_T_ready, 1)

                def step(t, p, before=True, after=True):
                    silu(t, p)
                    if before is not None:
                        copy_hid_T(t - 1, 1 - p, before)
                    if after is not None:
                        copy_x_T(t + 1, 1 - p, after)

                copy_x_T(0, 0, True)
                step(0, 0, before=None)
                step(1, 1)
                with act.Fori(1, TILES // 2 - 1) as h:
                    step(2 * h, 0)
                    step(2 * h + 1, 1)
                step(TILES - 2, 0)
                step(TILES - 1, 1, after=False)
                step(TILES, 0, after=False)
                step(TILES + 1, 1, False, False)
                with act.Fori(TILES // 2 + 1, PAIRS - 1) as h:
                    step(2 * h, 0, False, False)
                    step(2 * h + 1, 1, False, False)
                step(ALL_TILES - 2, 0, False, False)
                step(ALL_TILES - 1, 1, False, None)
                copy_hid_T(ALL_TILES - 1, 1, False)

            @block.vector
            def _(dve):
                links = [0]

                def link(instruction):
                    links[0] += 1
                    instruction.then_inc(chain, 1)
                    dve.wait_ge(chain, links[0])

                def over_experts(a):
                    return a.unsqueeze(2).broadcast_to([P, TILES, E])

                def x_low(t, p):
                    wait(dve, x_T_ready, t + 1)
                    wait(dve, b_ps, t - 1)
                    nc.vector.tensor_tensor(x_T_parts[1][:, p, :, :], X[:, 0:D].rearrange("p (k t) -> p k t", k=KD),
                                            x_T_parts[0][:, p, :, :].bitcast(F32), ALU.subtract)\
                        .then_inc(x_low_ready, 1)

                dve.wait_ge(gates_ready, 1)
                dve.wait_ge(route_consts, 9)
                for k in range(TOP):
                    link(nc.vector.tensor_reduce(top[:, k, :], gates[:], AX.X, ALU.max))
                    link(nc.vector.tensor_tensor(pick[:], gates[:], over_experts(top[:, k, :]), ALU.is_equal))
                    link(nc.vector.tensor_tensor(pick[:], pick[:], rank8[:].unsqueeze(1).broadcast_to([P, TILES, E]),
                                                 ALU.mult))
                    link(nc.vector.tensor_reduce(first[:], pick[:], AX.X, ALU.max))
                    link(nc.vector.tensor_tensor(hot[:, k, :, :], pick[:], over_experts(first[:]), ALU.is_equal))
                    if k + 1 < TOP:
                        link(nc.vector.scalar_tensor_tensor(gates[:], hot[:, k, :, :], -2.0, gates[:], ALU.mult,
                                                            ALU.add))
                        x_low(0, 0)
                nc.vector.tensor_tensor(mask[:], hot[:, 0, :, :], hot[:, 1, :, :], ALU.add).then_inc(mask_ready, 1)
                link(nc.vector.tensor_tensor(first[:], top[:, 0, :], top[:, 1, :], ALU.add))
                link(nc.vector.reciprocal(first[:], first[:]))
                for k in range(TOP):
                    link(nc.vector.scalar_tensor_tensor(labels[:, :, k, 1], top[:, k, :], 1.0 / (1 + TOP), first[:],
                                                        ALU.mult, ALU.mult))
                x_low(1, 1)
                dve.wait_ge(counts_ps, 1)
                within, of_tile = Y
                link(nc.vector.tensor_copy(total[:, 0, :, :], of_tile[:, 0:TILES * E].rearrange("p (t e) -> p t e", e=E)))
                at, d = 0, 1
                while d < TILES:
                    link(nc.vector.tensor_copy(total[:, 1 - at, 0:d, :], total[:, at, 0:d, :]))
                    link(nc.vector.tensor_tensor(total[:, 1 - at, d:TILES, :], total[:, at, d:TILES, :],
                                                 total[:, at, 0:TILES - d, :], ALU.add))
                    at, d = 1 - at, 2 * d
                link(nc.vector.tensor_scalar(n_tiles[:], total[:, at, TILES - 1, :], float(P - 1), None, ALU.add))
                link(nc.vector.tensor_copy(n_int[:], n_tiles[:]))
                link(nc.vector.tensor_scalar(n_int[:], n_int[:], P.bit_length() - 1, None, ALU.arith_shift_right))
                link(nc.vector.tensor_copy(n_tiles[:], n_int[:]))
                link(nc.vector.tensor_copy(ends[:, 0, :], n_tiles[:]))
                be, d = 0, 1
                while d < E:
                    link(nc.vector.tensor_copy(ends[:, 1 - be, 0:d], ends[:, be, 0:d]))
                    link(nc.vector.tensor_tensor(ends[:, 1 - be, d:E], ends[:, be, d:E], ends[:, be, 0:E - d], ALU.add))
                    be, d = 1 - be, 2 * d
                link(nc.vector.tensor_tensor(n_tiles[:], ends[:, be, :], n_tiles[:], ALU.subtract))
                link(nc.vector.tensor_scalar(n_tiles[:], n_tiles[:], float(P), None, ALU.mult))
                link(nc.vector.tensor_tensor(slot[:], total[:, at, :, :],
                                             of_tile[:, 0:TILES * E].rearrange("p (t e) -> p t e", e=E), ALU.subtract))
                link(nc.vector.tensor_tensor(slot[:], slot[:],
                                             within[:, 0:TILES * E].rearrange("p (t e) -> p t e", e=E), ALU.add))
                link(nc.vector.tensor_tensor(slot[:], slot[:], n_tiles[:].unsqueeze(1).broadcast_to([P, TILES, E]),
                                             ALU.add))
                for k in range(TOP):
                    link(nc.vector.tensor_tensor(picked[:], slot[:], hot[:, k, :, :], ALU.mult))
                    link(nc.vector.tensor_reduce(slot_f[:, k, :], picked[:], AX.X, ALU.add))
                    link(nc.vector.tensor_copy(slots[:, :, k], slot_f[:, k, :]))
                link(nc.vector.tensor_tensor(tile_ge[:], tile_no[:].unsqueeze(2).broadcast_to([1, SLOT_TILES, E - 1]),
                                             ends[0:1, be, 0:E - 1].unsqueeze(1)
                                             .broadcast_to([1, SLOT_TILES, E - 1]), ALU.is_ge))
                link(nc.vector.tensor_reduce(tile_e_f[:, 1:1 + SLOT_TILES], tile_ge[:], AX.X, ALU.add))
                link(nc.vector.memset(tile_e_f[:, 0:1], 0.0))
                link(nc.vector.tensor_copy(quad_f[:], tile_e_f[:, 4:4 + SLOT_TILES:4]))
                for i in range(3, -1, -1):
                    link(nc.vector.scalar_tensor_tensor(quad_f[:], quad_f[:], float(E), tile_e_f[:, i:i + SLOT_TILES - 3:4],
                                                        ALU.mult, ALU.add))
                nc.vector.tensor_copy(quad_experts[:], quad_f[:]).then_inc(routed, 1)

                def gate_by_up(t, p):
                    wait(dve, gate_ready, t + 1)
                    wait(dve, b_ps, t + 1)
                    wait(dve, h_ps, t - 1)
                    nc.vector.tensor_tensor(hid[:, p, :], gate[:, p, :], B[p][:], ALU.mult).then_inc(hid_ready, 1)

                def weigh_y(t, r):
                    wait(dve, y_ps, t + 1)
                    wait(dve, added, 16 * (t - TILES - 1))
                    nc.vector.tensor_scalar(y_t[:, r % 2, :], Y[r % 2][:, 0:D], x_t[:, r, 0, D + 1:ROW], None, ALU.mult)\
                        .then_inc(y_ready, 1)

                def add_residual(t, r):
                    p = r % 2
                    wait(dve, y_ps, t + 1)
                    wait(dve, x_r_loaded[p], 8 * (t - p) + 16)
                    nc.vector.scalar_tensor_tensor(x_r[:, p, :], Y[p][:, 0:D], 1.0 / (1 + TOP), x_r[:, p, :],
                                                   ALU.mult, ALU.add).then_inc(y_ready, 1)

                def hid_low(t, p):
                    wait(dve, hid_T_ready, t + 1)
                    wait(dve, y_ps, t - 1)
                    nc.vector.tensor_tensor(hid_T_parts[1][:, p, :, :], H[:].rearrange("p (k t) -> p k t", k=KF),
                                            hid_T_parts[0][:, p, :, :].bitcast(F32), ALU.subtract)\
                        .then_inc(hid_low_ready, 1)

                def shared_step(t, r, start=False, end=False):
                    p = r % 2
                    if not start:
                        hid_low(t - 1, 1 - p)
                    gate_by_up(t, p)
                    if not end and not start:
                        x_low(t + 1, 1 - p)
                    if not start:
                        add_residual(t - 1, (r - 1) % 4)

                for r in range(4):
                    shared_step(r, r, start=r == 0)
                with dve.Fori(1, TILES // 4 - 1) as m:
                    for r in range(4):
                        shared_step(4 * m + r, r)
                for r in range(4):
                    shared_step(TILES - 4 + r, r, end=r == 3)
                shared_step(TILES, 0, end=True)
                gate_by_up(TILES + 1, 1)
                for r in range(4):
                    weigh_y(TILES + r, r)
                    gate_by_up(TILES + r + 2, r % 2)
                with dve.Fori(TILES // 4 + 1, QUADS - 1) as m:
                    for r in range(4):
                        weigh_y(4 * m + r, r)
                        gate_by_up(4 * m + r + 2, r % 2)
                for r in range(4):
                    weigh_y(ALL_TILES - 4 + r, r)
                    if r < 2:
                        gate_by_up(ALL_TILES - 2 + r, r)

            @block.tensor
            def _(pe):
                pe.wait_ge(route_consts, 9)
                def transpose_x(t, r, shared):
                    wait(pe, x_T_ready, t)
                    if isinstance(t, int):
                        wait(pe, x_low_ready, min(t, TILES))
                    elif shared:
                        wait(pe, x_low_ready, t)
                    if shared:
                        wait(pe, row_copied, t + 1)
                    else:
                        wait(pe, x_loaded[r], 4 * (t - TILES - r) + 16)
                    for k in range(KD):
                        last = nc.tensor.transpose(X[:, k * P:(k + 1) * P], x_t[:, r, 0, k * P:(k + 1) * P], ident[:])
                    last.then_inc(x_ps, 1)

                PASSES = ((0, 0), (0, 1), (1, 0))

                def up(t, p, e, out, col, done):
                    if e is None:
                        for values_part, w_part in PASSES:
                            if values_part:
                                wait(pe, x_low_ready, t + 1)
                            for k in range(KD):
                                last = nc.tensor.matmul(out[p][:], x_T_parts[values_part][:, p, k, :],
                                                        s_up[w_part][:, k, col:col + FF],
                                                        start=values_part + w_part + k == 0,
                                                        stop=values_part == 1 and k == KD - 1)
                    else:
                        for k in range(KD):
                            last = nc.tensor.matmul(out[p][:], x_T[:, p, k, :], w_up[:, e, k, col:col + FF],
                                                    start=k == 0, stop=k == KD - 1)
                    last.then_inc(done, 1)

                def transpose_hid(t, p):
                    wait(pe, hid_ready, t + 1)
                    wait(pe, hid_T_ready, t)
                    for k in range(KF):
                        last = nc.tensor.transpose(H[:, k * P:(k + 1) * P], hid[:, p, k * P:(k + 1) * P], ident[:])
                    last.then_inc(h_ps, 1)

                def down(t, p, e):
                    wait(pe, hid_T_ready, t + 1)
                    wait(pe, y_ready, t - 1)
                    if e is None:
                        for values_part, w_part in PASSES:
                            if values_part:
                                wait(pe, hid_low_ready, t + 1)
                            for k in range(KF):
                                last = nc.tensor.matmul(Y[p][:, 0:D], hid_T_parts[values_part][:, p, k, :],
                                                        s_down[w_part][:, k, :], start=values_part + w_part + k == 0,
                                                        stop=values_part == 1 and k == KF - 1)
                    else:
                        for k in range(KF):
                            last = nc.tensor.matmul(Y[p][:, 0:D], hid_T[:, p, k, :], w_down[:, e, k, :],
                                                    start=k == 0, stop=k == KF - 1)
                    last.then_inc(y_ps, 1)

                def step(t, r, e, e_before, start=False, end=False, next_shared=False):
                    p = r % 2
                    wait(pe, x_T_ready, t + 1)
                    wait(pe, hid_ready, t - 1)
                    up(t, p, e, A, 0, a_ps)
                    if not start:
                        transpose_hid(t - 1, 1 - p)
                    up(t, p, e, B, FF, b_ps)
                    if not end:
                        transpose_x(t + 1, (r + 1) % 4, next_shared)
                    if not start:
                        down(t - 1, 1 - p, e_before)

                def quad(m, start=False, end=False):
                    code = pe.value_load(quad_experts[0:1, bass.ds(m - TILES // 4, 1)], min_val=0, max_val=E ** 5 - 1)
                    e = [(code >> (3 * i)) & (E - 1) for i in range(5)]
                    if start:
                        e[0] = None
                    for r in range(4):
                        step(4 * m + r, r, e[r + 1], e[r], end=end and r == 3)
                    return e[4]

                transpose_x(0, 0, True)
                step(0, 0, None, None, start=True, next_shared=True)
                pe.wait_ge(mask_ready, 1)
                for out, which in zip(Y, (below, ones)):
                    last = nc.tensor.matmul(out[:, 0:TILES * E], which[:], mask[:].rearrange("p t e -> p (t e)"),
                                            start=True, stop=True)
                last.then_inc(counts_ps, 1)
                for r in range(1, 4):
                    step(r, r, None, None, next_shared=True)
                with pe.Fori(1, TILES // 4 - 1) as m:
                    for r in range(4):
                        step(4 * m + r, r, None, None, next_shared=True)
                for r in range(4):
                    step(TILES - 4 + r, r, None, None, next_shared=r < 3)
                pe.wait_ge(w_loaded, 3 * 16 * E)
                pe.wait_ge(routed, 1)
                quad(TILES // 4, start=True)
                with pe.Fori(TILES // 4 + 1, QUADS - 1) as m:
                    quad(m)
                e_last = quad(QUADS - 1, end=True)
                transpose_hid(ALL_TILES - 1, 1)
                down(ALL_TILES - 1, 1, e_last)


def build_network(nc, x, a_w, b_w, f_w, out):
    def dram(name, shape):
        return nc.dram_tensor(name, shape, F32).ap()

    x1, x2, x3 = [dram(name, (T + P, D)) for name in ("after_a", "after_f1", "after_b")]
    v_d = dram("a_values", (T + 2 * P, D))
    rs_d = dram("a_row_sums", (TILES * 4, SEQ))
    slot_rows = [dram("slot_rows" + n, (SLOT_TILES * P, ROW)) for n in "12"]
    ext_d = dram("bias_rows", (HEADS, P * EXT))
    Wq, bq, Wk, bk, Wv, bv, Wo, bo = a_w
    W_qkv, b_qkv, W_out, b_out, rel_bias = b_w
    with ExitStack() as ctx:
        ext_sb = ctx.enter_context(nc.sbuf_tensor("ext_sb", [HEADS, EXT], F32))
        build_bias_rows(nc, rel_bias, ext_sb)
        build_attention_a(nc, x, Wq, bq, Wk, bk, Wv, bv, Wo, bo, x1, v_d, rs_d, slot_rows, ext_sb, ext_d)
    build_ffn(nc, "f1_", x1, *f_w, x2, slot_rows[0])
    build_attention_b(nc, x2, W_qkv, b_qkv, W_out, b_out, x3, ext_d)
    build_ffn(nc, "f2_", x3, *f_w, out, slot_rows[1])


A_NAMES = ["L0_attn_a_" + n for n in ("Wq", "bq", "Wk", "bk", "Wv", "bv", "Wo", "bo")]
B_NAMES = ["L0_attn_b_" + n for n in ("W_qkv", "b_qkv", "W_out", "b_out", "rel_bias")]
F_NAMES = ["L0_ffn_" + n for n in ("Wg", "Ws1", "Ws3", "Ws2", "We1", "We3", "We2")]


def kernel(**inputs):
    import numpy as np
    import concourse.bacc as bacc
    from concourse.bass_utils import run_bass_kernel_spmd

    nc = bacc.Bacc("TRN2", target_bir_lowering=False, num_devices=1)
    x = np.ascontiguousarray(inputs["L0_attn_a_X_embed"])
    arrays = {"in_x": x.reshape(T, D)}
    for name in A_NAMES + B_NAMES + F_NAMES:
        arrays["in_" + name] = np.ascontiguousarray(inputs[name])
    aps = {name: nc.dram_tensor(name, a.shape, mybir.dt.from_np(a.dtype), kind="ExternalInput").ap()
           for name, a in arrays.items()}
    out = nc.dram_tensor("out_x", (T + P, D), F32, kind="ExternalOutput").ap()
    build_network(nc, aps["in_x"], [aps["in_" + n] for n in A_NAMES], [aps["in_" + n] for n in B_NAMES],
                  [aps["in_" + n] for n in F_NAMES], out)
    r = run_bass_kernel_spmd(nc, [arrays], core_ids=[0])
    return r.results[0]["out_x"][0:T].reshape(x.shape)
```
